# Optimizing a Trainium2 kernel written in Bass

```python
import numpy as np
import jax
import jax.numpy as jnp

def _softmax(x, axis=-1):
    return jax.nn.softmax(x, axis=axis)

def _gelu(x):
    return jax.nn.gelu(x, approximate=True)

def _silu(x):
    return jax.nn.silu(x)

def _sigmoid(x):
    return jax.nn.sigmoid(x)

def _layernorm(x, axis=-1, eps=1e-05):
    m = jnp.mean(x, axis=axis, keepdims=True)
    v = jnp.var(x, axis=axis, keepdims=True)
    return (x - m) / jnp.sqrt(v + eps)

def _scatter_add(tgt, idx, src, axis=0):
    return tgt.at[idx].add(src)

def _segment_sum(src, seg, n):
    return jax.ops.segment_sum(src, seg, n)
kernel_name = 'mk_gnn_resnorm_d4_gnn_r8_ff4a90'

def setup_inputs(seed: int=0):
    np.random.seed(seed)
    _w = jnp.asarray

    def _rec_inputs():
        import jax
        import jax.numpy as jnp
        _gk = jax.random.key(seed)
        x = -0.0005121 + 1.001 * jax.random.normal(jax.random.fold_in(_gk, 1), (6250, 64), jnp.float32)
        _s = jax.random.randint(jax.random.fold_in(_gk, 2), (100000,), 0, 6250, jnp.int32)
        _d = jax.random.randint(jax.random.fold_in(_gk, 3), (100000,), 0, 6250, jnp.int32)
        _loop = jnp.arange(6250, dtype=jnp.int32)
        src = jnp.concatenate([_s, _d, _loop])
        dst = jnp.concatenate([_d, _s, _loop])
        _o = jnp.argsort(dst, stable=True)
        src = src[_o]
        dst = dst[_o]
        edge_attr_32 = -8.62073e-06 + 0.999901 * jax.random.normal(jax.random.fold_in(_gk, 12), (206250, 32), jnp.float32)
        edge_attr_64 = -9.77346e-05 + 0.999888 * jax.random.normal(jax.random.fold_in(_gk, 13), (206250, 64), jnp.float32)
        return (x, src, dst, edge_attr_32, edge_attr_64)
    x, src, dst, edge_attr_32, edge_attr_64 = _rec_inputs()

    def _L0_gnn_setup():
        import jax, jax.numpy as jnp
        import numpy as np
        N_NODES = 6250
        N_EDGES = 100000
        DIM = 64
        N_HEADS = 4

        def _scatter_softmax(scores, dst, n_nodes):
            m = jax.ops.segment_max(scores, dst, num_segments=n_nodes)
            m = jnp.maximum(m, jnp.float32(-1000000000.0))
            ex = jnp.exp(scores - m[dst])
            denom = jax.ops.segment_sum(ex, dst, num_segments=n_nodes)
            return ex / (denom[dst] + 1e-09)
        key = jax.random.key(seed)
        ks = jax.random.split(key, 7)
        x = jax.random.normal(ks[0], (N_NODES, DIM), dtype=jnp.float32)
        Wq = jax.random.normal(ks[1], (DIM, DIM), dtype=jnp.float32) / np.sqrt(DIM)
        Wk = jax.random.normal(ks[2], (DIM, DIM), dtype=jnp.float32) / np.sqrt(DIM)
        Wv = jax.random.normal(ks[3], (DIM, DIM), dtype=jnp.float32) / np.sqrt(DIM)
        Wo = jax.random.normal(ks[4], (DIM, DIM), dtype=jnp.float32) / np.sqrt(DIM)
        src = jax.random.randint(ks[5], (N_EDGES,), 0, N_NODES, dtype=jnp.int32)
        dst = jax.random.randint(ks[6], (N_EDGES,), 0, N_NODES, dtype=jnp.int32)
        return {'x': x, 'Wq': Wq, 'Wk': Wk, 'Wv': Wv, 'Wo': Wo, 'src': src, 'dst': dst}
    _L0_gnn_all = _L0_gnn_setup()
    _L0_gnn_in = {k: v for k, v in _L0_gnn_all.items() if k in ('Wq', 'Wk', 'Wv', 'Wo')}
    del _L0_gnn_all

    def _L1_gnn_setup():
        import jax, jax.numpy as jnp
        import numpy as np
        N_NODES = 12500
        N_EDGES = 125000
        NODE_DIM = 64
        EDGE_DIM = 32
        EPS = 1e-05
        SLOPE = 0.1

        def _mlp2(v, W1, b1, W2, b2):
            h = jax.nn.leaky_relu(v @ W1 + b1, negative_slope=SLOPE)
            return h @ W2 + b2
        key = jax.random.key(seed)
        ks = jax.random.split(key, 8)
        s = 0.05
        return {'x': jax.random.normal(ks[0], (N_NODES, NODE_DIM), dtype=jnp.float32), 'edge_attr': jax.random.normal(ks[1], (N_EDGES, EDGE_DIM), dtype=jnp.float32), 'W1n': jax.random.normal(ks[2], (NODE_DIM, 2 * NODE_DIM), dtype=jnp.float32) * s, 'b1n': jnp.zeros((2 * NODE_DIM,), dtype=jnp.float32), 'W2n': jax.random.normal(ks[3], (2 * NODE_DIM, NODE_DIM), dtype=jnp.float32) * s, 'b2n': jnp.zeros((NODE_DIM,), dtype=jnp.float32), 'W1e': jax.random.normal(ks[4], (EDGE_DIM, NODE_DIM), dtype=jnp.float32) * s, 'b1e': jnp.zeros((NODE_DIM,), dtype=jnp.float32), 'W2e': jax.random.normal(ks[5], (NODE_DIM, NODE_DIM), dtype=jnp.float32) * s, 'b2e': jnp.zeros((NODE_DIM,), dtype=jnp.float32), 'res_w': jnp.ones((1,), dtype=jnp.float32), 'dp_scale': jnp.ones((1,), dtype=jnp.float32), 'gamma': jnp.ones((NODE_DIM,), dtype=jnp.float32), 'beta': jnp.zeros((NODE_DIM,), dtype=jnp.float32), 'edge_index': jax.random.randint(ks[6], (2, N_EDGES), 0, N_NODES, dtype=jnp.int64) if jax.config.jax_enable_x64 else jax.random.randint(ks[6], (2, N_EDGES), 0, N_NODES, dtype=jnp.int32)}
    _L1_gnn_all = _L1_gnn_setup()
    _L1_gnn_in = {k: v for k, v in _L1_gnn_all.items() if k in ('W1n', 'b1n', 'W2n', 'b2n', 'W1e', 'b1e', 'W2e', 'b2e', 'res_w', 'dp_scale', 'gamma', 'beta')}
    del _L1_gnn_all

    def _L2_gnn_setup():
        import jax, jax.numpy as jnp
        import numpy as np
        N_NODES = 12500
        N_EDGES = 100000
        DIM = 64
        NUM_HEADS = 4
        HEAD_DIM = DIM // NUM_HEADS
        key = jax.random.key(seed)
        ks = jax.random.split(key, 7)
        w_scale = 1.0 / np.sqrt(DIM)
        x = jax.random.normal(ks[0], (N_NODES, DIM), dtype=jnp.float32)
        edge_attr = jax.random.normal(ks[1], (N_EDGES, DIM), dtype=jnp.float32)
        edge_index = jax.random.randint(ks[2], (2, N_EDGES), 0, N_NODES, dtype=jnp.int64)
        Wq = jax.random.normal(ks[3], (DIM, DIM), dtype=jnp.float32) * w_scale
        Wk = jax.random.normal(ks[4], (DIM, DIM), dtype=jnp.float32) * w_scale
        We = jax.random.normal(ks[5], (DIM, DIM), dtype=jnp.float32) * w_scale
        Wv = jax.random.normal(ks[6], (DIM, DIM), dtype=jnp.float32) * w_scale
        return {'x': x, 'edge_attr': edge_attr, 'Wq': Wq, 'Wk': Wk, 'We': We, 'Wv': Wv, 'edge_index': edge_index}
    _L2_gnn_all = _L2_gnn_setup()
    _L2_gnn_in = {k: v for k, v in _L2_gnn_all.items() if k in ('Wq', 'Wk', 'We', 'Wv')}
    del _L2_gnn_all

    def _L3_gnn_setup():
        import jax, jax.numpy as jnp
        import numpy as np
        N_NODES = 12500
        N_EDGES = 200000
        IN_C, HID_C, OUT_C = (64, 128, 64)

        def _gin_agg(x, src, dst, num_nodes):
            agg = jax.ops.segment_sum(x[src], dst, num_segments=num_nodes)
            return agg + x
        key = jax.random.key(seed)
        k1, k2, k3, k4 = jax.random.split(key, 4)
        node_emb = jax.random.normal(k1, (N_NODES, IN_C), dtype=jnp.float32)
        W1 = jax.random.normal(k2, (IN_C, HID_C), dtype=jnp.float32) * (1.0 / np.sqrt(IN_C))
        b1 = jnp.zeros((HID_C,), dtype=jnp.float32)
        W2 = jax.random.normal(k3, (HID_C, OUT_C), dtype=jnp.float32) * (1.0 / np.sqrt(HID_C))
        b2 = jnp.zeros((OUT_C,), dtype=jnp.float32)
        edge_index = jax.random.randint(k4, (2, N_EDGES), 0, N_NODES, dtype=jnp.int64)
        return {'node_emb': node_emb, 'W1': W1, 'b1': b1, 'W2': W2, 'b2': b2, 'edge_index': edge_index}
    _L3_gnn_all = _L3_gnn_setup()
    _L3_gnn_in = {k: v for k, v in _L3_gnn_all.items() if k in ('W1', 'b1', 'W2', 'b2')}
    del _L3_gnn_all
    return {'x': x, 'src': src, 'dst': dst, 'edge_attr_32': edge_attr_32, 'edge_attr_64': edge_attr_64, 'L0_gnn_Wq': _L0_gnn_in['Wq'], 'L0_gnn_Wk': _L0_gnn_in['Wk'], 'L0_gnn_Wv': _L0_gnn_in['Wv'], 'L0_gnn_Wo': _L0_gnn_in['Wo'], 'L1_gnn_W1n': _L1_gnn_in['W1n'], 'L1_gnn_b1n': _L1_gnn_in['b1n'], 'L1_gnn_W2n': _L1_gnn_in['W2n'], 'L1_gnn_b2n': _L1_gnn_in['b2n'], 'L1_gnn_W1e': _L1_gnn_in['W1e'], 'L1_gnn_b1e': _L1_gnn_in['b1e'], 'L1_gnn_W2e': _L1_gnn_in['W2e'], 'L1_gnn_b2e': _L1_gnn_in['b2e'], 'L1_gnn_res_w': _L1_gnn_in['res_w'], 'L1_gnn_dp_scale': _L1_gnn_in['dp_scale'], 'L1_gnn_gamma': _L1_gnn_in['gamma'], 'L1_gnn_beta': _L1_gnn_in['beta'], 'L2_gnn_Wq': _L2_gnn_in['Wq'], 'L2_gnn_Wk': _L2_gnn_in['Wk'], 'L2_gnn_We': _L2_gnn_in['We'], 'L2_gnn_Wv': _L2_gnn_in['Wv'], 'L3_gnn_W1': _L3_gnn_in['W1'], 'L3_gnn_b1': _L3_gnn_in['b1'], 'L3_gnn_W2': _L3_gnn_in['W2'], 'L3_gnn_b2': _L3_gnn_in['b2']}

def reference(x, src, dst, edge_attr_32, edge_attr_64, L0_gnn_Wq, L0_gnn_Wk, L0_gnn_Wv, L0_gnn_Wo, L1_gnn_W1n, L1_gnn_b1n, L1_gnn_W2n, L1_gnn_b2n, L1_gnn_W1e, L1_gnn_b1e, L1_gnn_W2e, L1_gnn_b2e, L1_gnn_res_w, L1_gnn_dp_scale, L1_gnn_gamma, L1_gnn_beta, L2_gnn_Wq, L2_gnn_Wk, L2_gnn_We, L2_gnn_Wv, L3_gnn_W1, L3_gnn_b1, L3_gnn_W2, L3_gnn_b2):
    import jax
    import jax.numpy as jnp

    def _L0_gnn_ref(x, Wq, Wk, Wv, Wo, src, dst):
        import jax, jax.numpy as jnp
        import numpy as np
        N_NODES = 6250
        N_EDGES = 100000
        DIM = 64
        N_HEADS = 4

        def _scatter_softmax(scores, dst, n_nodes):
            m = jax.ops.segment_max(scores, dst, num_segments=n_nodes)
            m = jnp.maximum(m, jnp.float32(-1000000000.0))
            ex = jnp.exp(scores - m[dst])
            denom = jax.ops.segment_sum(ex, dst, num_segments=n_nodes)
            return ex / (denom[dst] + 1e-09)
        N, D = x.shape
        H = N_HEADS
        Dh = D // H
        q = (x @ Wq).reshape(N, H, Dh)
        k = (x @ Wk).reshape(N, H, Dh)
        v = (x @ Wv).reshape(N, H, Dh)
        scores = jnp.einsum('ehd,ehd->eh', q[dst], k[src]) / jnp.sqrt(jnp.float32(Dh))
        alpha = _scatter_softmax(scores, dst, N)
        agg = jax.ops.segment_sum(alpha[:, :, None] * v[src], dst, num_segments=N)
        return agg.reshape(N, D) @ Wo

    def _L1_gnn_ref(x, edge_attr, W1n, b1n, W2n, b2n, W1e, b1e, W2e, b2e, res_w, dp_scale, gamma, beta, edge_index):
        import jax, jax.numpy as jnp
        import numpy as np
        N_NODES = 12500
        N_EDGES = 125000
        NODE_DIM = 64
        EDGE_DIM = 32
        EPS = 1e-05
        SLOPE = 0.1

        def _mlp2(v, W1, b1, W2, b2):
            h = jax.nn.leaky_relu(v @ W1 + b1, negative_slope=SLOPE)
            return h @ W2 + b2
        num_nodes = x.shape[0]
        x_t = _mlp2(x, W1n, b1n, W2n, b2n)
        e_t = _mlp2(edge_attr, W1e, b1e, W2e, b2e)
        src, dst = (edge_index[0], edge_index[1])
        msgs = x_t[src] * e_t * dp_scale
        aggregated = jax.ops.segment_sum(msgs, dst, num_segments=num_nodes)
        out = x + aggregated * res_w
        mu = jnp.mean(out, axis=-1, keepdims=True)
        var = jnp.mean(jnp.square(out - mu), axis=-1, keepdims=True)
        return (out - mu) * jax.lax.rsqrt(var + EPS) * gamma + beta

    def _L2_gnn_ref(x, edge_attr, Wq, Wk, We, Wv, edge_index):
        import jax, jax.numpy as jnp
        import numpy as np
        N_NODES = 12500
        N_EDGES = 100000
        DIM = 64
        NUM_HEADS = 4
        HEAD_DIM = DIM // NUM_HEADS
        n = x.shape[0]
        Q_h = (x @ Wq.T).reshape(n, NUM_HEADS, HEAD_DIM)
        K_h = (x @ Wk.T).reshape(n, NUM_HEADS, HEAD_DIM)
        V_h = (x @ Wv.T).reshape(n, NUM_HEADS, HEAD_DIM)
        E = (edge_attr @ We.T).reshape(-1, NUM_HEADS, HEAD_DIM)
        src_idx = edge_index[0]
        dst_idx = edge_index[1]
        src = K_h[src_idx]
        dest = Q_h[dst_idx]
        score = src * dest / np.sqrt(HEAD_DIM).astype(np.float32)
        score = score * E
        score = jnp.exp(jnp.clip(score.sum(-1, keepdims=True), -5.0, 5.0))
        msg = V_h[src_idx] * score
        wV = jax.ops.segment_sum(msg, dst_idx, num_segments=n)
        Z = jax.ops.segment_sum(score, dst_idx, num_segments=n)
        h_out = wV / (Z + 1e-06)
        return h_out.reshape(n, NUM_HEADS * HEAD_DIM)

    def _L3_gnn_ref(node_emb, W1, b1, W2, b2, edge_index):
        import jax, jax.numpy as jnp
        import numpy as np
        N_NODES = 12500
        N_EDGES = 200000
        IN_C, HID_C, OUT_C = (64, 128, 64)

        def _gin_agg(x, src, dst, num_nodes):
            agg = jax.ops.segment_sum(x[src], dst, num_segments=num_nodes)
            return agg + x
        src, dst = (edge_index[0], edge_index[1])
        n = node_emb.shape[0]
        x = node_emb
        x = _gin_agg(x, src, dst, n) @ W1 + b1
        x = jax.nn.relu(x)
        x = _gin_agg(x, src, dst, n) @ W2 + b2
        return x
    edge_index = jnp.stack([src, dst])
    x = _layernorm(x + _L0_gnn_ref(x, L0_gnn_Wq, L0_gnn_Wk, L0_gnn_Wv, L0_gnn_Wo, src, dst), axis=-1)
    x = _layernorm(x + _L1_gnn_ref(x, edge_attr_32, L1_gnn_W1n, L1_gnn_b1n, L1_gnn_W2n, L1_gnn_b2n, L1_gnn_W1e, L1_gnn_b1e, L1_gnn_W2e, L1_gnn_b2e, L1_gnn_res_w, L1_gnn_dp_scale, L1_gnn_gamma, L1_gnn_beta, edge_index), axis=-1)
    x = _layernorm(x + _L2_gnn_ref(x, edge_attr_64, L2_gnn_Wq, L2_gnn_Wk, L2_gnn_We, L2_gnn_Wv, edge_index), axis=-1)
    x = _layernorm(x + _L3_gnn_ref(x, L3_gnn_W1, L3_gnn_b1, L3_gnn_W2, L3_gnn_b2, edge_index), axis=-1)
    return x

_drawn_inputs = setup_inputs


def setup_inputs(seed=0):
    import zlib

    import numpy as np

    out = dict(_drawn_inputs(seed))
    spreads = {'L1_gnn_b1n': (0.0, 0.1),
     'L1_gnn_b2n': (0.0, 0.1),
     'L1_gnn_b1e': (0.0, 0.1),
     'L1_gnn_b2e': (0.0, 0.1),
     'L1_gnn_gamma': (1.0, 0.2),
     'L1_gnn_beta': (0.0, 0.1),
     'L3_gnn_b1': (0.0, 0.1),
     'L3_gnn_b2': (0.0, 0.1)}
    factors = {}
    for name, (base, spread) in spreads.items():
        noise = np.random.default_rng([zlib.crc32(name.encode()), seed]).standard_normal(out[name].shape)
        drawn = base * np.exp(spread * noise) if base else spread * noise
        out[name] = jnp.asarray(drawn.astype(out[name].dtype))
    for name, factor in factors.items():
        out[name] = (out[name] * factor).astype(out[name].dtype)
    return out
```

```python
import concourse.bass as bass
from concourse import mybir
from contextlib import ExitStack

P = 128
GROUP = 8
CHUNK = 4
INDEXES = 4
BIG = 1.0e30
SLOPE = 0.1
EPS = 1.0e-5
CHAIN2 = 4


def build_gnn(nc, x, src, dst, edge_attr_32, edge_attr_64,
              L0_gnn_Wq, L0_gnn_Wk, L0_gnn_Wv, L0_gnn_Wo,
              L1_gnn_W1n, L1_gnn_b1n, L1_gnn_W2n, L1_gnn_b2n, L1_gnn_W1e, L1_gnn_b1e,
              L1_gnn_W2e, L1_gnn_b2e, L1_gnn_res_w, L1_gnn_dp_scale, L1_gnn_gamma, L1_gnn_beta,
              L2_gnn_Wq, L2_gnn_Wk, L2_gnn_We, L2_gnn_Wv,
              L3_gnn_W1, L3_gnn_b1, L3_gnn_W2, L3_gnn_b2, out):
    f32, i32 = mybir.dt.float32, mybir.dt.int32
    ALU, ACT, AX = mybir.AluOpType, mybir.ActivationFunctionType, mybir.AxisListType.X

    N, D = x.shape
    E = src.shape[0]
    H = 4
    DH = D // H
    DE = edge_attr_32.shape[1]
    HID = L3_gnn_W1.shape[1]
    A = D + H

    TILES = -(-E // P)
    GROUPS = -(-TILES // GROUP)
    GROUPS += GROUPS % 2
    PAIRS = GROUPS // 2
    assert (GROUPS - 2) % INDEXES == 0
    EG = GROUP * P
    LAST = GROUPS - 1
    TAIL_TILES = (E - LAST * EG) // P
    TAIL_ROWS = (E - LAST * EG) % P
    assert 0 < TAIL_TILES < GROUP and TAIL_ROWS

    CG = 7
    CHAINS = -(-GROUPS // CG)
    SG = CHAINS * CG
    LEN = CG * EG
    SP_ = H * CHAINS
    assert SP_ <= P

    NAT = -(-SG * GROUP // P)
    FULL = TILES - 1
    NODE_TILES = -(-(N + P) // P)
    NODE_TILES += -NODE_TILES % CHUNK
    CHUNKS = NODE_TILES // CHUNK
    NPAD = NODE_TILES * P
    NREM = N % P
    NFULL = N // P
    CD = CHUNK * D
    CP = CHUNK * P

    def dram(name, shape, dt=f32):
        return nc.dram_tensor(name, shape, dt, kind="Internal").ap()

    kv_table = dram("kv_table", [NPAD, 2 * D])
    q_table = dram("q_table", [NPAD, D])
    kv2_table = dram("kv2_table", [NPAD, 2 * D])
    q2_table = dram("q2_table", [NPAD, D])
    xt_table = dram("xt_table", [NPAD, D])
    x3_table = dram("x3_table", [NPAD, D])
    y3_table = dram("y3_table", [NPAD, D])
    v_edges = dram("v_edges", [GROUPS, P, GROUP * D])
    s_edges = dram("s_edges", [SG, H * GROUP, P])
    p_edges = dram("p_edges", [SG, H * GROUP, P])
    dst_line = dram("dst_line", [1, P + NAT * P * P + LEN])
    start_line = dram("start_line", [NAT, P], i32)

    ctx = ExitStack()
    with ctx:
        def sb(name, shape, dt=f32):
            return ctx.enter_context(nc.sbuf_tensor(name, shape, dt))

        def sem(name):
            return ctx.enter_context(nc.semaphore(name))

        def sems(prefix, names):
            return {n: sem(f"{prefix}_{n}") for n in names.split()}

        src_idx = sb("src_idx", [P, NAT * P], i32)
        dst_rel = sb("dst_rel", [P, NAT * P])
        starts = sb("starts", [1, NAT * P], i32)
        nodes = sb("nodes", [P, NODE_TILES, D])
        acc = sb("acc", [P, NPAD])
        ident = sb("ident", [P, P])
        iota = sb("iota", [P, P])
        ones = sb("ones", [1, P])
        w_qkv = sb("w_qkv", [D, 3 * D])
        w_o = sb("w_o", [D, D])
        w_1n = sb("w_1n", [D, HID])
        w_2n = sb("w_2n", [HID, D])
        w_1e = sb("w_1e", [P, P // DE, 2 * D])
        w_2e = sb("w_2e", [P, D])
        w_nat = sb("w_nat", [D, 4 * D])
        w_2 = sb("w_2", [D, 3 * D])
        w_e = sb("w_e", [P, 2 * D])
        w_g1 = sb("w_g1", [D, HID])
        w_g2 = sb("w_g2", [HID, D])
        b_1n = sb("b_1n", [HID, 1])
        b_1e = sb("b_1e", [P, 1])
        b_g1 = sb("b_g1", [HID, 1])
        b_2n = sb("b_2n", [1, D])
        b_2e = sb("b_2e", [1, D])
        b_g2 = sb("b_g2", [P, D])
        gamma = sb("gamma", [P, D])
        beta = sb("beta", [P, D])
        gains = sb("gains", [P, 2])
        gain = sb("gain", [P, 1])
        index = sb("index", [P, INDEXES, GROUP], i32)
        rows = sb("rows", [P, 2, GROUP, 2 * D])
        window = sb("window", [P, 2, GROUP, D])
        onehot = sb("onehot", [P, 2, GROUP, P])
        onehot_t = sb("onehot_t", [P, 2, GROUP, P])
        message = sb("message", [P, 2, GROUP, A])
        product = sb("product", [P, 2, GROUP, D])
        score = sb("score", [P, 2, H * GROUP])
        score_t = sb("score_t", [H * GROUP, 2, P])
        edge_in = sb("edge_in", [P, 2, GROUP, D])
        edge_t = sb("edge_t", [P, 2, 4, P])
        hidden_t = onehot_t
        big = sb("big", [P, 3 * (LEN + 2)])
        line_s = big[0:SP_, 0:LEN]
        line_d = big[0:SP_, LEN:2 * LEN + 2]
        line_r = big[0:SP_, 2 * LEN + 2:3 * LEN + 4]
        chain_cols = sb("chain_cols", [P, 8])
        chain_rows = sb("chain_rows", [1, 4, P])

        bank = [ctx.enter_context(nc.psum_tensor(f"bank{i}", [P, 2, 512], f32)) for i in range(4)]

        def banks(n, k=1):
            return bank[n // 2][:, n % 2, :] if k == 1 else bank[n // 2][:].rearrange("p a b -> p (a b)")

        block = ctx.enter_context(nc.Block())


        def gathers(name):
            return [sem(f"{name}_gathered{u}") for u in range(2)]

        filled = sem("filled")
        consts = sem("consts")
        graph_in = sem("graph_in")
        weights_in = sem("weights_in")
        nodes_in = sem("nodes_in")
        graph_cast = sem("graph_cast")
        graph_ps = sem("graph_ps")
        graph_out = sem("graph_out")
        lines_out = sem("lines_out")
        starts_in = sem("starts_in")
        weights_ps = sem("weights_ps")
        weights_t = sem("weights_t")
        norm = sem("norm")
        chains_ps = sem("chains_ps")
        chains_dve = sem("chains_dve")
        lines_less = sem("lines_less")
        lines_in = sem("lines_in")
        lines_exp = sem("lines_exp")
        probs_out = sem("probs_out")
        w_scaled = sem("w_scaled")
        variance = sem("variance")
        root = sem("root")
        zeroed = sem("zeroed")
        normed = sem("normed")
        stored = sem("stored")
        K0 = sems("kv0", "staged xt_ps xt proj_ps proj table")
        O0 = sems("out0", "staged acc_ps den mixed mixed_ps mixed_t proj_ps added")
        K1 = sems("mlp1", "staged xt_ps xt hid_ps hid leaky proj_ps proj table")
        O1 = sems("out1", "staged acc_ps added")
        K2 = sems("kv2", "staged xt_ps xt proj_ps proj table")
        O2 = sems("out2", "staged acc_ps den mixed")
        M3 = sems("gin_mid", "staged xt_ps sum hid_ps hid proj_ps proj")
        O3 = sems("out3", "staged acc_ps added")
        A0 = sems("scores", "index onehot onehot_ps onehot_t expanded product score score_ps score_t")
        A0["gathered"], A0["window"] = gathers("scores"), [sem(f"scores_window{u}") for u in range(2)]
        A0["spilled"], A0["stored"] = [sem(f"scores_v_out{u}") for u in range(2)], [sem(f"scores_out{u}") for u in range(2)]
        A1 = sems("values", "onehot weights_ps weights message reduced added")
        A1["edge"], A1["probs"] = [sem(f"values_v{u}") for u in range(2)], [sem(f"values_p{u}") for u in range(2)]
        B0 = sems("gated", "index onehot edge_ps edge_t hid_ps hid edge_mm message reduced added")
        B0["gathered"], B0["edge"] = gathers("gated"), [sem(f"gated_edge{u}") for u in range(2)]
        C0 = sems("attend", "index onehot onehot_ps onehot_t expanded edge_ps edge_t edge_mm chain weights "
                            "message reduced added")
        C0["gathered"], C0["window"] = gathers("attend"), [sem(f"attend_window{u}") for u in range(2)]
        C0["edge"] = [sem(f"attend_edge{u}") for u in range(2)]
        G0 = sems("gin_a", "index onehot reduced added")
        G0["gathered"] = gathers("gin_a")
        G1 = sems("gin_b", "index onehot reduced added")
        G1["gathered"] = gathers("gin_b")

        NATW = NAT * P
        nat_src = big[:, 0:NATW].bitcast(i32).rearrange("p (c e) -> p c e", e=P)
        nat_dst = big[:, NATW:2 * NATW].bitcast(i32).rearrange("p (c e) -> p c e", e=P)
        flt_src = big[:, 2 * NATW:3 * NATW].rearrange("p (c e) -> p c e", e=P)
        flt_dst = big[:, 3 * NATW:4 * NATW].rearrange("p (c e) -> p c e", e=P)
        flt_rel = big[:, 4 * NATW:5 * NATW].rearrange("p (c e) -> p c e", e=P)
        start_f = big[:, 5 * NATW:5 * NATW + NAT]
        start_i = big[:, 5 * NATW + NAT:5 * NATW + 2 * NAT].bitcast(i32)
        minus = big[0:1, 5 * NATW + 2 * NAT:5 * NATW + 2 * NAT + P]
        blank = big[0:H * GROUP, 5 * NATW + 2 * NAT + P:5 * NATW + 2 * NAT + 2 * P]

        W = NODE_TILES * D
        mix = big[:, 0:W].rearrange("p (t d) -> p t d", d=D)
        squares = big[:, W:2 * W].rearrange("p (t d) -> p t d", d=D)
        stats = big[:, 2 * W:2 * W + 2 * NODE_TILES].rearrange("p (a t) -> p a t", a=2)
        at = 2 * W + 2 * NODE_TILES
        chunk_t = big[0:D, at:at + CP]
        chunk_h = big[:, at + CP:at + 2 * CP]
        chunk_l = big[:, at + 2 * CP:at + 3 * CP]
        chunk_p = big[:, at + 3 * CP:at + 3 * CP + 3 * CD].rearrange("p (t f) -> p t f", f=3 * D)
        chunk_m = big[:, at + 3 * CP + 3 * CD:at + 3 * CP + 4 * CD].rearrange("p (t f) -> p t f", f=D)
        chunk_d = big[:, at + 3 * CP + 4 * CD:at + 3 * CP + 4 * CD + CHUNK * H].rearrange("p (t h) -> p t h", h=H)
        at += 3 * CP + 4 * CD + CHUNK * H
        stage_x = big[:, at:at + CD].rearrange("p (t d) -> p t d", d=D)
        stage_a = big[:, at + CD:at + CD + CP]
        assert at + CD + CP <= 3 * (LEN + 2)
        chunk_x = banks(0)[0:D, :]
        chunk_a = banks(1)[:, 0:CHUNK * A].rearrange("p (t f) -> p t f", f=A)
        chunk_u = banks(4)[:, :]
        chunk_v = banks(5)[:, 0:CD].rearrange("p (t f) -> p t f", f=D)

        def chunk_w(t):
            return bank[1][:, t // 2, (t % 2) * 3 * D:(t % 2 + 1) * 3 * D]

        def tiles(i):
            return bass.ds(i * CHUNK, CHUNK)

        def loop_pairs(eng, body):
            body(0, True, False)
            with eng.Fori(1, PAIRS - 1) as i:
                body(i, False, False)
            body(PAIRS - 1, False, True)

        def loop_chunks(eng, body):
            body(0, True)
            with eng.Fori(1, CHUNKS) as i:
                body(i, False)

        def heads(ap):
            return ap.rearrange("p t (h d) -> p t h d", h=H)

        def blocks_of(v):
            c = FULL // P
            yield (slice(0, P), slice(0, c), slice(0, P)), v[0:c * P * P].rearrange("(c p e) -> p c e", p=P, e=P)
            yield (slice(0, FULL - c * P), c, slice(0, P)), v[c * P * P:FULL * P].rearrange("(p e) -> p e", e=P)
            yield (slice(FULL - c * P, FULL - c * P + 1), c, slice(0, E - FULL * P)), v[FULL * P:E].rearrange("(p e) -> p e", p=1)

        def row_of(v):
            return v.rearrange("(a n) -> a n", a=1)

        weight_loads = [
            (w_qkv[:, 0:D], L0_gnn_Wk), (w_qkv[:, D:2 * D], L0_gnn_Wv), (w_qkv[:, 2 * D:], L0_gnn_Wq),
            (w_o[:], L0_gnn_Wo), (w_1n[:], L1_gnn_W1n), (w_2n[:], L1_gnn_W2n),
            (w_2e[0:D, :], L1_gnn_W2e), (w_2e[D:P, :], L1_gnn_W2e),
            (w_nat[:, 0:D], L2_gnn_Wk), (w_nat[:, D:2 * D], L2_gnn_Wv), (w_nat[:, 2 * D:3 * D], L2_gnn_Wq),
            (w_nat[:, 3 * D:], L2_gnn_We), (w_g1[:], L3_gnn_W1), (w_g2[:], L3_gnn_W2),
            (b_1n[:], L1_gnn_b1n.rearrange("(n a) -> n a", a=1)),
            (b_1e[0:D, :], L1_gnn_b1e.rearrange("(n a) -> n a", a=1)),
            (b_1e[D:P, :], L1_gnn_b1e.rearrange("(n a) -> n a", a=1)),
            (b_g1[:], L3_gnn_b1.rearrange("(n a) -> n a", a=1)),
            (b_2n[:], row_of(L1_gnn_b2n)), (b_2e[:], row_of(L1_gnn_b2e)),
            (b_g2[:], row_of(L3_gnn_b2).to_broadcast([P, D])),
            (gamma[:], row_of(L1_gnn_gamma).to_broadcast([P, D])),
            (beta[:], row_of(L1_gnn_beta).to_broadcast([P, D])),
            (gains[:, 0:1], row_of(L1_gnn_dp_scale).to_broadcast([P, 1])),
            (gains[:, 1:2], row_of(L1_gnn_res_w).to_broadcast([P, 1])),
        ] + [(w_1e[DE * r:DE * (r + 1), r, D * c:D * (c + 1)], L1_gnn_W1e) for r in range(P // DE) for c in range(2)]
        WEIGHTS_IN = 16 * len(weight_loads)
        GRAPH_IN = 16 * 6
        assert NFULL % CHUNK == 0
        NODES_IN = 16 * (NFULL // CHUNK + 1)
        LINES_OUT = 16 * (3 + SG - GROUPS)

        def store_tables(sp, K, parts):
            with sp.Fori(0, CHUNKS) as i:
                sp.wait_ge(K["proj"], parts * (i + 1))
                if parts == 2:
                    sp.dma_start(kv_table.rearrange("(t p) f -> p t f", p=P)[:, tiles(i), :],
                                 chunk_p[:, :, 0:2 * D]).then_inc(K["table"], 16)
                    sp.dma_start(q_table.rearrange("(t p) f -> p t f", p=P)[:, tiles(i), :],
                                 chunk_p[:, :, 2 * D:3 * D]).then_inc(K["table"], 16)
                else:
                    sp.dma_start(xt_table.rearrange("(t p) f -> p t f", p=P)[:, tiles(i), :],
                                 chunk_p[:, :, 0:D]).then_inc(K["table"], 16)

        def load_edges(sp, C, edges, g, u, first, tail):
            to = edge_in[:, u, :, :].rearrange("p k f -> p (k f)")[:, 0:GROUP * edges.shape[1]].rearrange(
                "p (k f) -> p k f", k=GROUP)
            if not first:
                sp.wait_ge(C["edge_ps"], g - 1)
            if not tail:
                sp.dma_start(to, edges[bass.ds(g * EG, EG), :].rearrange("(k p) f -> p k f", p=P)).then_inc(C["edge"][u], 16)
            else:
                at = LAST * EG
                sp.dma_start(to[:, 0:TAIL_TILES, :], edges[at:at + TAIL_TILES * P, :].rearrange(
                    "(k p) f -> p k f", p=P)).then_inc(C["edge"][u], 16)
                sp.dma_start(to[0:TAIL_ROWS, TAIL_TILES, :], edges[at + TAIL_TILES * P:E, :]).then_inc(C["edge"][u], 16)

        def edge_landed(i, tail):
            return 16 * (PAIRS - 1) + 32 if tail else 16 * (i + 1)

        def load_windows(sp, C, regs, edges):
            if C is A0:
                sp.wait_ge(K0["table"], 32 * CHUNKS)
            else:
                sp.wait_ge(K2["table"], 32 * CHUNKS)

            def body(i, first, last):
                for u in range(2):
                    g = 2 * i + u
                    if edges is not None:
                        load_edges(sp, C, edges, g, u, first, last and u == 1)
                    if not first:
                        sp.wait_ge(C["expanded"], g - 1)
                        sp.nop()
                    sp.load(regs, starts[0:1, bass.ds(g * GROUP, GROUP)])
                    for k in range(GROUP):
                        at = sp.snap(regs[k], min_val=0, max_val=N - 1)
                        sp.dma_start(window[:, u, k, :], q_table[bass.ds(at, P), :]).then_inc(C["window"][u], 16)
            loop_pairs(sp, body)

        def line_views(h):
            on = slice(h * CHAINS, (h + 1) * CHAINS)
            return (line_s[on, :].rearrange("c (g n) -> c g n", g=CG),
                    s_edges.rearrange("(c g) (h k) e -> h c g (k e)", g=CG, h=H)[h],
                    line_d[on, :],
                    line_r[on, 0:LEN].rearrange("c (g n) -> c g n", g=CG),
                    p_edges.rearrange("(c g) (h k) e -> h c g (k e)", g=CG, h=H)[h])

        def probabilities_dma(sp):
            for u in range(2):
                sp.wait_ge(A0["stored"][u], 16 * PAIRS)
            for h in range(H):
                to_s, of_s, to_d, _, _ = line_views(h)
                sp.dma_start(to_s, of_s).then_inc(lines_in, 16)
                sp.dma_start(to_d[:, 0:LEN], dst_line[0, P - 1:P - 1 + CHAINS * LEN].rearrange(
                    "(c n) -> c n", n=LEN)).then_inc(lines_in, 16)
                sp.dma_start(to_d[:, LEN:LEN + 2], dst_line[0, P - 1 + LEN:P - 1 + LEN + CHAINS * LEN].rearrange(
                    "(c n) -> c n", n=LEN)[:, 0:2]).then_inc(lines_in, 16)
            sp.wait_ge(lines_exp, 1)
            for h in range(H):
                _, _, _, of_p, to_p = line_views(h)
                sp.dma_start(to_p, of_p).then_inc(probs_out, 16)

        def values_dma(sp):
            for u in range(2):
                sp.wait_ge(A0["spilled"][u], 16 * PAIRS)
            sp.wait_ge(probs_out, 16 * H)

            def body(i, first, last):
                for u in range(2):
                    g = 2 * i + u
                    if not first:
                        sp.wait_ge(A1["message"], g - 1)
                    sp.dma_start(edge_in[:, u, :, :].rearrange("p k f -> p (k f)"),
                                 v_edges[bass.ds(g, 1)].rearrange("a p n -> (a p) n")).then_inc(A1["edge"][u], 16)
                    sp.dma_start(score_t[:, u, :], p_edges[bass.ds(g, 1)].rearrange("a r e -> (a r) e")).then_inc(A1["probs"][u], 16)
            loop_pairs(sp, body)

        def gated_dma(sp):
            loop_pairs(sp, lambda i, first, last: [
                load_edges(sp, B0, edge_attr_32, 2 * i + u, u, first, last and u == 1) for u in range(2)])

        def gathered_rows(u, width):
            return rows[:, u, :, :].rearrange("p k f -> p (k f)")[:, 0:GROUP * width].rearrange("p (k f) -> p k f", k=GROUP)

        def gather(pool, C, table, width, users):
            def body(g, pair, m, first, last):
                u = m % 2
                if not first:
                    for s, n in users:
                        if isinstance(s, list):
                            pool.wait_ge(s[u], n * pair)
                        else:
                            pool.wait_ge(s, n * (g - 1))
                pool.wait_ge(C["index"], g + 1)
                if not last:
                    nc.gpsimd.tensor_copy(index[:, (m + 1) % INDEXES, :], src_idx[:, bass.ds((g + 1) * GROUP, GROUP)]
                                          ).then_inc(C["index"], 1)
                for k in range(GROUP):
                    pool.indirect_dma_start(gathered_rows(u, width)[:, k, :], None, table,
                                            bass.IndirectOffsetOnAxis(index[:, m, k:k + 1], 0)
                                            ).then_inc(C["gathered"][u], 16)

            nc.gpsimd.tensor_copy(index[:, 0, :], src_idx[:, 0:GROUP]).then_inc(C["index"], 1)
            body(0, 0, 0, True, False)
            body(1, 0, 1, True, False)
            with pool.Fori(0, (GROUPS - 2) // INDEXES - 1) as i:
                for v in range(INDEXES):
                    body(INDEXES * i + 2 + v, INDEXES // 2 * i + 1 + v // 2, (2 + v) % INDEXES, False, False)
            for v in range(INDEXES):
                g = GROUPS - INDEXES + v
                body(g, g // 2, g % INDEXES, False, v == INDEXES - 1)

        def landed(i):
            return 16 * GROUP * (i + 1)

        def stage_nodes(act, K, i, first):
            if not first:
                act.wait_ge(K["xt_ps"], i)
            nc.scalar.copy(stage_x, nodes[:, tiles(i), :]).then_inc(K["staged"], 1)

        def stage_sums(act, O, i, first, width):
            if not first:
                act.wait_ge(O["acc_ps"], i)
            nc.scalar.copy(stage_a[0:width, :], acc[0:width, bass.ds(i * CP, CP)]).then_inc(O["staged"], 1)

        def stage_act(act, O, C, width):
            act.wait_ge(C["added"], GROUP * GROUPS)
            loop_chunks(act, lambda i, first: stage_sums(act, O, i, first, width))

        def square_root(act, n):
            act.wait_ge(variance, n)
            nc.scalar.activation(stats[:, 1, :], stats[:, 1, :], ACT.Sqrt).then_inc(root, 1)

        def copy_projections(act, K, parts):
            def body(i, first):
                stage_nodes(act, K, i, first)
                act.wait_ge(K["xt_ps"], i + 1)
                nc.scalar.copy(chunk_t, chunk_x).then_inc(K["xt"], 1)
                act.wait_ge(K["proj_ps"], i + 1)
                if not first:
                    act.wait_ge(K["table"], 16 * parts * i)
                nc.scalar.copy(chunk_p[:, 0:2, :], bank[1][:, 0, 0:6 * D].rearrange("p (t f) -> p t f", t=2)).then_inc(K["proj"], 1)
                nc.scalar.copy(chunk_p[:, 2:4, :], bank[1][:, 1, 0:6 * D].rearrange("p (t f) -> p t f", t=2)).then_inc(K["proj"], 1)
            loop_chunks(act, body)

        def scores_act(act):
            def body(i, first, last):
                for u in range(2):
                    g = 2 * i + u
                    act.wait_ge(A0["onehot_ps"], g + 1)
                    if not first:
                        act.wait_ge(A0["expanded"], g - 1)
                    nc.scalar.copy(onehot_t[:, u, :, :], bank[u][:].rearrange("p a (k j) -> p (a k) j", j=P)
                                   ).then_inc(A0["onehot_t"], 1)
                    act.wait_ge(A0["gathered"][u], landed(i))
                    act.dma_start(v_edges[bass.ds(g, 1)].rearrange("a p (k f) -> (a p) k f", k=GROUP),
                                  rows[:, u, :, D:2 * D]).then_inc(A0["spilled"][u], 16)
                    act.wait_ge(A0["score_ps"], g + 1)
                    if not first:
                        act.wait_ge(A0["stored"][u], 16 * i)
                    nc.scalar.mul(score_t[:, u, :], bank[3][0:H * GROUP, u, 0:P], DH ** -0.5).then_inc(A0["score_t"], 1)
                    act.wait_ge(A0["score_t"], g + 1)
                    act.dma_start(s_edges[bass.ds(g, 1)].rearrange("a r e -> (a r) e"), score_t[:, u, :]
                                  ).then_inc(A0["stored"][u], 16)
            loop_pairs(act, body)

        def mixed_act(act):
            act.wait_ge(A1["added"], GROUP * GROUPS)

            def body(i, first):
                stage_sums(act, O0, i, first, A)
                act.wait_ge(O0["mixed_ps"], i + 1)
                if not first:
                    act.wait_ge(O0["proj_ps"], i)
                nc.scalar.copy(chunk_t, chunk_x).then_inc(O0["mixed_t"], 1)
            loop_chunks(act, body)

        def mlp_act(act):
            act.wait_ge(normed, 1)

            def body(i, first):
                stage_nodes(act, K1, i, first)
                act.wait_ge(K1["xt_ps"], i + 1)
                nc.scalar.copy(chunk_t, chunk_x).then_inc(K1["xt"], 1)
                act.wait_ge(K1["hid_ps"], i + 1)
                if not first:
                    act.wait_ge(K1["leaky"], i)
                nc.scalar.activation(chunk_h, chunk_u, ACT.Identity, bias=b_1n[:, 0:1]).then_inc(K1["hid"], 1)
                act.wait_ge(K1["proj_ps"], i + 1)
                if not first:
                    act.wait_ge(K1["table"], 16 * i)
                nc.scalar.copy(chunk_p[:, :, 0:D], chunk_v).then_inc(K1["proj"], 1)
            loop_chunks(act, body)

        def gated_act(act):
            def body(i, first, last):
                for u in range(2):
                    g = 2 * i + u
                    act.wait_ge(B0["edge_ps"], g + 1)
                    if not first:
                        act.wait_ge(B0["hid_ps"], g - 1)
                    nc.scalar.copy(edge_t[:, u, 0:2, :], bank[2][:, 0, 0:2 * P].rearrange("p (m e) -> p m e", m=2)
                                   ).then_inc(B0["edge_t"], 1)
                    act.wait_ge(B0["hid_ps"], g + 1)
                    if not first:
                        act.wait_ge(B0["edge_mm"], g - 1)
                    hid = bank[1][:].rearrange("p a (k e) -> p (a k) e", e=P)
                    nc.scalar.activation(hidden_t[0:D, u, :, :], hid[0:D], ACT.Identity, bias=b_1e[0:D, 0:1]
                                         ).then_inc(B0["hid"], 1)
                    nc.scalar.activation(hidden_t[D:P, u, :, :], hid[D:P], ACT.Relu, bias=b_1e[D:P, 0:1]
                                         ).then_inc(B0["hid"], 1)
            loop_pairs(act, body)

        def attend_act(act):
            def body(i, first, last):
                for u in range(2):
                    g = 2 * i + u
                    act.wait_ge(C0["onehot_ps"], g + 1)
                    if not first:
                        act.wait_ge(C0["expanded"], g - 1)
                        act.wait_ge(C0["edge_mm"], g - 1)
                    nc.scalar.copy(onehot_t[:, u, :, :], bank[1][:].rearrange("p a (k j) -> p (a k) j", j=P)
                                   ).then_inc(C0["onehot_t"], 1)
                    act.wait_ge(C0["edge_ps"], g + 1)
                    nc.scalar.copy(edge_t[:, u, :, :], bank[3][:, 0, :].rearrange("p (m e) -> p m e", m=4)
                                   ).then_inc(C0["edge_t"], 1)
                    act.wait_ge(C0["chain"], CHAIN2 * (g + 1))
                    if not first:
                        act.wait_ge(C0["reduced"], g - 1)
                    nc.scalar.activation(message[:, u, :, D:A], score[:, u, :].rearrange("p (k h) -> p k h", h=H),
                                         ACT.Exp, scale=DH ** -0.5).then_inc(C0["weights"], 1)
            loop_pairs(act, body)

        def gin_act(act):
            act.wait_ge(G0["added"], GROUP * GROUPS)

            def body(i, first):
                stage_nodes(act, M3, i, first)
                act.wait_ge(M3["hid_ps"], i + 1)
                nc.scalar.activation(chunk_h, chunk_u, ACT.Relu, bias=b_g1[:, 0:1]).then_inc(M3["hid"], 1)
                act.wait_ge(M3["proj_ps"], i + 1)
                nc.scalar.copy(mix[:, tiles(i), :], chunk_v).then_inc(M3["proj"], 1)
            loop_chunks(act, body)

        def turned(to, of, eye):
            return nc.tensor.matmul(to, of, eye, start=True, stop=True)

        def turn_nodes(pe, i, K):
            pe.wait_ge(K["staged"], i + 1)
            for t in range(CHUNK):
                last = turned(chunk_x[:, t * P:(t + 1) * P],
                                           stage_x[:, t, :], ident[:])
            last.then_inc(K["xt_ps"], 1)

        def project(pe, K, w):
            def body(i, first):
                if not first:
                    pe.wait_ge(K["xt"], i)
                turn_nodes(pe, i, K)
                pe.wait_ge(K["xt"], i + 1)
                if not first:
                    pe.wait_ge(K["proj"], 2 * i)
                for t in range(CHUNK):
                    last = nc.tensor.matmul(chunk_w(t), chunk_t[:, t * P:(t + 1) * P], w[:], start=True, stop=True)
                last.then_inc(K["proj_ps"], 1)
            loop_chunks(pe, body)

        def expand(C, u, to):
            for k in range(GROUP):
                last = nc.tensor.matmul(to[:, k * D:(k + 1) * D], onehot_t[:, u, k, :], window[:, u, k, :],
                                        start=True, stop=True)
            last.then_inc(C["expanded"], 1)

        def turn_onehots(C, u, to):
            for k in range(GROUP):
                last = nc.tensor.transpose(to[:, k // 4, k % 4 * P:(k % 4 + 1) * P], onehot[:, u, k, :], ident[:])
            last.then_inc(C["onehot_ps"], 1)

        def reduce(C, u, to, width, of):
            for k in range(GROUP):
                last = nc.tensor.matmul(to[0:width, k // 4, k % 4 * P:(k % 4 + 1) * P], of(k), onehot[:, u, k, :],
                                        start=True, stop=True)
            last.then_inc(C["reduced"], 1)

        def scores_pe(pe):
            pe.wait_ge(K0["proj"], 2 * CHUNKS)

            def body(i, first, last):
                for u in range(2):
                    g = 2 * i + u
                    pe.wait_ge(A0["onehot"], g + 1)
                    if not first:
                        pe.wait_ge(A0["onehot_t"], g - 1)
                    turn_onehots(A0, u, bank[u])
                    pe.wait_ge(A0["onehot_t"], g + 1)
                    pe.wait_ge(A0["window"][u], landed(i))
                    if not first:
                        pe.wait_ge(A0["product"], g - 1)
                    expand(A0, u, bank[2][:, u, :])
                    pe.wait_ge(A0["score"], g + 1)
                    if not first:
                        pe.wait_ge(A0["score_t"], g - 1)
                    turned(bank[3][0:H * GROUP, u, 0:P], score[:, u, :], ident[:]).then_inc(A0["score_ps"], 1)
            loop_pairs(pe, body)

        def chains_pe(pe):
            for n in range(2):
                pe.wait_ge(chains_dve, 2 * n + 1)
                for m in range(2):
                    last = nc.tensor.transpose(banks(0)[0:1, m * P:m * P + SP_], chain_cols[0:SP_, 4 * n + m:4 * n + m + 1],
                                               ident[0:SP_, 0:SP_])
                last.then_inc(chains_ps, 1)
                pe.wait_ge(chains_dve, 2 * n + 2)
                nc.tensor.transpose(banks(1)[0:SP_, 0:1], chain_rows[0:1, 2, n:n + SP_],
                                    ident[0:1, 0:1]).then_inc(chains_ps, 1)

        def values_pe(pe):
            def body(i, first, last):
                for u in range(2):
                    g = 2 * i + u
                    pe.wait_ge(A1["probs"][u], 16 * (i + 1))
                    if not first:
                        pe.wait_ge(A1["message"], g - 1)
                    turned(bank[3][:, u, 0:H * GROUP], score_t[:, u, :], ident[0:H * GROUP, 0:H * GROUP]
                                        ).then_inc(A1["weights_ps"], 1)
                    pe.wait_ge(A1["message"], g + 1)
                    if not first:
                        pe.wait_ge(A1["added"], GROUP * (g - 1))
                    reduce(A1, u, bank[u], A, lambda k: message[:, u, k, :])
            loop_pairs(pe, body)

        def turn_sums(pe, O, C, width):
            def body(i, first):
                if not first:
                    pe.wait_ge(O["mixed"] if O is O2 else O["added"], i)
                turn_chunk_sums(pe, i, O, width)
            loop_chunks(pe, body)

        def turn_chunk_sums(pe, i, O, width):
            pe.wait_ge(O["staged"], i + 1)
            for t in range(CHUNK):
                last = turned(chunk_a[:, t, 0:width], stage_a[0:width, t * P:(t + 1) * P],
                                           ident[0:width, 0:width])
            last.then_inc(O["acc_ps"], 1)

        def mix_out_pe(pe):
            def body(i, first):
                if not first:
                    pe.wait_ge(O0["mixed"], i)
                turn_chunk_sums(pe, i, O0, A)
                pe.wait_ge(O0["mixed"], i + 1)
                if not first:
                    pe.wait_ge(O0["mixed_t"], i)
                for t in range(CHUNK):
                    last = turned(chunk_x[:, t * P:(t + 1) * P], chunk_m[:, t, :], ident[:])
                last.then_inc(O0["mixed_ps"], 1)
                pe.wait_ge(O0["mixed_t"], i + 1)
                if not first:
                    pe.wait_ge(O0["added"], i)
                for t in range(CHUNK):
                    last = nc.tensor.matmul(chunk_v[:, t, :], chunk_t[:, t * P:(t + 1) * P], w_o[:], start=True, stop=True)
                last.then_inc(O0["proj_ps"], 1)
            loop_chunks(pe, body)

        def mlp_pe(pe):
            pe.wait_ge(normed, 1)

            def body(i, first):
                if not first:
                    pe.wait_ge(K1["xt"], i)
                turn_nodes(pe, i, K1)
                pe.wait_ge(K1["xt"], i + 1)
                if not first:
                    pe.wait_ge(K1["hid"], i)
                nc.tensor.matmul(chunk_u, w_1n[:], chunk_t, start=True, stop=True).then_inc(K1["hid_ps"], 1)
                pe.wait_ge(K1["leaky"], i + 1)
                if not first:
                    pe.wait_ge(K1["proj"], i)
                for t in range(CHUNK):
                    nc.tensor.matmul(chunk_v[:, t, :], chunk_l[:, t * P:(t + 1) * P], w_2n[:], start=True, stop=False)
                    last = nc.tensor.matmul(chunk_v[:, t, :], ones[:], b_2n[:], start=False, stop=True)
                last.then_inc(K1["proj_ps"], 1)
            loop_chunks(pe, body)

        def gated_pe(pe):
            pe.wait_ge(w_scaled, 2)
            pe.wait_ge(K1["proj"], CHUNKS)

            def body(i, first, last_pair):
                for u in range(2):
                    g = 2 * i + u
                    pe.wait_ge(B0["edge"][u], edge_landed(i, last_pair and u == 1))
                    if not (first and u == 0):
                        pe.wait_ge(B0["edge_t"], g)
                    flat = edge_in[:, u, :, :].rearrange("p k f -> p (k f)")
                    for m in range(2):
                        last = nc.tensor.transpose(bank[2][:, 0, m * P:(m + 1) * P], flat[:, m * P:(m + 1) * P], ident[:])
                    last.then_inc(B0["edge_ps"], 1)
                    if not (first and u == 0):
                        reduce_last(pe, B0, g, 1 - u, bank[3 * (1 - u)], D, lambda k: message[:, 1 - u, k, 0:D], first)
                    pe.wait_ge(B0["edge_t"], g + 1)
                    if not (first and u == 0):
                        pe.wait_ge(B0["hid"], 2 * g)
                    for k in range(GROUP):
                        last = nc.tensor.matmul(bank[1][:, k // 4, k % 4 * P:(k % 4 + 1) * P], w_1e[:, k % (P // DE), :],
                                                edge_t[:, u, k * DE // P, :], start=True, stop=True)
                    last.then_inc(B0["hid_ps"], 1)
                    pe.wait_ge(B0["hid"], 2 * (g + 1))
                    if not (first and u == 0):
                        pe.wait_ge(B0["message"], g)
                    for k in range(GROUP):
                        to = bank[2][:, 1, k * D:(k + 1) * D]
                        nc.tensor.matmul(to, hidden_t[:, u, k, :], w_2e[:], start=True, stop=False)
                        last = nc.tensor.matmul(to, ones[:], b_2e[:], start=False, stop=True)
                    last.then_inc(B0["edge_mm"], 1)
            loop_pairs(pe, body)
            pe.wait_ge(B0["message"], GROUPS)
            pe.wait_ge(B0["added"], GROUP * (GROUPS - 2))
            reduce(B0, 1, bank[3], D, lambda k: message[:, 1, k, 0:D])

        def reduce_last(pe, C, g, v, to, width, of, no_wait):
            pe.wait_ge(C["message"], g)
            if not no_wait:
                pe.wait_ge(C["added"], GROUP * (g - 2) + 1)
            reduce(C, v, to, width, of)

        def attend_pe(pe):
            pe.wait_ge(K2["proj"], 2 * CHUNKS)

            def body(i, first, last_pair):
                for u in range(2):
                    g = 2 * i + u
                    start = first and u == 0
                    pe.wait_ge(C0["onehot"], g + 1)
                    if not start:
                        pe.wait_ge(C0["onehot_t"], g)
                    turn_onehots(C0, u, bank[1])
                    pe.wait_ge(C0["edge"][u], edge_landed(i, last_pair and u == 1))
                    if not start:
                        pe.wait_ge(C0["edge_t"], g)
                    for m in range(4):
                        last = nc.tensor.transpose(bank[3][:, 0, m * P:(m + 1) * P],
                                                   edge_in[:, u, 2 * m:2 * m + 2, :].rearrange("p k f -> p (k f)"), ident[:])
                    last.then_inc(C0["edge_ps"], 1)
                    if not start:
                        pe.wait_ge(C0["message"], g)
                        if not (first and u == 1):
                            pe.wait_ge(C0["added"], GROUP * (g - 1))
                        reduce(C0, 1 - u, bank[0], A, lambda k: message[:, 1 - u, k, :])
                    pe.wait_ge(C0["onehot_t"], g + 1)
                    pe.wait_ge(C0["window"][u], landed(i))
                    if not start:
                        pe.wait_ge(C0["chain"], CHAIN2 * g)
                    expand(C0, u, bank[2][:, 0, :])
                    pe.wait_ge(C0["edge_t"], g + 1)
                    for m in range(GROUP // 2):
                        last = nc.tensor.matmul(bank[2][:, 1, m * 2 * D:(m + 1) * 2 * D], edge_t[:, u, m, :], w_e[:],
                                                start=True, stop=True)
                    last.then_inc(C0["edge_mm"], 1)
            loop_pairs(pe, body)
            pe.wait_ge(C0["message"], GROUPS)
            pe.wait_ge(C0["added"], GROUP * (GROUPS - 1))
            reduce(C0, 1, bank[0], A, lambda k: message[:, 1, k, :])

        def gin_pe(pe, G):
            def body(i, first, last):
                for u in range(2):
                    g = 2 * i + u
                    pe.wait_ge(G["onehot"], g + 1)
                    pe.wait_ge(G["gathered"][u], landed(i))
                    if not first:
                        pe.wait_ge(G["added"], GROUP * (g - 1))
                    reduce(G, u, bank[u], D, lambda k: gathered_rows(u, D)[:, k, :])
            loop_pairs(pe, body)

        def gin_mid_pe(pe):
            def body(i, first):
                if not first:
                    pe.wait_ge(M3["sum"], i)
                turn_nodes(pe, i, M3)
                pe.wait_ge(M3["sum"], i + 1)
                if not first:
                    pe.wait_ge(M3["hid"], i)
                nc.tensor.matmul(chunk_u, w_g1[:], chunk_t, start=True, stop=True).then_inc(M3["hid_ps"], 1)
                pe.wait_ge(M3["hid"], i + 1)
                if not first:
                    pe.wait_ge(M3["proj"], i)
                for t in range(CHUNK):
                    last = nc.tensor.matmul(chunk_v[:, t, :], chunk_h[:, t * P:(t + 1) * P], w_g2[:], start=True, stop=True)
                last.then_inc(M3["proj_ps"], 1)
            loop_chunks(pe, body)

        def clear_sums():
            nc.vector.memset(acc[:], 0.0).then_inc(zeroed, 1)

        roots = [0]

        def layer_norm(dve, v, link, signal):
            mean, var = stats[:, 0, :], stats[:, 1, :]
            link(nc.vector.tensor_reduce(mean, v, AX, ALU.add))
            link(nc.vector.tensor_scalar_mul(mean, mean, 1.0 / D))
            link(nc.vector.tensor_tensor(v, v, mean.unsqueeze(2).to_broadcast([P, NODE_TILES, D]), ALU.subtract))
            link(nc.vector.tensor_tensor(squares, v, v, ALU.mult))
            link(nc.vector.tensor_reduce(var, squares, AX, ALU.add))
            nc.vector.tensor_scalar(var, var, 1.0 / D, EPS, ALU.mult, ALU.add).then_inc(variance, 1)
            roots[0] += 1
            dve.wait_ge(root, roots[0])
            link(nc.vector.reciprocal(var, var))
            last = nc.vector.tensor_tensor(v, v, var.unsqueeze(2).to_broadcast([P, NODE_TILES, D]), ALU.mult)
            if signal:
                last.then_inc(normed, 1)
            else:
                link(last)

        def quotients(dve, O, i, first, to, eps):
            if not first:
                dve.wait_ge(O["mixed_ps"] if O is O0 else O["mixed"], i)
            nc.vector.tensor_scalar_add(chunk_d, chunk_a[:, :, D:A], eps).then_inc(O["den"], 1)
            dve.wait_ge(O["den"], 2 * i + 1)
            nc.vector.reciprocal(chunk_d, chunk_d).then_inc(O["den"], 1)
            dve.wait_ge(O["den"], 2 * i + 2)
            nc.vector.tensor_tensor(heads(to), heads(chunk_a[:, :, 0:D]), chunk_d.unsqueeze(3).to_broadcast([P, CHUNK, H, DH]),
                                    ALU.mult).then_inc(O["mixed"], 1)

        def one_hots(dve, C, g, u):
            nc.vector.tensor_tensor(onehot[:, u, :, :], iota[:].unsqueeze(1).to_broadcast([P, GROUP, P]),
                                    dst_rel[:, bass.ds(g * GROUP, GROUP)].unsqueeze(2).to_broadcast([P, GROUP, P]),
                                    ALU.is_equal).then_inc(C["onehot"], 1)

        def add_sums(dve, C, g, ps, width, regs, first):
            dve.wait_ge(C["reduced"], g + 1)
            dve.load(regs, starts[0:1, bass.ds(g * GROUP, GROUP)])
            for k in range(GROUP):
                at = dve.snap(regs[k], min_val=0, max_val=N - 1)
                if not (first and k == 0):
                    dve.wait_ge(C["added"], g * GROUP + k)
                to = acc[0:width, bass.ds(at, P)]
                nc.vector.tensor_tensor(to, to, ps[0:width, k // 4, k % 4 * P:(k % 4 + 1) * P], ALU.add).then_inc(C["added"], 1)

        def weighted(dve, u, values):
            return nc.vector.tensor_tensor(heads(message[:, u, :, 0:D]), heads(values),
                                           message[:, u, :, D:A].unsqueeze(3).to_broadcast([P, GROUP, H, DH]), ALU.mult)

        def scores_dve(dve):
            def body(i, first, last):
                for u in range(2):
                    g = 2 * i + u
                    if not first:
                        dve.wait_ge(A0["onehot_ps"], g - 1)
                    one_hots(dve, A0, g, u)
                    dve.wait_ge(A0["expanded"], g + 1)
                    dve.wait_ge(A0["gathered"][u], landed(i))
                    if not first:
                        dve.wait_ge(A0["score"], g - 1)
                    nc.vector.tensor_tensor(product[:, u, :, :], rows[:, u, :, 0:D],
                                            bank[2][:, u, :].rearrange("p (k f) -> p k f", k=GROUP), ALU.mult
                                            ).then_inc(A0["product"], 1)
                    dve.wait_ge(A0["product"], g + 1)
                    if not first:
                        dve.wait_ge(A0["score_ps"], g - 1)
                    nc.vector.tensor_reduce(score[:, u, :].rearrange("p (h k) -> p k h", h=H),
                                            heads(product[:, u, :, :]), AX, ALU.add).then_inc(A0["score"], 1)
            loop_pairs(dve, body)

        def maxima_dve(dve, link):
            dve.wait_ge(lines_in, 16 * 3 * H)
            cuts = line_r
            flat = line_d[:, 0:LEN]
            cols = chain_cols[0:SP_, :]
            single = cols[:, 7:8]
            n = 0
            link(nc.vector.tensor_tensor(single, line_d[:, 1:2], line_d[:, LEN:LEN + 1], ALU.not_equal))
            link(nc.vector.tensor_scalar_mul(single, single, -BIG))
            link(nc.vector.tensor_tensor(cuts[:, 0:LEN + 1], line_d[:, 1:LEN + 2], line_d[:, 0:LEN + 1], ALU.not_equal))
            link(nc.vector.tensor_scalar_mul(cuts[:, 0:LEN + 1], cuts[:, 0:LEN + 1], -BIG))
            ways = [(line_s, cuts[:, 0:LEN], slice(None), cuts[:, 0:1], flat[:, LEN - 1:LEN]),
                    (flat, cuts[:, 1:LEN + 1], slice(None, None, -1), cuts[:, LEN:LEN + 1], flat[:, 0:1])]
            for n, (of, cut, way, edge, last) in enumerate(ways):
                link(nc.vector.tensor_tensor_scan(flat[:, way], cut[:, way], of[:, way], -BIG, ALU.add, ALU.max))
                link(nc.vector.tensor_copy(cols[:, 4 * n:4 * n + 1], last))
                nc.vector.tensor_tensor(cols[:, 4 * n + 1:4 * n + 2], edge, single, ALU.add).then_inc(chains_dve, 1)
                dve.wait_ge(chains_ps, 2 * n + 1)
                link(nc.vector.tensor_copy(chain_rows[0:1, 0:2, 0:SP_],
                                           banks(0)[0:1, 0:2 * P].rearrange("p (m s) -> p m s", m=2)[:, :, 0:SP_]))
                link(nc.vector.memset(chain_rows[0:1, 2, :], -BIG))
                carry = chain_rows[0:1, 2, 1 - n:1 - n + SP_]
                nc.vector.tensor_tensor_scan(carry[:, way], chain_rows[0:1, 1, 0:SP_][:, way],
                                             chain_rows[0:1, 0, 0:SP_][:, way], -BIG, ALU.add, ALU.max
                                             ).then_inc(chains_dve, 1)
                dve.wait_ge(chains_ps, 2 * n + 2)
                link(nc.vector.tensor_copy(cols[:, 4 * n + 2:4 * n + 3], banks(1)[0:SP_, 0:1]))
                link(nc.vector.tensor_tensor_scan(flat[:, way], cut[:, way], flat[:, way],
                                                  cols[:, 4 * n + 2:4 * n + 3], ALU.add, ALU.max))
            nc.vector.scalar_tensor_tensor(flat, flat, -1.0e9, line_s, ALU.max, ALU.subtract).then_inc(lines_less, 1)

        def values_dve(dve, regs):
            dve.wait_ge(zeroed, 1)

            def body(i, first, last):
                for u in range(2):
                    g = 2 * i + u
                    if not first:
                        dve.wait_ge(A1["reduced"], g - 1)
                    one_hots(dve, A1, g, u)
                    dve.wait_ge(A1["weights_ps"], g + 1)
                    nc.vector.tensor_copy(message[:, u, :, D:A], bank[3][:, u, 0:H * GROUP].rearrange("p (h k) -> p k h", h=H)
                                          ).then_inc(A1["weights"], 1)
                    dve.wait_ge(A1["weights"], g + 1)
                    dve.wait_ge(A1["edge"][u], 16 * (i + 1))
                    weighted(dve, u, edge_in[:, u, :, :]).then_inc(A1["message"], 1)
                    if not (first and u == 0):
                        add_sums(dve, A1, g - 1, bank[1 - u], A, regs, first and u == 1)
            loop_pairs(dve, body)
            add_sums(dve, A1, GROUPS - 1, bank[1], A, regs, False)

        def gated_dve(dve, regs):
            dve.wait_ge(zeroed, 2)

            def body(i, first, last):
                for u in range(2):
                    g = 2 * i + u
                    if not first:
                        dve.wait_ge(B0["reduced"], g - 1)
                    one_hots(dve, B0, g, u)
                    if not (first and u == 0):
                        add_sums(dve, B0, g - 1, bank[3 * (1 - u)], D, regs, first and u == 1)
                    dve.wait_ge(B0["edge_mm"], g + 1)
                    dve.wait_ge(B0["gathered"][u], landed(i))
                    nc.vector.tensor_tensor(message[:, u, :, 0:D], gathered_rows(u, D),
                                            bank[2][:, 1, :].rearrange("p (k f) -> p k f", k=GROUP), ALU.mult
                                            ).then_inc(B0["message"], 1)
            loop_pairs(dve, body)
            add_sums(dve, B0, GROUPS - 1, bank[3], D, regs, False)

        def attend_dve(dve, regs):
            dve.wait_ge(zeroed, 3)

            def body(i, first, last):
                for u in range(2):
                    g = 2 * i + u
                    if not first:
                        dve.wait_ge(C0["reduced"], g - 1)
                    one_hots(dve, C0, g, u)
                    if not (first and u == 0):
                        add_sums(dve, C0, g - 1, bank[0], A, regs, first and u == 1)
                    dve.wait_ge(C0["expanded"], g + 1)
                    dve.wait_ge(C0["gathered"][u], landed(i))
                    qd = bank[2][:, 0, :].rearrange("p (k f) -> p k f", k=GROUP)
                    ee = bank[2][:, 1, :].rearrange("p (k f) -> p k f", k=GROUP)
                    nc.vector.tensor_tensor(product[:, u, :, :], rows[:, u, :, 0:D], qd, ALU.mult).then_inc(C0["chain"], 1)
                    dve.wait_ge(C0["chain"], CHAIN2 * g + 1)
                    dve.wait_ge(C0["edge_mm"], g + 1)
                    nc.vector.tensor_tensor(product[:, u, :, :], product[:, u, :, :], ee, ALU.mult).then_inc(C0["chain"], 1)
                    dve.wait_ge(C0["chain"], CHAIN2 * g + 2)
                    if not first:
                        dve.wait_ge(C0["weights"], g - 1)
                    nc.vector.tensor_reduce(score[:, u, :].rearrange("p (k h) -> p k h", h=H),
                                            heads(product[:, u, :, :]), AX, ALU.add).then_inc(C0["chain"], 1)
                    dve.wait_ge(C0["chain"], CHAIN2 * g + 3)
                    nc.vector.tensor_scalar(score[:, u, :], score[:, u, :], 5.0 * DH ** 0.5, -5.0 * DH ** 0.5,
                                            ALU.min, ALU.max).then_inc(C0["chain"], 1)
                    dve.wait_ge(C0["weights"], g + 1)
                    weighted(dve, u, rows[:, u, :, D:2 * D]).then_inc(C0["message"], 1)
            loop_pairs(dve, body)
            add_sums(dve, C0, GROUPS - 1, bank[0], A, regs, False)

        def gin_dve(dve, G, regs):
            dve.wait_ge(zeroed, 4 if G is G0 else 5)

            def body(i, first, last):
                for u in range(2):
                    g = 2 * i + u
                    if not first:
                        dve.wait_ge(G["reduced"], g - 1)
                    one_hots(dve, G, g, u)
                    if not (first and u == 0):
                        add_sums(dve, G, g - 1, bank[1 - u], D, regs, first and u == 1)
            loop_pairs(dve, body)
            add_sums(dve, G, GROUPS - 1, bank[1], D, regs, False)

        @block.sync
        def _(sp):
            sp.wait_ge(filled, 1)
            for nat, v in ((nat_src, src), (nat_dst, dst)):
                for where, part in blocks_of(v):
                    sp.dma_start(nat[where], part).then_inc(graph_in, 16)
            with sp.Fori(0, NFULL // CHUNK) as i:
                sp.dma_start(nodes[:, tiles(i), :], x[bass.ds(i * CP, CP), :].rearrange("(t p) d -> p t d", p=P)
                             ).then_inc(nodes_in, 16)
            sp.dma_start(nodes[0:NREM, NFULL, :], x[NFULL * P:N, :]).then_inc(nodes_in, 16)
            for to, v in weight_loads:
                sp.dma_start(to, v).then_inc(weights_in, 16)
            sp.wait_ge(graph_cast, 2)
            sp.dma_start(dst_line[0:1, 0:P], minus).then_inc(lines_out, 16)
            sp.dma_start(dst_line[0:1, P:P + NAT * P * P].rearrange("a (c p e) -> (a p) c e", p=P, e=P), flt_dst).then_inc(lines_out, 16)
            sp.dma_start(start_line.rearrange("c p -> p c"), start_i, allow_slow_non_contiguous=True).then_inc(lines_out, 16)
            for g in range(GROUPS, SG):
                sp.dma_start(s_edges[g], blank).then_inc(lines_out, 16)
            sp.wait_ge(lines_out, LINES_OUT)
            sp.dma_start(starts[:], start_line.rearrange("c p -> (c p)").rearrange("(a n) -> a n", a=1)).then_inc(starts_in, 16)

            store_tables(sp, K0, 2)
            sp.wait_ge(starts_in, 16)
            score_regs = [sp.alloc_register(f"sp_start{k}") for k in range(GROUP)]
            load_windows(sp, A0, score_regs, None)
            probabilities_dma(sp)
            values_dma(sp)
            store_tables(sp, K1, 1)
            gated_dma(sp)
            store_tables(sp, K2, 2)
            load_windows(sp, C0, score_regs, edge_attr_64)
            sp.wait_ge(normed, 3)
            sp.dma_start(x3_table.rearrange("(t p) d -> p t d", p=P), nodes[:]).then_inc(stored, 16)
            sp.wait_ge(M3["proj"], CHUNKS)
            sp.dma_start(y3_table.rearrange("(t p) d -> p t d", p=P), mix).then_inc(stored, 16)
            sp.wait_ge(normed, 4)
            sp.dma_start(out[0:NFULL * P, :].rearrange("(t p) d -> p t d", p=P), nodes[:, 0:NFULL, :]).then_inc(stored, 16)
            sp.dma_start(out[NFULL * P:N, :], nodes[0:NREM, NFULL, :]).then_inc(stored, 16)
            sp.wait_ge(stored, 64)

        @block.gpsimd
        def _(pool):
            nc.gpsimd.memset(ones[:], 1.0).then_inc(consts, 1)
            nc.gpsimd.memset(ident[:], 0.0).then_inc(consts, 1)
            nc.gpsimd.iota(iota[:], pattern=[[1, P]], base=0, channel_multiplier=0,
                           allow_small_or_imprecise_dtypes=True).then_inc(consts, 1)
            pool.wait_ge(consts, 3)
            nc.gpsimd.affine_select(out=ident[:], in_=ident[:], compare_op=ALU.not_equal, fill=1.0, base=0,
                                    pattern=[[-1, P]], channel_multiplier=1).then_inc(consts, 1)
            pool.wait_ge(graph_out, 2)
            pool.wait_ge(K0["table"], 32 * CHUNKS)
            gather(pool, A0, kv_table, 2 * D, [(A0["product"], 1), (A0["spilled"], 16)])
            pool.wait_ge(K1["table"], 16 * CHUNKS)
            gather(pool, B0, xt_table, D, [(B0["message"], 1)])
            pool.wait_ge(K2["table"], 32 * CHUNKS)
            gather(pool, C0, kv_table, 2 * D, [(C0["message"], 1)])
            pool.wait_ge(stored, 16)
            gather(pool, G0, x3_table, D, [(G0["reduced"], 1)])
            pool.wait_ge(stored, 32)
            gather(pool, G1, y3_table, D, [(G1["reduced"], 1)])

        @block.scalar
        def _(act):
            act.wait_ge(graph_ps, 1)
            for b in range(2):
                n = min(NATW - b * 1024, 1024)
                last = nc.scalar.copy(dst_rel[:, b * 1024:b * 1024 + n],
                                      bank[b][:].rearrange("p a b -> p (a b)")[:, 0:n])
            last.then_inc(graph_out, 1)
            for b in range(2):
                n = min(NATW - b * 1024, 1024)
                last = nc.scalar.copy(src_idx[:, b * 1024:b * 1024 + n],
                                      bank[2 + b][:].rearrange("p a b -> p (a b)")[:, 0:n])
            last.then_inc(graph_out, 1)
            act.wait_ge(weights_ps, 1)
            nc.scalar.copy(w_2[:], banks(0)[0:D, 0:3 * D]).then_inc(weights_t, 1)
            nc.scalar.copy(w_e[0:D, 0:D], banks(0)[0:D, 3 * D:4 * D]).then_inc(weights_t, 1)
            nc.scalar.copy(w_e[D:P, D:2 * D], banks(0)[0:D, 3 * D:4 * D]).then_inc(weights_t, 1)
            act.wait_ge(nodes_in, NODES_IN)
            act.wait_ge(lines_out, LINES_OUT)
            copy_projections(act, K0, 2)
            scores_act(act)
            act.wait_ge(lines_less, 1)
            nc.scalar.activation(line_r[:, 0:LEN], line_d[:, 0:LEN], ACT.Exp, scale=-1.0).then_inc(lines_exp, 1)
            mixed_act(act)
            square_root(act, 1)
            mlp_act(act)
            gated_act(act)
            stage_act(act, O1, B0, D)
            square_root(act, 2)
            square_root(act, 3)
            act.wait_ge(normed, 2)
            copy_projections(act, K2, 2)
            attend_act(act)
            stage_act(act, O2, C0, A)
            square_root(act, 4)
            gin_act(act)
            stage_act(act, O3, G1, D)
            square_root(act, 5)

        @block.tensor
        def _(pe):
            pe.wait_ge(consts, 4)
            pe.wait_ge(graph_cast, 3)
            for c in range(NAT):
                nc.tensor.transpose(bank[c // 8][:, c // 4 % 2, c % 4 * P:(c % 4 + 1) * P], flt_rel[:, c, :], ident[:])
                last = nc.tensor.transpose(bank[2 + c // 8][:, c // 4 % 2, c % 4 * P:(c % 4 + 1) * P], flt_src[:, c, :], ident[:])
            last.then_inc(graph_ps, 1)
            pe.wait_ge(weights_in, WEIGHTS_IN)
            pe.wait_ge(graph_out, 2)
            for n in range(4):
                last = nc.tensor.transpose(banks(0)[0:D, n * D:(n + 1) * D], w_nat[:, n * D:(n + 1) * D], ident[0:D, 0:D])
            last.then_inc(weights_ps, 1)
            pe.wait_ge(weights_t, 3)
            project(pe, K0, w_qkv)
            scores_pe(pe)
            chains_pe(pe)
            values_pe(pe)
            mix_out_pe(pe)
            mlp_pe(pe)
            gated_pe(pe)
            turn_sums(pe, O1, B0, D)
            pe.wait_ge(normed, 2)
            project(pe, K2, w_2)
            attend_pe(pe)
            turn_sums(pe, O2, C0, A)
            gin_pe(pe, G0)
            gin_mid_pe(pe)
            gin_pe(pe, G1)
            turn_sums(pe, O3, G1, D)

        @block.vector
        def _(dve):
            steps = [0]

            def link(ins):
                steps[0] += 1
                ins.then_inc(norm, 1)
                dve.wait_ge(norm, steps[0])

            regs = [dve.alloc_register(f"dve_start{k}") for k in range(GROUP)]
            nc.vector.memset(nat_src, 0)
            nc.vector.memset(nat_dst, 4 * NPAD)
            nc.vector.memset(nodes[:], 0.0)
            nc.vector.memset(minus, -1.0)
            nc.vector.memset(w_1e[:], 0.0)
            nc.vector.memset(w_e[:], 0.0)
            nc.vector.memset(blank, 0.0).then_inc(filled, 1)
            nc.vector.memset(acc[:], 0.0).then_inc(zeroed, 1)
            dve.wait_ge(graph_in, GRAPH_IN)
            link(nc.vector.tensor_copy(flt_dst, nat_dst))
            link(nc.vector.tensor_scalar_min(start_f, flt_dst[:, :, 0], float(N - 1)))
            nc.vector.tensor_copy(start_i, start_f).then_inc(graph_cast, 1)
            nc.vector.tensor_copy(flt_src, nat_src).then_inc(graph_cast, 1)
            nc.vector.tensor_tensor(flt_rel, flt_dst, start_f.unsqueeze(2).to_broadcast([P, NAT, P]),
                                    ALU.subtract).then_inc(graph_cast, 1)
            dve.wait_ge(weights_in, WEIGHTS_IN)
            nc.vector.tensor_tensor(gain[:], gains[:, 0:1], gains[:, 1:2], ALU.mult).then_inc(w_scaled, 1)
            nc.vector.tensor_scalar_mul(w_2e[0:D, :], w_2e[0:D, :], SLOPE)
            nc.vector.tensor_scalar_mul(w_2e[D:P, :], w_2e[D:P, :], 1.0 - SLOPE).then_inc(w_scaled, 1)
            dve.wait_ge(graph_out, 2)
            dve.wait_ge(consts, 4)

            scores_dve(dve)
            maxima_dve(dve, link)
            values_dve(dve, regs)

            def mixed(i, first):
                dve.wait_ge(O0["acc_ps"], i + 1)
                quotients(dve, O0, i, first, chunk_m, 1e-9)
                dve.wait_ge(O0["proj_ps"], i + 1)
                nc.vector.tensor_tensor(nodes[:, tiles(i), :], nodes[:, tiles(i), :], chunk_v, ALU.add).then_inc(O0["added"], 1)
            loop_chunks(dve, mixed)
            dve.wait_ge(O0["added"], CHUNKS)
            clear_sums()
            layer_norm(dve, nodes[:], link, True)

            def leaky(i, first):
                dve.wait_ge(K1["hid"], i + 1)
                if not first:
                    dve.wait_ge(K1["proj_ps"], i)
                nc.vector.scalar_tensor_tensor(chunk_l, chunk_h, SLOPE, chunk_h, ALU.mult, ALU.max).then_inc(K1["leaky"], 1)
            loop_chunks(dve, leaky)
            gated_dve(dve, regs)

            def gated_out(i, first):
                dve.wait_ge(O1["acc_ps"], i + 1)
                nc.vector.scalar_tensor_tensor(mix[:, tiles(i), :], chunk_a[:, :, 0:D], gain[:, 0:1],
                                               nodes[:, tiles(i), :], ALU.mult, ALU.add).then_inc(O1["added"], 1)
            loop_chunks(dve, gated_out)
            dve.wait_ge(O1["added"], CHUNKS)
            clear_sums()
            layer_norm(dve, mix, link, False)
            link(nc.vector.tensor_tensor(mix, mix, gamma[:].unsqueeze(1).to_broadcast([P, NODE_TILES, D]), ALU.mult))
            link(nc.vector.tensor_tensor(mix, mix, beta[:].unsqueeze(1).to_broadcast([P, NODE_TILES, D]), ALU.add))
            link(nc.vector.tensor_tensor(nodes[:], nodes[:], mix, ALU.add))
            layer_norm(dve, nodes[:], link, True)
            attend_dve(dve, regs)

            def attend_out(i, first):
                dve.wait_ge(O2["acc_ps"], i + 1)
                quotients(dve, O2, i, first, mix[:, tiles(i), :], 1e-6)
            loop_chunks(dve, attend_out)
            dve.wait_ge(O2["mixed"], CHUNKS)
            clear_sums()
            link(nc.vector.tensor_tensor(nodes[:], nodes[:], mix, ALU.add))
            layer_norm(dve, nodes[:], link, True)
            gin_dve(dve, G0, regs)

            def gin_sum(i, first):
                dve.wait_ge(M3["xt_ps"], i + 1)
                if not first:
                    dve.wait_ge(M3["hid_ps"], i)
                nc.vector.tensor_tensor(chunk_t, chunk_x, acc[0:D, bass.ds(i * CP, CP)], ALU.add).then_inc(M3["sum"], 1)
            loop_chunks(dve, gin_sum)
            dve.wait_ge(M3["sum"], CHUNKS)
            clear_sums()
            gin_dve(dve, G1, regs)

            def gin_out(i, first):
                dve.wait_ge(O3["acc_ps"], i + 1)
                nc.vector.tensor_tensor(mix[:, tiles(i), :], mix[:, tiles(i), :], chunk_a[:, :, 0:D], ALU.add).then_inc(O3["added"], 1)
            loop_chunks(dve, gin_out)
            dve.wait_ge(O3["added"], CHUNKS)
            link(nc.vector.tensor_tensor(mix, mix, b_g2[:].unsqueeze(1).to_broadcast([P, NODE_TILES, D]), ALU.add))
            link(nc.vector.tensor_tensor(nodes[:], nodes[:], mix, ALU.add))
            layer_norm(dve, nodes[:], link, True)


_INS = ["x", "src", "dst", "edge_attr_32", "edge_attr_64",
        "L0_gnn_Wq", "L0_gnn_Wk", "L0_gnn_Wv", "L0_gnn_Wo",
        "L1_gnn_W1n", "L1_gnn_b1n", "L1_gnn_W2n", "L1_gnn_b2n", "L1_gnn_W1e", "L1_gnn_b1e",
        "L1_gnn_W2e", "L1_gnn_b2e", "L1_gnn_res_w", "L1_gnn_dp_scale", "L1_gnn_gamma", "L1_gnn_beta",
        "L2_gnn_Wq", "L2_gnn_Wk", "L2_gnn_We", "L2_gnn_Wv",
        "L3_gnn_W1", "L3_gnn_b1", "L3_gnn_W2", "L3_gnn_b2"]


def kernel(**inputs):
    import numpy as _np
    import concourse.bacc as _bacc
    from concourse import mybir as _mybir
    from concourse.bass_utils import run_bass_kernel_spmd as _run

    nc = _bacc.Bacc("TRN2", target_bir_lowering=False, num_devices=1)
    arrays, args = {}, []
    for name in _INS:
        a = _np.ascontiguousarray(inputs[name])
        arrays[f"in_{name}_dram"] = a
        args.append(nc.dram_tensor(f"in_{name}_dram", a.shape, _mybir.dt.from_np(a.dtype), kind="ExternalInput").ap())
    shape = tuple(inputs["x"].shape)
    args.append(nc.dram_tensor("out_0_dram", shape, _mybir.dt.float32, kind="ExternalOutput").ap())
    build_gnn(nc, *args)
    r = _run(nc, [arrays], core_ids=[0])
    return r.results[0]["out_0_dram"]
```

```python
import concourse.bass as bass
from concourse import mybir
from contextlib import ExitStack

P = 128
GROUP = 8
CHUNK = 4
INDEXES = 4
BIG = 1.0e30
SLOPE = 0.1
EPS = 1.0e-5
CHAIN2 = 4


def build_gnn(nc, x, src, dst, edge_attr_32, edge_attr_64,
              L0_gnn_Wq, L0_gnn_Wk, L0_gnn_Wv, L0_gnn_Wo,
              L1_gnn_W1n, L1_gnn_b1n, L1_gnn_W2n, L1_gnn_b2n, L1_gnn_W1e, L1_gnn_b1e,
              L1_gnn_W2e, L1_gnn_b2e, L1_gnn_res_w, L1_gnn_dp_scale, L1_gnn_gamma, L1_gnn_beta,
              L2_gnn_Wq, L2_gnn_Wk, L2_gnn_We, L2_gnn_Wv,
              L3_gnn_W1, L3_gnn_b1, L3_gnn_W2, L3_gnn_b2, out):
    f32, i32 = mybir.dt.float32, mybir.dt.int32
    ALU, ACT, AX = mybir.AluOpType, mybir.ActivationFunctionType, mybir.AxisListType.X

    N, D = x.shape
    E = src.shape[0]
    H = 4
    DH = D // H
    DE = edge_attr_32.shape[1]
    HID = L3_gnn_W1.shape[1]
    A = D + H

    TILES = -(-E // P)
    GROUPS = -(-TILES // GROUP)
    GROUPS += GROUPS % 2
    PAIRS = GROUPS // 2
    assert (GROUPS - 2) % INDEXES == 0
    EG = GROUP * P
    LAST = GROUPS - 1
    TAIL_TILES = (E - LAST * EG) // P
    TAIL_ROWS = (E - LAST * EG) % P
    assert 0 < TAIL_TILES < GROUP and TAIL_ROWS

    CG = 7
    CHAINS = -(-GROUPS // CG)
    SG = CHAINS * CG
    LEN = CG * EG
    SP_ = H * CHAINS
    assert SP_ <= P

    NAT = -(-SG * GROUP // P)
    FULL = TILES - 1
    NODE_TILES = -(-(N + P) // P)
    NODE_TILES += -NODE_TILES % CHUNK
    CHUNKS = NODE_TILES // CHUNK
    NPAD = NODE_TILES * P
    NREM = N % P
    NFULL = N // P
    CD = CHUNK * D
    CP = CHUNK * P

    def dram(name, shape, dt=f32):
        return nc.dram_tensor(name, shape, dt, kind="Internal").ap()

    kv_table = dram("kv_table", [NPAD, 2 * D])
    q_table = dram("q_table", [NPAD, D])
    kv2_table = dram("kv2_table", [NPAD, 2 * D])
    q2_table = dram("q2_table", [NPAD, D])
    xt_table = dram("xt_table", [NPAD, D])
    x3_table = dram("x3_table", [NPAD, D])
    y3_table = dram("y3_table", [NPAD, D])
    v_edges = dram("v_edges", [GROUPS, P, GROUP * D])
    s_edges = dram("s_edges", [SG, H * GROUP, P])
    p_edges = dram("p_edges", [SG, H * GROUP, P])
    dst_line = dram("dst_line", [1, P + NAT * P * P + LEN])
    start_line = dram("start_line", [NAT, P], i32)

    ctx = ExitStack()
    with ctx:
        def sb(name, shape, dt=f32):
            return ctx.enter_context(nc.sbuf_tensor(name, shape, dt))

        def sem(name):
            return ctx.enter_context(nc.semaphore(name))

        def sems(prefix, names):
            return {n: sem(f"{prefix}_{n}") for n in names.split()}

        src_idx = sb("src_idx", [P, NAT * P], i32)
        dst_rel = sb("dst_rel", [P, NAT * P])
        starts = sb("starts", [1, NAT * P], i32)
        nodes = sb("nodes", [P, NODE_TILES, D])
        acc = sb("acc", [P, NPAD])
        ident = sb("ident", [P, P])
        iota = sb("iota", [P, P])
        ones = sb("ones", [1, P])
        w_qkv = sb("w_qkv", [D, 3 * D])
        w_o = sb("w_o", [D, D])
        w_1n = sb("w_1n", [D, HID])
        w_2n = sb("w_2n", [HID, D])
        w_1e = sb("w_1e", [P, P // DE, 2 * D])
        w_2e = sb("w_2e", [P, D])
        w_nat = sb("w_nat", [D, 4 * D])
        w_2 = sb("w_2", [D, 3 * D])
        w_e = sb("w_e", [P, 2 * D])
        w_g1 = sb("w_g1", [D, HID])
        w_g2 = sb("w_g2", [HID, D])
        b_1n = sb("b_1n", [HID, 1])
        b_1e = sb("b_1e", [P, 1])
        b_g1 = sb("b_g1", [HID, 1])
        b_2n = sb("b_2n", [1, D])
        b_2e = sb("b_2e", [1, D])
        b_g2 = sb("b_g2", [P, D])
        gamma = sb("gamma", [P, D])
        beta = sb("beta", [P, D])
        gains = sb("gains", [P, 2])
        gain = sb("gain", [P, 1])
        index = sb("index", [P, INDEXES, GROUP], i32)
        rows = sb("rows", [P, 2, GROUP, 2 * D])
        window = sb("window", [P, 2, GROUP, D])
        onehot = sb("onehot", [P, 2, GROUP, P])
        onehot_t = sb("onehot_t", [P, 2, GROUP, P])
        message = sb("message", [P, 2, GROUP, A])
        product = sb("product", [P, 2, GROUP, D])
        score = sb("score", [P, 2, H * GROUP])
        score_t = sb("score_t", [H * GROUP, 2, P])
        edge_in = sb("edge_in", [P, 2, GROUP, D])
        edge_t = sb("edge_t", [P, 2, 4, P])
        hidden_t = onehot_t
        big = sb("big", [P, 3 * (LEN + 2)])
        line_s = big[0:SP_, 0:LEN]
        line_d = big[0:SP_, LEN:2 * LEN + 2]
        line_r = big[0:SP_, 2 * LEN + 2:3 * LEN + 4]
        chain_cols = sb("chain_cols", [P, 8])
        chain_rows = sb("chain_rows", [1, 4, P])

        bank = [ctx.enter_context(nc.psum_tensor(f"bank{i}", [P, 2, 512], f32)) for i in range(4)]

        def banks(n, k=1):
            return bank[n // 2][:, n % 2, :] if k == 1 else bank[n // 2][:].rearrange("p a b -> p (a b)")

        block = ctx.enter_context(nc.Block())


        def gathers(name):
            return [sem(f"{name}_gathered{u}") for u in range(2)]

        filled = sem("filled")
        consts = sem("consts")
        graph_in = sem("graph_in")
        weights_in = sem("weights_in")
        nodes_in = sem("nodes_in")
        graph_cast = sem("graph_cast")
        graph_ps = sem("graph_ps")
        graph_out = sem("graph_out")
        lines_out = sem("lines_out")
        starts_in = sem("starts_in")
        weights_ps = sem("weights_ps")
        weights_t = sem("weights_t")
        norm = sem("norm")
        chains_ps = sem("chains_ps")
        chains_dve = sem("chains_dve")
        lines_less = sem("lines_less")
        lines_in = sem("lines_in")
        lines_exp = sem("lines_exp")
        probs_out = sem("probs_out")
        w_scaled = sem("w_scaled")
        variance = sem("variance")
        root = sem("root")
        zeroed = sem("zeroed")
        normed = sem("normed")
        stored = sem("stored")
        K0 = sems("kv0", "staged xt_ps xt proj_ps proj table")
        O0 = sems("out0", "staged acc_ps den mixed mixed_ps mixed_t proj_ps added")
        K1 = sems("mlp1", "staged xt_ps xt hid_ps hid leaky proj_ps proj table")
        O1 = sems("out1", "staged acc_ps added")
        K2 = sems("kv2", "staged xt_ps xt proj_ps proj table")
        O2 = sems("out2", "staged acc_ps den mixed")
        M3 = sems("gin_mid", "staged part xt_ps sum hid_ps hid proj_ps proj")
        O3 = sems("out3", "staged acc_ps added")
        A0 = sems("scores", "index onehot onehot_ps onehot_t expanded product score score_ps score_t")
        A0["gathered"], A0["window"] = gathers("scores"), [sem(f"scores_window{u}") for u in range(2)]
        A0["spilled"], A0["stored"] = [sem(f"scores_v_out{u}") for u in range(2)], [sem(f"scores_out{u}") for u in range(2)]
        A1 = sems("values", "onehot weights_ps weights message reduced added")
        A1["edge"], A1["probs"] = [sem(f"values_v{u}") for u in range(2)], [sem(f"values_p{u}") for u in range(2)]
        B0 = sems("gated", "index onehot edge_ps edge_t hid_ps hid edge_mm message reduced added")
        B0["gathered"], B0["edge"] = gathers("gated"), [sem(f"gated_edge{u}") for u in range(2)]
        C0 = sems("attend", "index onehot onehot_ps onehot_t expanded edge_ps edge_t edge_mm chain weights "
                            "message reduced added")
        C0["gathered"], C0["window"] = gathers("attend"), [sem(f"attend_window{u}") for u in range(2)]
        C0["edge"] = [sem(f"attend_edge{u}") for u in range(2)]
        G0 = sems("gin_a", "index onehot reduced added")
        G0["gathered"] = gathers("gin_a")
        G1 = sems("gin_b", "index onehot reduced added")
        G1["gathered"] = gathers("gin_b")

        NATW = NAT * P
        nat_src = big[:, 0:NATW].bitcast(i32).rearrange("p (c e) -> p c e", e=P)
        nat_dst = big[:, NATW:2 * NATW].bitcast(i32).rearrange("p (c e) -> p c e", e=P)
        flt_src = big[:, 2 * NATW:3 * NATW].rearrange("p (c e) -> p c e", e=P)
        flt_dst = big[:, 3 * NATW:4 * NATW].rearrange("p (c e) -> p c e", e=P)
        flt_rel = big[:, 4 * NATW:5 * NATW].rearrange("p (c e) -> p c e", e=P)
        start_f = big[:, 5 * NATW:5 * NATW + NAT]
        start_i = big[:, 5 * NATW + NAT:5 * NATW + 2 * NAT].bitcast(i32)
        minus = big[0:1, 5 * NATW + 2 * NAT:5 * NATW + 2 * NAT + P]
        blank = big[0:H * GROUP, 5 * NATW + 2 * NAT + P:5 * NATW + 2 * NAT + 2 * P]

        W = NODE_TILES * D
        mix = big[:, 0:W].rearrange("p (t d) -> p t d", d=D)
        squares = big[:, W:2 * W].rearrange("p (t d) -> p t d", d=D)
        stats = big[:, 2 * W:2 * W + 2 * NODE_TILES].rearrange("p (a t) -> p a t", a=2)
        at = 2 * W + 2 * NODE_TILES
        chunk_t = big[0:D, at:at + CP]
        chunk_h = big[:, at + CP:at + 2 * CP]
        chunk_l = big[:, at + 2 * CP:at + 3 * CP]
        chunk_p = big[:, at + 3 * CP:at + 3 * CP + 3 * CD].rearrange("p (t f) -> p t f", f=3 * D)
        chunk_m = big[:, at + 3 * CP + 3 * CD:at + 3 * CP + 4 * CD].rearrange("p (t f) -> p t f", f=D)
        chunk_d = big[:, at + 3 * CP + 4 * CD:at + 3 * CP + 4 * CD + CHUNK * H].rearrange("p (t h) -> p t h", h=H)
        at += 3 * CP + 4 * CD + CHUNK * H
        stage_x = big[:, at:at + CD].rearrange("p (t d) -> p t d", d=D)
        stage_a = big[:, at + CD:at + CD + CP]
        assert at + CD + CP <= 3 * (LEN + 2)
        acc_odd = big[:, 3 * (LEN + 2) - NPAD:3 * (LEN + 2)]
        assert at + CD + CP <= 3 * (LEN + 2) - NPAD - CP
        stage_b = big[:, at + CD + CP:at + CD + 2 * CP]
        chunk_x = banks(0)[0:D, :]
        chunk_a = banks(1)[:, 0:CHUNK * A].rearrange("p (t f) -> p t f", f=A)
        chunk_u = banks(4)[:, :]
        chunk_v = banks(5)[:, 0:CD].rearrange("p (t f) -> p t f", f=D)

        def chunk_w(t):
            return bank[1][:, t // 2, (t % 2) * 3 * D:(t % 2 + 1) * 3 * D]

        def tiles(i):
            return bass.ds(i * CHUNK, CHUNK)

        def loop_pairs(eng, body, peeled=1):
            for i in range(peeled):
                body(i)
            with eng.Fori(peeled, PAIRS - 1) as i:
                body(i)
            body(PAIRS - 1)

        def group_at(i, u, k=0):
            return 2 * i + u + k, (u + k) % 2, i + (u + k) // 2

        def since(g, n):
            return not isinstance(g, int) or g >= n

        def is_group(g):
            return not isinstance(g, int) or g < GROUPS

        def loop_chunks(eng, body):
            body(0, True)
            with eng.Fori(1, CHUNKS) as i:
                body(i, False)

        def heads(ap):
            return ap.rearrange("p t (h d) -> p t h d", h=H)

        def blocks_of(v):
            c = FULL // P
            yield (slice(0, P), slice(0, c), slice(0, P)), v[0:c * P * P].rearrange("(c p e) -> p c e", p=P, e=P)
            yield (slice(0, FULL - c * P), c, slice(0, P)), v[c * P * P:FULL * P].rearrange("(p e) -> p e", e=P)
            yield (slice(FULL - c * P, FULL - c * P + 1), c, slice(0, E - FULL * P)), v[FULL * P:E].rearrange("(p e) -> p e", p=1)

        def row_of(v):
            return v.rearrange("(a n) -> a n", a=1)

        weight_loads = [
            (w_qkv[:, 0:D], L0_gnn_Wk), (w_qkv[:, D:2 * D], L0_gnn_Wv), (w_qkv[:, 2 * D:], L0_gnn_Wq),
            (w_o[:], L0_gnn_Wo), (w_1n[:], L1_gnn_W1n), (w_2n[:], L1_gnn_W2n),
            (w_2e[0:D, :], L1_gnn_W2e), (w_2e[D:P, :], L1_gnn_W2e),
            (w_nat[:, 0:D], L2_gnn_Wk), (w_nat[:, D:2 * D], L2_gnn_Wv), (w_nat[:, 2 * D:3 * D], L2_gnn_Wq),
            (w_nat[:, 3 * D:], L2_gnn_We), (w_g1[:], L3_gnn_W1), (w_g2[:], L3_gnn_W2),
            (b_1n[:], L1_gnn_b1n.rearrange("(n a) -> n a", a=1)),
            (b_1e[0:D, :], L1_gnn_b1e.rearrange("(n a) -> n a", a=1)),
            (b_1e[D:P, :], L1_gnn_b1e.rearrange("(n a) -> n a", a=1)),
            (b_g1[:], L3_gnn_b1.rearrange("(n a) -> n a", a=1)),
            (b_2n[:], row_of(L1_gnn_b2n)), (b_2e[:], row_of(L1_gnn_b2e)),
            (b_g2[:], row_of(L3_gnn_b2).to_broadcast([P, D])),
            (gamma[:], row_of(L1_gnn_gamma).to_broadcast([P, D])),
            (beta[:], row_of(L1_gnn_beta).to_broadcast([P, D])),
            (gains[:, 0:1], row_of(L1_gnn_dp_scale).to_broadcast([P, 1])),
            (gains[:, 1:2], row_of(L1_gnn_res_w).to_broadcast([P, 1])),
        ] + [(w_1e[DE * r:DE * (r + 1), r, D * c:D * (c + 1)], L1_gnn_W1e) for r in range(P // DE) for c in range(2)]
        WEIGHTS_IN = 16 * len(weight_loads)
        GRAPH_IN = 16 * 6
        assert NFULL % CHUNK == 0
        NODES_IN = 16 * (NFULL // CHUNK + 1)
        LINES_OUT = 16 * (3 + SG - GROUPS)

        def store_tables(sp, K, parts):
            with sp.Fori(0, CHUNKS) as i:
                sp.wait_ge(K["proj"], parts * (i + 1))
                if parts == 2:
                    sp.dma_start(kv_table.rearrange("(t p) f -> p t f", p=P)[:, tiles(i), :],
                                 chunk_p[:, :, 0:2 * D]).then_inc(K["table"], 16)
                    sp.dma_start(q_table.rearrange("(t p) f -> p t f", p=P)[:, tiles(i), :],
                                 chunk_p[:, :, 2 * D:3 * D]).then_inc(K["table"], 16)
                else:
                    sp.dma_start(xt_table.rearrange("(t p) f -> p t f", p=P)[:, tiles(i), :],
                                 chunk_p[:, :, 0:D]).then_inc(K["table"], 16)

        def load_edges(sp, C, edges, g, u):
            to = edge_in[:, u, :, :].rearrange("p k f -> p (k f)")[:, 0:GROUP * edges.shape[1]].rearrange(
                "p (k f) -> p k f", k=GROUP)
            if since(g, 2):
                sp.wait_ge(C["edge_ps"], g - 1)
            if not (isinstance(g, int) and g == LAST):
                sp.dma_start(to, edges[bass.ds(g * EG, EG), :].rearrange("(k p) f -> p k f", p=P)).then_inc(C["edge"][u], 16)
            else:
                at = LAST * EG
                sp.dma_start(to[:, 0:TAIL_TILES, :], edges[at:at + TAIL_TILES * P, :].rearrange(
                    "(k p) f -> p k f", p=P)).then_inc(C["edge"][u], 16)
                sp.dma_start(to[0:TAIL_ROWS, TAIL_TILES, :], edges[at + TAIL_TILES * P:E, :]).then_inc(C["edge"][u], 16)

        def edge_landed(g, i):
            return 16 * (i + 2) if isinstance(g, int) and g == LAST else 16 * (i + 1)

        def load_windows(sp, C, regs, edges):
            if C is A0:
                sp.wait_ge(K0["table"], 32 * CHUNKS)
            else:
                sp.wait_ge(K2["table"], 32 * CHUNKS)

            def body(i):
                for u in range(2):
                    g = 2 * i + u
                    if edges is not None:
                        load_edges(sp, C, edges, g, u)
                    if since(g, 2):
                        sp.wait_ge(C["expanded"], g - 1)
                    sp.load(regs, starts[0:1, bass.ds(g * GROUP, GROUP)])
                    for k in range(GROUP):
                        at = sp.snap(regs[k], min_val=0, max_val=N - 1)
                        sp.dma_start(window[:, u, k, :], q_table[bass.ds(at, P), :]).then_inc(C["window"][u], 16)
            loop_pairs(sp, body)

        def line_views(h):
            on = slice(h * CHAINS, (h + 1) * CHAINS)
            return (line_s[on, :].rearrange("c (g n) -> c g n", g=CG),
                    s_edges.rearrange("(c g) (h k) e -> h c g (k e)", g=CG, h=H)[h],
                    line_d[on, :],
                    line_r[on, 0:LEN].rearrange("c (g n) -> c g n", g=CG),
                    p_edges.rearrange("(c g) (h k) e -> h c g (k e)", g=CG, h=H)[h])

        def probabilities_dma(sp):
            for u in range(2):
                sp.wait_ge(A0["stored"][u], 16 * PAIRS)
            for h in range(H):
                to_s, of_s, to_d, _, _ = line_views(h)
                sp.dma_start(to_s, of_s).then_inc(lines_in, 16)
                sp.dma_start(to_d[:, 0:LEN], dst_line[0, P - 1:P - 1 + CHAINS * LEN].rearrange(
                    "(c n) -> c n", n=LEN)).then_inc(lines_in, 16)
                sp.dma_start(to_d[:, LEN:LEN + 2], dst_line[0, P - 1 + LEN:P - 1 + LEN + CHAINS * LEN].rearrange(
                    "(c n) -> c n", n=LEN)[:, 0:2]).then_inc(lines_in, 16)
            sp.wait_ge(lines_exp, 1)
            for h in range(H):
                _, _, _, of_p, to_p = line_views(h)
                sp.dma_start(to_p, of_p).then_inc(probs_out, 16)

        def values_dma(sp):
            for u in range(2):
                sp.wait_ge(A0["spilled"][u], 16 * PAIRS)
            sp.wait_ge(probs_out, 16 * H)

            def body(i):
                for u in range(2):
                    g = 2 * i + u
                    if since(g, 2):
                        sp.wait_ge(A1["weights_ps"], g - 1)
                    sp.dma_start(score_t[:, u, :], p_edges[bass.ds(g, 1)].rearrange("a r e -> (a r) e")).then_inc(A1["probs"][u], 16)
                    if since(g, 2):
                        sp.wait_ge(A1["message"], g - 1)
                    sp.dma_start(edge_in[:, u, :, :].rearrange("p k f -> p (k f)"),
                                 v_edges[bass.ds(g, 1)].rearrange("a p n -> (a p) n")).then_inc(A1["edge"][u], 16)
            loop_pairs(sp, body)

        def gated_dma(sp):
            def body(i):
                for u in range(2):
                    load_edges(sp, B0, edge_attr_32, 2 * i + u, u)
            loop_pairs(sp, body)

        def gathered_rows(u, width):
            return rows[:, u, :, :].rearrange("p k f -> p (k f)")[:, 0:GROUP * width].rearrange("p (k f) -> p k f", k=GROUP)

        def gather(pool, C, table, width, users):
            def body(g, pair, m, first, last):
                u = m % 2
                if not first:
                    for s, n in users:
                        if isinstance(s, list):
                            pool.wait_ge(s[u], n * pair)
                        else:
                            pool.wait_ge(s, n * (g - 1))
                pool.wait_ge(C["index"], g + 1)
                if not last:
                    nc.gpsimd.tensor_copy(index[:, (m + 1) % INDEXES, :], src_idx[:, bass.ds((g + 1) * GROUP, GROUP)]
                                          ).then_inc(C["index"], 1)
                for k in range(GROUP):
                    pool.indirect_dma_start(gathered_rows(u, width)[:, k, :], None, table,
                                            bass.IndirectOffsetOnAxis(index[:, m, k:k + 1], 0)
                                            ).then_inc(C["gathered"][u], 16)

            nc.gpsimd.tensor_copy(index[:, 0, :], src_idx[:, 0:GROUP]).then_inc(C["index"], 1)
            body(0, 0, 0, True, False)
            body(1, 0, 1, True, False)
            with pool.Fori(0, (GROUPS - 2) // INDEXES - 1) as i:
                for v in range(INDEXES):
                    body(INDEXES * i + 2 + v, INDEXES // 2 * i + 1 + v // 2, (2 + v) % INDEXES, False, False)
            for v in range(INDEXES):
                g = GROUPS - INDEXES + v
                body(g, g // 2, g % INDEXES, False, v == INDEXES - 1)

        def landed(i):
            return 16 * GROUP * (i + 1)

        def stage_nodes(act, K, i, first):
            if not first:
                act.wait_ge(K["xt_ps"], i)
            nc.scalar.copy(stage_x, nodes[:, tiles(i), :]).then_inc(K["staged"], 1)

        def stage_sums(act, O, i, first, width):
            if not first:
                act.wait_ge(O["acc_ps"], i)
            nc.scalar.copy(stage_a[0:width, :], acc[0:width, bass.ds(i * CP, CP)])
            nc.scalar.copy(stage_b[0:width, :], acc_odd[0:width, bass.ds(i * CP, CP)]).then_inc(O["staged"], 1)

        def stage_act(act, O, C, width):
            act.wait_ge(C["added"], GROUP * GROUPS)
            loop_chunks(act, lambda i, first: stage_sums(act, O, i, first, width))

        def square_root(act, n):
            act.wait_ge(variance, n)
            nc.scalar.activation(stats[:, 1, :], stats[:, 1, :], ACT.Sqrt).then_inc(root, 1)

        def copy_projections(act, K, parts):
            def body(i, first):
                stage_nodes(act, K, i, first)
                act.wait_ge(K["xt_ps"], i + 1)
                nc.scalar.copy(chunk_t, chunk_x).then_inc(K["xt"], 1)
                act.wait_ge(K["proj_ps"], i + 1)
                if not first:
                    act.wait_ge(K["table"], 16 * parts * i)
                nc.scalar.copy(chunk_p[:, 0:2, :], bank[1][:, 0, 0:6 * D].rearrange("p (t f) -> p t f", t=2)).then_inc(K["proj"], 1)
                nc.scalar.copy(chunk_p[:, 2:4, :], bank[1][:, 1, 0:6 * D].rearrange("p (t f) -> p t f", t=2)).then_inc(K["proj"], 1)
            loop_chunks(act, body)

        def scores_act(act):
            def onehots(g, u):
                act.wait_ge(A0["onehot_ps"], g + 1)
                if since(g, 2):
                    act.wait_ge(A0["expanded"], g - 1)
                nc.scalar.copy(onehot_t[:, u, :, :], bank[u][:].rearrange("p a (k j) -> p (a k) j", j=P)
                               ).then_inc(A0["onehot_t"], 1)

            def scores(g, u, i):
                act.wait_ge(A0["score_ps"], g + 1)
                if since(g, 2):
                    act.wait_ge(A0["stored"][u], 16 * i)
                nc.scalar.mul(score_t[:, u, :], bank[3][0:H * GROUP, u, 0:P], DH ** -0.5).then_inc(A0["score_t"], 1)
                act.wait_ge(A0["score_t"], g + 1)
                act.dma_start(s_edges[bass.ds(g, 1)].rearrange("a r e -> (a r) e"), score_t[:, u, :]
                              ).then_inc(A0["stored"][u], 16)

            def body(i):
                for u in range(2):
                    h, v, _ = group_at(i, u, 1)
                    if is_group(h):
                        onehots(h, v)
                    h, v, j = group_at(i, u, -1)
                    if since(h, 0):
                        scores(h, v, j)
                    act.wait_ge(A0["gathered"][u], landed(i))
                    act.dma_start(v_edges[bass.ds(2 * i + u, 1)].rearrange("a p (k f) -> (a p) k f", k=GROUP),
                                  rows[:, u, :, D:2 * D]).then_inc(A0["spilled"][u], 16)
            onehots(0, 0)
            loop_pairs(act, body)
            scores(*group_at(PAIRS - 1, 1))

        def values_act(act):
            def body(i):
                for u in range(2):
                    g = 2 * i + u
                    act.wait_ge(A1["weights_ps"], g + 1)
                    if since(g, 2):
                        act.wait_ge(A1["reduced"], g - 1)
                    nc.scalar.copy(message[:, u, :, D:A], bank[3][:, u, 0:H * GROUP].rearrange("p (h k) -> p k h", h=H)
                                   ).then_inc(A1["weights"], 1)
            loop_pairs(act, body)

        def mixed_act(act):
            act.wait_ge(A1["added"], GROUP * GROUPS)

            def body(i, first):
                stage_sums(act, O0, i, first, A)
                act.wait_ge(O0["mixed_ps"], i + 1)
                if not first:
                    act.wait_ge(O0["proj_ps"], i)
                nc.scalar.copy(chunk_t, chunk_x).then_inc(O0["mixed_t"], 1)
            loop_chunks(act, body)

        def mlp_act(act):
            act.wait_ge(normed, 1)

            def body(i, first):
                stage_nodes(act, K1, i, first)
                act.wait_ge(K1["xt_ps"], i + 1)
                nc.scalar.copy(chunk_t, chunk_x).then_inc(K1["xt"], 1)
                act.wait_ge(K1["hid_ps"], i + 1)
                if not first:
                    act.wait_ge(K1["leaky"], i)
                nc.scalar.activation(chunk_h, chunk_u, ACT.Identity, bias=b_1n[:, 0:1]).then_inc(K1["hid"], 1)
                act.wait_ge(K1["proj_ps"], i + 1)
                if not first:
                    act.wait_ge(K1["table"], 16 * i)
                nc.scalar.copy(chunk_p[:, :, 0:D], chunk_v).then_inc(K1["proj"], 1)
            loop_chunks(act, body)

        def gated_act(act):
            def features(g, u):
                act.wait_ge(B0["edge_ps"], g + 1)
                if since(g, 2):
                    act.wait_ge(B0["hid_ps"], g - 1)
                nc.scalar.copy(edge_t[:, u, 0:2, :], bank[2][:, 0, 0:2 * P].rearrange("p (m e) -> p m e", m=2)
                               ).then_inc(B0["edge_t"], 1)

            def hidden(g, u):
                act.wait_ge(B0["hid_ps"], g + 1)
                if since(g, 2):
                    act.wait_ge(B0["edge_mm"], g - 1)
                hid = bank[1][:].rearrange("p a (k e) -> p (a k) e", e=P)
                nc.scalar.activation(hidden_t[0:D, u, :, :], hid[0:D], ACT.Identity, bias=b_1e[0:D, 0:1]
                                     ).then_inc(B0["hid"], 1)
                nc.scalar.activation(hidden_t[D:P, u, :, :], hid[D:P], ACT.Relu, bias=b_1e[D:P, 0:1]
                                     ).then_inc(B0["hid"], 1)

            def body(i):
                for u in range(2):
                    h, v, _ = group_at(i, u, 1)
                    if is_group(h):
                        features(h, v)
                        hidden(h, v)
            features(0, 0)
            hidden(0, 0)
            loop_pairs(act, body)

        def attend_act(act):
            def body(i):
                for u in range(2):
                    g = 2 * i + u
                    act.wait_ge(C0["onehot_ps"], g + 1)
                    if since(g, 2):
                        act.wait_ge(C0["expanded"], g - 1)
                        act.wait_ge(C0["edge_mm"], g - 1)
                    nc.scalar.copy(onehot_t[:, u, :, :], bank[1][:].rearrange("p a (k j) -> p (a k) j", j=P)
                                   ).then_inc(C0["onehot_t"], 1)
                    act.wait_ge(C0["edge_ps"], g + 1)
                    nc.scalar.copy(edge_t[:, u, :, :], bank[3][:, 0, :].rearrange("p (m e) -> p m e", m=4)
                                   ).then_inc(C0["edge_t"], 1)
                    act.wait_ge(C0["chain"], CHAIN2 * (g + 1))
                    if since(g, 2):
                        act.wait_ge(C0["reduced"], g - 1)
                    nc.scalar.activation(message[:, u, :, D:A], score[:, u, :].rearrange("p (k h) -> p k h", h=H),
                                         ACT.Exp, scale=DH ** -0.5).then_inc(C0["weights"], 1)
            loop_pairs(act, body)

        def gin_act(act):
            act.wait_ge(G0["added"], GROUP * GROUPS)

            def body(i, first):
                stage_nodes(act, M3, i, first)
                act.wait_ge(M3["hid_ps"], i + 1)
                nc.scalar.activation(chunk_h, chunk_u, ACT.Relu, bias=b_g1[:, 0:1]).then_inc(M3["hid"], 1)
                act.wait_ge(M3["proj_ps"], i + 1)
                nc.scalar.copy(mix[:, tiles(i), :], chunk_v).then_inc(M3["proj"], 1)
            loop_chunks(act, body)

        def turned(to, of, eye):
            return nc.tensor.matmul(to, of, eye, start=True, stop=True)

        def turn_nodes(pe, i, K):
            pe.wait_ge(K["staged"], i + 1)
            for t in range(CHUNK):
                last = turned(chunk_x[:, t * P:(t + 1) * P],
                                           stage_x[:, t, :], ident[:])
            last.then_inc(K["xt_ps"], 1)

        def project(pe, K, w):
            def body(i, first):
                if not first:
                    pe.wait_ge(K["xt"], i)
                turn_nodes(pe, i, K)
                pe.wait_ge(K["xt"], i + 1)
                if not first:
                    pe.wait_ge(K["proj"], 2 * i)
                for t in range(CHUNK):
                    last = nc.tensor.matmul(chunk_w(t), chunk_t[:, t * P:(t + 1) * P], w[:], start=True, stop=True)
                last.then_inc(K["proj_ps"], 1)
            loop_chunks(pe, body)

        def expand(C, u, to):
            for k in range(GROUP):
                last = nc.tensor.matmul(to[:, k * D:(k + 1) * D], onehot_t[:, u, k, :], window[:, u, k, :],
                                        start=True, stop=True)
            last.then_inc(C["expanded"], 1)

        def turn_onehots(C, u, to):
            for k in range(GROUP):
                last = nc.tensor.transpose(to[:, k // 4, k % 4 * P:(k % 4 + 1) * P], onehot[:, u, k, :], ident[:])
            last.then_inc(C["onehot_ps"], 1)

        def reduce(C, u, to, width, of):
            for k in range(GROUP):
                last = nc.tensor.matmul(to[0:width, k // 4, k % 4 * P:(k % 4 + 1) * P], of(k), onehot[:, u, k, :],
                                        start=True, stop=True)
            last.then_inc(C["reduced"], 1)

        def scores_pe(pe):
            pe.wait_ge(K0["proj"], 2 * CHUNKS)

            def turn(g, u):
                pe.wait_ge(A0["onehot"], g + 1)
                if since(g, 2):
                    pe.wait_ge(A0["onehot_t"], g - 1)
                turn_onehots(A0, u, bank[u])

            def turn_scores(g, u):
                pe.wait_ge(A0["score"], g + 1)
                if since(g, 2):
                    pe.wait_ge(A0["score_t"], g - 1)
                turned(bank[3][0:H * GROUP, u, 0:P], score[:, u, :], ident[:]).then_inc(A0["score_ps"], 1)

            def body(i):
                for u in range(2):
                    g = 2 * i + u
                    if is_group(g + 1):
                        turn(g + 1, 1 - u)
                    if since(g, 1):
                        turn_scores(g - 1, 1 - u)
                    pe.wait_ge(A0["onehot_t"], g + 1)
                    pe.wait_ge(A0["window"][u], landed(i))
                    if since(g, 2):
                        pe.wait_ge(A0["product"], g - 1)
                    expand(A0, u, bank[2][:, u, :])
            turn(0, 0)
            loop_pairs(pe, body)
            turn_scores(LAST, 1)

        def chains_pe(pe):
            for n in range(2):
                pe.wait_ge(chains_dve, 2 * n + 1)
                for m in range(2):
                    last = nc.tensor.transpose(banks(0)[0:1, m * P:m * P + SP_], chain_cols[0:SP_, 4 * n + m:4 * n + m + 1],
                                               ident[0:SP_, 0:SP_])
                last.then_inc(chains_ps, 1)
                pe.wait_ge(chains_dve, 2 * n + 2)
                nc.tensor.transpose(banks(1)[0:SP_, 0:1], chain_rows[0:1, 2, n:n + SP_],
                                    ident[0:1, 0:1]).then_inc(chains_ps, 1)

        def values_pe(pe):
            def turn_weights(g, u, i):
                pe.wait_ge(A1["probs"][u], 16 * (i + 1))
                if since(g, 2):
                    pe.wait_ge(A1["weights"], g - 1)
                turned(bank[3][:, u, 0:H * GROUP], score_t[:, u, :], ident[0:H * GROUP, 0:H * GROUP]
                       ).then_inc(A1["weights_ps"], 1)

            def body(i):
                for u in range(2):
                    g = 2 * i + u
                    h, v, j = group_at(i, u, 1)
                    if is_group(h):
                        turn_weights(h, v, j)
                    pe.wait_ge(A1["message"], g + 1)
                    pe.wait_ge(A1["onehot"], g + 1)
                    if since(g, 2):
                        pe.wait_ge(A1["added"], GROUP * (g - 1))
                    reduce(A1, u, bank[u], A, message_of(u, A))
            turn_weights(0, 0, 0)
            loop_pairs(pe, body)

        def turn_sums(pe, O, C, width):
            def body(i, first):
                if not first:
                    pe.wait_ge(O["mixed"] if O is O2 else O["added"], i)
                turn_chunk_sums(pe, i, O, width)
            loop_chunks(pe, body)

        def turn_chunk_sums(pe, i, O, width):
            pe.wait_ge(O["staged"], i + 1)
            for t in range(CHUNK):
                nc.tensor.matmul(chunk_a[:, t, 0:width], stage_a[0:width, t * P:(t + 1) * P], ident[0:width, 0:width],
                                 start=True, stop=False)
                last = nc.tensor.matmul(chunk_a[:, t, 0:width], stage_b[0:width, t * P:(t + 1) * P], ident[0:width, 0:width],
                                        start=False, stop=True)
            last.then_inc(O["acc_ps"], 1)

        def mix_out_pe(pe):
            def body(i, first):
                if not first:
                    pe.wait_ge(O0["mixed"], i)
                turn_chunk_sums(pe, i, O0, A)
                pe.wait_ge(O0["mixed"], i + 1)
                if not first:
                    pe.wait_ge(O0["mixed_t"], i)
                for t in range(CHUNK):
                    last = turned(chunk_x[:, t * P:(t + 1) * P], chunk_m[:, t, :], ident[:])
                last.then_inc(O0["mixed_ps"], 1)
                pe.wait_ge(O0["mixed_t"], i + 1)
                if not first:
                    pe.wait_ge(O0["added"], i)
                for t in range(CHUNK):
                    last = nc.tensor.matmul(chunk_v[:, t, :], chunk_t[:, t * P:(t + 1) * P], w_o[:], start=True, stop=True)
                last.then_inc(O0["proj_ps"], 1)
            loop_chunks(pe, body)

        def mlp_pe(pe):
            pe.wait_ge(normed, 1)

            def body(i, first):
                if not first:
                    pe.wait_ge(K1["xt"], i)
                turn_nodes(pe, i, K1)
                pe.wait_ge(K1["xt"], i + 1)
                if not first:
                    pe.wait_ge(K1["hid"], i)
                nc.tensor.matmul(chunk_u, w_1n[:], chunk_t, start=True, stop=True).then_inc(K1["hid_ps"], 1)
                pe.wait_ge(K1["leaky"], i + 1)
                if not first:
                    pe.wait_ge(K1["proj"], i)
                for t in range(CHUNK):
                    nc.tensor.matmul(chunk_v[:, t, :], chunk_l[:, t * P:(t + 1) * P], w_2n[:], start=True, stop=False)
                    last = nc.tensor.matmul(chunk_v[:, t, :], ones[:], b_2n[:], start=False, stop=True)
                last.then_inc(K1["proj_ps"], 1)
            loop_chunks(pe, body)

        def gated_pe(pe):
            pe.wait_ge(w_scaled, 2)
            pe.wait_ge(K1["proj"], CHUNKS)

            def turn_features(g, u, i):
                pe.wait_ge(B0["edge"][u], edge_landed(g, i))
                if since(g, 1):
                    pe.wait_ge(B0["edge_t"], g)
                flat = edge_in[:, u, :, :].rearrange("p k f -> p (k f)")
                for m in range(2):
                    last = nc.tensor.transpose(bank[2][:, 0, m * P:(m + 1) * P], flat[:, m * P:(m + 1) * P], ident[:])
                last.then_inc(B0["edge_ps"], 1)

            def hidden(g, u):
                pe.wait_ge(B0["edge_t"], g + 1)
                if since(g, 1):
                    pe.wait_ge(B0["hid"], 2 * g)
                for k in range(GROUP):
                    last = nc.tensor.matmul(bank[1][:, k // 4, k % 4 * P:(k % 4 + 1) * P], w_1e[:, k % (P // DE), :],
                                            edge_t[:, u, k * DE // P, :], start=True, stop=True)
                last.then_inc(B0["hid_ps"], 1)

            def second(g, u):
                pe.wait_ge(B0["hid"], 2 * (g + 1))
                if since(g, 1):
                    pe.wait_ge(B0["message"], g)
                for k in range(GROUP):
                    to = bank[2][:, 1, k * D:(k + 1) * D]
                    nc.tensor.matmul(to, hidden_t[:, u, k, :], w_2e[:], start=True, stop=False)
                    last = nc.tensor.matmul(to, ones[:], b_2e[:], start=False, stop=True)
                last.then_inc(B0["edge_mm"], 1)

            def sums(g, u):
                pe.wait_ge(B0["message"], g + 1)
                pe.wait_ge(B0["onehot"], g + 1)
                if since(g, 2):
                    pe.wait_ge(B0["added"], GROUP * (g - 1))
                reduce(B0, u, bank[3 * u], D, message_of(u, D))

            def body(i):
                for u in range(2):
                    g = 2 * i + u
                    h, v, j = group_at(i, u, 1)
                    if is_group(h):
                        turn_features(h, v, j)
                    second(g, u)
                    if is_group(h):
                        hidden(h, v)
                    if since(g, 1):
                        sums(g - 1, 1 - u)
            turn_features(0, 0, 0)
            hidden(0, 0)
            loop_pairs(pe, body)
            sums(LAST, 1)

        def message_of(u, width):
            return lambda k: message[:, u, k, 0:width]

        def attend_pe(pe):
            pe.wait_ge(K2["proj"], 2 * CHUNKS)

            def sums(g, u):
                pe.wait_ge(C0["message"], g + 1)
                if since(g, 1):
                    pe.wait_ge(C0["added"], GROUP * g)
                reduce(C0, u, bank[0], A, message_of(u, A))

            def body(i):
                for u in range(2):
                    g = 2 * i + u
                    pe.wait_ge(C0["onehot"], g + 1)
                    if since(g, 1):
                        pe.wait_ge(C0["onehot_t"], g)
                    turn_onehots(C0, u, bank[1])
                    pe.wait_ge(C0["edge"][u], edge_landed(g, i))
                    if since(g, 1):
                        pe.wait_ge(C0["edge_t"], g)
                    for m in range(4):
                        last = nc.tensor.transpose(bank[3][:, 0, m * P:(m + 1) * P],
                                                   edge_in[:, u, 2 * m:2 * m + 2, :].rearrange("p k f -> p (k f)"), ident[:])
                    last.then_inc(C0["edge_ps"], 1)
                    pe.wait_ge(C0["onehot_t"], g + 1)
                    pe.wait_ge(C0["window"][u], landed(i))
                    if since(g, 1):
                        pe.wait_ge(C0["chain"], CHAIN2 * (g - 1) + 2)
                    expand(C0, u, bank[2][:, 0, :])
                    pe.wait_ge(C0["edge_t"], g + 1)
                    for m in range(GROUP // 2):
                        last = nc.tensor.matmul(bank[2][:, 1, m * 2 * D:(m + 1) * 2 * D], edge_t[:, u, m, :], w_e[:],
                                                start=True, stop=True)
                    last.then_inc(C0["edge_mm"], 1)
                    if since(g, 1):
                        sums(g - 1, 1 - u)
            loop_pairs(pe, body)
            sums(LAST, 1)

        def gin_pe(pe, G):
            def body(i):
                for u in range(2):
                    g = 2 * i + u
                    pe.wait_ge(G["onehot"], g + 1)
                    pe.wait_ge(G["gathered"][u], landed(i))
                    if since(g, 2):
                        pe.wait_ge(G["added"], GROUP * (g - 1))
                    reduce(G, u, bank[u], D, lambda k: gathered_rows(u, D)[:, k, :])
            loop_pairs(pe, body)

        def gin_mid_pe(pe):
            def body(i, first):
                if not first:
                    pe.wait_ge(M3["sum"], i)
                turn_nodes(pe, i, M3)
                pe.wait_ge(M3["sum"], i + 1)
                if not first:
                    pe.wait_ge(M3["hid"], i)
                nc.tensor.matmul(chunk_u, w_g1[:], chunk_t, start=True, stop=True).then_inc(M3["hid_ps"], 1)
                pe.wait_ge(M3["hid"], i + 1)
                if not first:
                    pe.wait_ge(M3["proj"], i)
                for t in range(CHUNK):
                    last = nc.tensor.matmul(chunk_v[:, t, :], chunk_h[:, t * P:(t + 1) * P], w_g2[:], start=True, stop=True)
                last.then_inc(M3["proj_ps"], 1)
            loop_chunks(pe, body)

        def clear_sums():
            nc.vector.memset(acc[:], 0.0)
            nc.vector.memset(acc_odd, 0.0).then_inc(zeroed, 1)

        roots = [0]

        def layer_norm(dve, v, link, signal):
            mean, var = stats[:, 0, :], stats[:, 1, :]
            link(nc.vector.tensor_reduce(mean, v, AX, ALU.add))
            link(nc.vector.tensor_scalar_mul(mean, mean, 1.0 / D))
            link(nc.vector.tensor_tensor(v, v, mean.unsqueeze(2).to_broadcast([P, NODE_TILES, D]), ALU.subtract))
            link(nc.vector.tensor_tensor(squares, v, v, ALU.mult))
            link(nc.vector.tensor_reduce(var, squares, AX, ALU.add))
            nc.vector.tensor_scalar(var, var, 1.0 / D, EPS, ALU.mult, ALU.add).then_inc(variance, 1)
            roots[0] += 1
            dve.wait_ge(root, roots[0])
            link(nc.vector.reciprocal(var, var))
            last = nc.vector.tensor_tensor(v, v, var.unsqueeze(2).to_broadcast([P, NODE_TILES, D]), ALU.mult)
            if signal:
                last.then_inc(normed, 1)
            else:
                link(last)

        def quotients(dve, O, i, first, to, eps):
            if not first:
                dve.wait_ge(O["mixed_ps"] if O is O0 else O["mixed"], i)
            nc.vector.tensor_scalar_add(chunk_d, chunk_a[:, :, D:A], eps).then_inc(O["den"], 1)
            dve.wait_ge(O["den"], 2 * i + 1)
            nc.vector.reciprocal(chunk_d, chunk_d).then_inc(O["den"], 1)
            dve.wait_ge(O["den"], 2 * i + 2)
            nc.vector.tensor_tensor(heads(to), heads(chunk_a[:, :, 0:D]), chunk_d.unsqueeze(3).to_broadcast([P, CHUNK, H, DH]),
                                    ALU.mult).then_inc(O["mixed"], 1)

        def one_hots(C, g, u):
            nc.vector.tensor_tensor(onehot[:, u, :, :], iota[:].unsqueeze(1).to_broadcast([P, GROUP, P]),
                                    dst_rel[:, bass.ds(g * GROUP, GROUP)].unsqueeze(2).to_broadcast([P, GROUP, P]),
                                    ALU.is_equal).then_inc(C["onehot"], 1)

        def add_sums(dve, C, g, ps, width, regs):
            dve.wait_ge(C["reduced"], g + 1)
            dve.load(regs, starts[0:1, bass.ds(g * GROUP, GROUP)])
            for k in range(GROUP):
                at = dve.snap(regs[k], min_val=0, max_val=N - 1)
                if not isinstance(g, int) or g * GROUP + k >= 2:
                    dve.wait_ge(C["added"], g * GROUP + k - 1)
                to = (acc if k % 2 == 0 else acc_odd)[0:width, bass.ds(at, P)]
                nc.vector.tensor_tensor(to, to, ps[0:width, k // 4, k % 4 * P:(k % 4 + 1) * P], ALU.add).then_inc(C["added"], 1)

        def weighted(u, values):
            return nc.vector.tensor_tensor(heads(message[:, u, :, 0:D]), heads(values),
                                           message[:, u, :, D:A].unsqueeze(3).to_broadcast([P, GROUP, H, DH]), ALU.mult)

        def scores_dve(dve):
            def onehots(g, u):
                if since(g, 2):
                    dve.wait_ge(A0["onehot_ps"], g - 1)
                one_hots(A0, g, u)

            def body(i):
                for u in range(2):
                    g = 2 * i + u
                    if is_group(g + 2):
                        onehots(g + 2, u)
                    dve.wait_ge(A0["expanded"], g + 1)
                    dve.wait_ge(A0["gathered"][u], landed(i))
                    if since(g, 2):
                        dve.wait_ge(A0["score"], g - 1)
                    nc.vector.tensor_tensor(product[:, u, :, :], rows[:, u, :, 0:D],
                                            bank[2][:, u, :].rearrange("p (k f) -> p k f", k=GROUP), ALU.mult
                                            ).then_inc(A0["product"], 1)
                    dve.wait_ge(A0["product"], g + 1)
                    if since(g, 2):
                        dve.wait_ge(A0["score_ps"], g - 1)
                    nc.vector.tensor_reduce(score[:, u, :].rearrange("p (h k) -> p k h", h=H),
                                            heads(product[:, u, :, :]), AX, ALU.add).then_inc(A0["score"], 1)
            onehots(0, 0)
            onehots(1, 1)
            loop_pairs(dve, body)

        def maxima_dve(dve, link):
            dve.wait_ge(lines_in, 16 * 3 * H)
            cuts = line_r
            flat = line_d[:, 0:LEN]
            cols = chain_cols[0:SP_, :]
            single = cols[:, 7:8]
            n = 0
            link(nc.vector.tensor_tensor(single, line_d[:, 1:2], line_d[:, LEN:LEN + 1], ALU.not_equal))
            link(nc.vector.tensor_scalar_mul(single, single, -BIG))
            link(nc.vector.tensor_tensor(cuts[:, 0:LEN + 1], line_d[:, 1:LEN + 2], line_d[:, 0:LEN + 1], ALU.not_equal))
            link(nc.vector.tensor_scalar_mul(cuts[:, 0:LEN + 1], cuts[:, 0:LEN + 1], -BIG))
            ways = [(line_s, cuts[:, 0:LEN], slice(None), cuts[:, 0:1], flat[:, LEN - 1:LEN]),
                    (flat, cuts[:, 1:LEN + 1], slice(None, None, -1), cuts[:, LEN:LEN + 1], flat[:, 0:1])]
            for n, (of, cut, way, edge, last) in enumerate(ways):
                link(nc.vector.tensor_tensor_scan(flat[:, way], cut[:, way], of[:, way], -BIG, ALU.add, ALU.max))
                link(nc.vector.tensor_copy(cols[:, 4 * n:4 * n + 1], last))
                nc.vector.tensor_tensor(cols[:, 4 * n + 1:4 * n + 2], edge, single, ALU.add).then_inc(chains_dve, 1)
                dve.wait_ge(chains_ps, 2 * n + 1)
                link(nc.vector.tensor_copy(chain_rows[0:1, 0:2, 0:SP_],
                                           banks(0)[0:1, 0:2 * P].rearrange("p (m s) -> p m s", m=2)[:, :, 0:SP_]))
                link(nc.vector.memset(chain_rows[0:1, 2, :], -BIG))
                carry = chain_rows[0:1, 2, 1 - n:1 - n + SP_]
                nc.vector.tensor_tensor_scan(carry[:, way], chain_rows[0:1, 1, 0:SP_][:, way],
                                             chain_rows[0:1, 0, 0:SP_][:, way], -BIG, ALU.add, ALU.max
                                             ).then_inc(chains_dve, 1)
                dve.wait_ge(chains_ps, 2 * n + 2)
                link(nc.vector.tensor_copy(cols[:, 4 * n + 2:4 * n + 3], banks(1)[0:SP_, 0:1]))
                link(nc.vector.tensor_tensor_scan(flat[:, way], cut[:, way], flat[:, way],
                                                  cols[:, 4 * n + 2:4 * n + 3], ALU.add, ALU.max))
            nc.vector.scalar_tensor_tensor(flat, flat, -1.0e9, line_s, ALU.max, ALU.subtract).then_inc(lines_less, 1)

        def values_dve(dve, regs):
            dve.wait_ge(zeroed, 1)

            def body(i):
                for u in range(2):
                    g = 2 * i + u
                    if since(g, 2):
                        dve.wait_ge(A1["reduced"], g - 1)
                    one_hots(A1, g, u)
                    dve.wait_ge(A1["weights"], g + 1)
                    dve.wait_ge(A1["edge"][u], 16 * (i + 1))
                    weighted(u, edge_in[:, u, :, :]).then_inc(A1["message"], 1)
                    if since(g, 1):
                        add_sums(dve, A1, g - 1, bank[1 - u], A, regs)
            loop_pairs(dve, body)
            add_sums(dve, A1, LAST, bank[1], A, regs)

        def gated_dve(dve, regs):
            dve.wait_ge(zeroed, 2)

            def body(i):
                for u in range(2):
                    g = 2 * i + u
                    if since(g, 2):
                        dve.wait_ge(B0["reduced"], g - 1)
                    one_hots(B0, g, u)
                    dve.wait_ge(B0["edge_mm"], g + 1)
                    dve.wait_ge(B0["gathered"][u], landed(i))
                    nc.vector.tensor_tensor(message[:, u, :, 0:D], gathered_rows(u, D),
                                            bank[2][:, 1, :].rearrange("p (k f) -> p k f", k=GROUP), ALU.mult
                                            ).then_inc(B0["message"], 1)
                    if since(g, 2):
                        add_sums(dve, B0, g - 2, bank[3 * u], D, regs)
            loop_pairs(dve, body, 2)
            add_sums(dve, B0, LAST - 1, bank[0], D, regs)
            add_sums(dve, B0, LAST, bank[3], D, regs)

        def attend_dve(dve, regs):
            dve.wait_ge(zeroed, 3)

            def body(i):
                for u in range(2):
                    g = 2 * i + u
                    dve.wait_ge(C0["expanded"], g + 1)
                    dve.wait_ge(C0["gathered"][u], landed(i))
                    qd = bank[2][:, 0, :].rearrange("p (k f) -> p k f", k=GROUP)
                    ee = bank[2][:, 1, :].rearrange("p (k f) -> p k f", k=GROUP)
                    nc.vector.tensor_tensor(product[:, u, :, :], rows[:, u, :, 0:D], qd, ALU.mult).then_inc(C0["chain"], 1)
                    dve.wait_ge(C0["chain"], CHAIN2 * g + 1)
                    dve.wait_ge(C0["edge_mm"], g + 1)
                    nc.vector.tensor_tensor(product[:, u, :, :], product[:, u, :, :], ee, ALU.mult).then_inc(C0["chain"], 1)
                    dve.wait_ge(C0["chain"], CHAIN2 * g + 2)
                    if since(g, 2):
                        dve.wait_ge(C0["weights"], g - 1)
                    nc.vector.tensor_reduce(score[:, u, :].rearrange("p (k h) -> p k h", h=H),
                                            heads(product[:, u, :, :]), AX, ALU.add).then_inc(C0["chain"], 1)
                    dve.wait_ge(C0["chain"], CHAIN2 * g + 3)
                    nc.vector.tensor_scalar(score[:, u, :], score[:, u, :], 5.0 * DH ** 0.5, -5.0 * DH ** 0.5,
                                            ALU.min, ALU.max).then_inc(C0["chain"], 1)
                    if is_group(g + 1):
                        if since(g, 1):
                            dve.wait_ge(C0["reduced"], g)
                        one_hots(C0, g + 1, 1 - u)
                    dve.wait_ge(C0["weights"], g + 1)
                    weighted(u, rows[:, u, :, D:2 * D]).then_inc(C0["message"], 1)
                    if since(g, 1):
                        add_sums(dve, C0, g - 1, bank[0], A, regs)
            one_hots(C0, 0, 0)
            loop_pairs(dve, body)
            add_sums(dve, C0, LAST, bank[0], A, regs)

        def gin_dve(dve, G, regs):
            dve.wait_ge(zeroed, 4 if G is G0 else 5)

            def body(i):
                for u in range(2):
                    g = 2 * i + u
                    if since(g, 2):
                        dve.wait_ge(G["reduced"], g - 1)
                    one_hots(G, g, u)
                    if since(g, 1):
                        add_sums(dve, G, g - 1, bank[1 - u], D, regs)
            loop_pairs(dve, body)
            add_sums(dve, G, LAST, bank[1], D, regs)

        @block.sync
        def _(sp):
            sp.wait_ge(filled, 1)
            for nat, v in ((nat_src, src), (nat_dst, dst)):
                for where, part in blocks_of(v):
                    sp.dma_start(nat[where], part).then_inc(graph_in, 16)
            with sp.Fori(0, NFULL // CHUNK) as i:
                sp.dma_start(nodes[:, tiles(i), :], x[bass.ds(i * CP, CP), :].rearrange("(t p) d -> p t d", p=P)
                             ).then_inc(nodes_in, 16)
            sp.dma_start(nodes[0:NREM, NFULL, :], x[NFULL * P:N, :]).then_inc(nodes_in, 16)
            for to, v in weight_loads:
                sp.dma_start(to, v).then_inc(weights_in, 16)
            sp.wait_ge(graph_cast, 2)
            sp.dma_start(dst_line[0:1, 0:P], minus).then_inc(lines_out, 16)
            sp.dma_start(dst_line[0:1, P:P + NAT * P * P].rearrange("a (c p e) -> (a p) c e", p=P, e=P), flt_dst).then_inc(lines_out, 16)
            sp.dma_start(start_line.rearrange("c p -> p c"), start_i, allow_slow_non_contiguous=True).then_inc(lines_out, 16)
            for g in range(GROUPS, SG):
                sp.dma_start(s_edges[g], blank).then_inc(lines_out, 16)
            sp.wait_ge(lines_out, LINES_OUT)
            sp.dma_start(starts[:], start_line.rearrange("c p -> (c p)").rearrange("(a n) -> a n", a=1)).then_inc(starts_in, 16)

            store_tables(sp, K0, 2)
            sp.wait_ge(starts_in, 16)
            score_regs = [sp.alloc_register(f"sp_start{k}") for k in range(GROUP)]
            load_windows(sp, A0, score_regs, None)
            probabilities_dma(sp)
            values_dma(sp)
            store_tables(sp, K1, 1)
            gated_dma(sp)
            store_tables(sp, K2, 2)
            load_windows(sp, C0, score_regs, edge_attr_64)
            sp.wait_ge(normed, 3)
            sp.dma_start(x3_table.rearrange("(t p) d -> p t d", p=P), nodes[:]).then_inc(stored, 16)
            sp.wait_ge(M3["proj"], CHUNKS)
            sp.dma_start(y3_table.rearrange("(t p) d -> p t d", p=P), mix).then_inc(stored, 16)
            sp.wait_ge(normed, 4)
            sp.dma_start(out[0:NFULL * P, :].rearrange("(t p) d -> p t d", p=P), nodes[:, 0:NFULL, :]).then_inc(stored, 16)
            sp.dma_start(out[NFULL * P:N, :], nodes[0:NREM, NFULL, :]).then_inc(stored, 16)
            sp.wait_ge(stored, 64)

        @block.gpsimd
        def _(pool):
            nc.gpsimd.memset(ones[:], 1.0).then_inc(consts, 1)
            nc.gpsimd.memset(ident[:], 0.0).then_inc(consts, 1)
            nc.gpsimd.iota(iota[:], pattern=[[1, P]], base=0, channel_multiplier=0,
                           allow_small_or_imprecise_dtypes=True).then_inc(consts, 1)
            pool.wait_ge(consts, 3)
            nc.gpsimd.affine_select(out=ident[:], in_=ident[:], compare_op=ALU.not_equal, fill=1.0, base=0,
                                    pattern=[[-1, P]], channel_multiplier=1).then_inc(consts, 1)
            pool.wait_ge(graph_out, 2)
            pool.wait_ge(K0["table"], 32 * CHUNKS)
            gather(pool, A0, kv_table, 2 * D, [(A0["product"], 1), (A0["spilled"], 16)])
            pool.wait_ge(K1["table"], 16 * CHUNKS)
            gather(pool, B0, xt_table, D, [(B0["message"], 1)])
            pool.wait_ge(K2["table"], 32 * CHUNKS)
            gather(pool, C0, kv_table, 2 * D, [(C0["message"], 1)])
            pool.wait_ge(stored, 16)
            gather(pool, G0, x3_table, D, [(G0["reduced"], 1)])
            pool.wait_ge(stored, 32)
            gather(pool, G1, y3_table, D, [(G1["reduced"], 1)])

        @block.scalar
        def _(act):
            act.wait_ge(graph_ps, 1)
            for b in range(2):
                n = min(NATW - b * 1024, 1024)
                last = nc.scalar.copy(dst_rel[:, b * 1024:b * 1024 + n],
                                      bank[b][:].rearrange("p a b -> p (a b)")[:, 0:n])
            last.then_inc(graph_out, 1)
            for b in range(2):
                n = min(NATW - b * 1024, 1024)
                last = nc.scalar.copy(src_idx[:, b * 1024:b * 1024 + n],
                                      bank[2 + b][:].rearrange("p a b -> p (a b)")[:, 0:n])
            last.then_inc(graph_out, 1)
            act.wait_ge(weights_ps, 1)
            nc.scalar.copy(w_2[:], banks(0)[0:D, 0:3 * D]).then_inc(weights_t, 1)
            nc.scalar.copy(w_e[0:D, 0:D], banks(0)[0:D, 3 * D:4 * D]).then_inc(weights_t, 1)
            nc.scalar.copy(w_e[D:P, D:2 * D], banks(0)[0:D, 3 * D:4 * D]).then_inc(weights_t, 1)
            act.wait_ge(nodes_in, NODES_IN)
            act.wait_ge(lines_out, LINES_OUT)
            copy_projections(act, K0, 2)
            scores_act(act)
            act.wait_ge(lines_less, 1)
            nc.scalar.activation(line_r[:, 0:LEN], line_d[:, 0:LEN], ACT.Exp, scale=-1.0).then_inc(lines_exp, 1)
            values_act(act)
            mixed_act(act)
            square_root(act, 1)
            mlp_act(act)
            gated_act(act)
            stage_act(act, O1, B0, D)
            square_root(act, 2)
            square_root(act, 3)
            act.wait_ge(normed, 2)
            copy_projections(act, K2, 2)
            attend_act(act)
            stage_act(act, O2, C0, A)
            square_root(act, 4)
            gin_act(act)
            stage_act(act, O3, G1, D)
            square_root(act, 5)

        @block.tensor
        def _(pe):
            pe.wait_ge(consts, 4)
            pe.wait_ge(graph_cast, 3)
            for c in range(NAT):
                nc.tensor.transpose(bank[c // 8][:, c // 4 % 2, c % 4 * P:(c % 4 + 1) * P], flt_rel[:, c, :], ident[:])
                last = nc.tensor.transpose(bank[2 + c // 8][:, c // 4 % 2, c % 4 * P:(c % 4 + 1) * P], flt_src[:, c, :], ident[:])
            last.then_inc(graph_ps, 1)
            pe.wait_ge(weights_in, WEIGHTS_IN)
            pe.wait_ge(graph_out, 2)
            for n in range(4):
                last = nc.tensor.transpose(banks(0)[0:D, n * D:(n + 1) * D], w_nat[:, n * D:(n + 1) * D], ident[0:D, 0:D])
            last.then_inc(weights_ps, 1)
            pe.wait_ge(weights_t, 3)
            project(pe, K0, w_qkv)
            scores_pe(pe)
            chains_pe(pe)
            values_pe(pe)
            mix_out_pe(pe)
            mlp_pe(pe)
            gated_pe(pe)
            turn_sums(pe, O1, B0, D)
            pe.wait_ge(normed, 2)
            project(pe, K2, w_2)
            attend_pe(pe)
            turn_sums(pe, O2, C0, A)
            gin_pe(pe, G0)
            gin_mid_pe(pe)
            gin_pe(pe, G1)
            turn_sums(pe, O3, G1, D)

        @block.vector
        def _(dve):
            steps = [0]

            def link(ins):
                steps[0] += 1
                ins.then_inc(norm, 1)
                dve.wait_ge(norm, steps[0])

            regs = [dve.alloc_register(f"dve_start{k}") for k in range(GROUP)]
            nc.vector.memset(nat_src, 0)
            nc.vector.memset(nat_dst, 4 * NPAD)
            nc.vector.memset(nodes[:], 0.0)
            nc.vector.memset(minus, -1.0)
            nc.vector.memset(w_1e[:], 0.0)
            nc.vector.memset(w_e[:], 0.0)
            nc.vector.memset(blank, 0.0).then_inc(filled, 1)
            dve.wait_ge(graph_in, GRAPH_IN)
            link(nc.vector.tensor_copy(flt_dst, nat_dst))
            link(nc.vector.tensor_scalar_min(start_f, flt_dst[:, :, 0], float(N - 1)))
            nc.vector.tensor_copy(start_i, start_f).then_inc(graph_cast, 1)
            nc.vector.tensor_copy(flt_src, nat_src).then_inc(graph_cast, 1)
            nc.vector.tensor_tensor(flt_rel, flt_dst, start_f.unsqueeze(2).to_broadcast([P, NAT, P]),
                                    ALU.subtract).then_inc(graph_cast, 1)
            dve.wait_ge(weights_in, WEIGHTS_IN)
            nc.vector.tensor_tensor(gain[:], gains[:, 0:1], gains[:, 1:2], ALU.mult).then_inc(w_scaled, 1)
            nc.vector.tensor_scalar_mul(w_2e[0:D, :], w_2e[0:D, :], SLOPE)
            nc.vector.tensor_scalar_mul(w_2e[D:P, :], w_2e[D:P, :], 1.0 - SLOPE).then_inc(w_scaled, 1)
            dve.wait_ge(graph_out, 2)
            dve.wait_ge(consts, 4)

            scores_dve(dve)
            maxima_dve(dve, link)
            dve.wait_ge(probs_out, 16 * H)
            clear_sums()
            values_dve(dve, regs)

            def mixed(i, first):
                dve.wait_ge(O0["acc_ps"], i + 1)
                quotients(dve, O0, i, first, chunk_m, 1e-9)
                dve.wait_ge(O0["proj_ps"], i + 1)
                nc.vector.tensor_tensor(nodes[:, tiles(i), :], nodes[:, tiles(i), :], chunk_v, ALU.add).then_inc(O0["added"], 1)
            loop_chunks(dve, mixed)
            dve.wait_ge(O0["added"], CHUNKS)
            clear_sums()
            layer_norm(dve, nodes[:], link, True)

            def leaky(i, first):
                dve.wait_ge(K1["hid"], i + 1)
                if not first:
                    dve.wait_ge(K1["proj_ps"], i)
                nc.vector.scalar_tensor_tensor(chunk_l, chunk_h, SLOPE, chunk_h, ALU.mult, ALU.max).then_inc(K1["leaky"], 1)
            loop_chunks(dve, leaky)
            gated_dve(dve, regs)

            def gated_out(i, first):
                dve.wait_ge(O1["acc_ps"], i + 1)
                nc.vector.scalar_tensor_tensor(mix[:, tiles(i), :], chunk_a[:, :, 0:D], gain[:, 0:1],
                                               nodes[:, tiles(i), :], ALU.mult, ALU.add).then_inc(O1["added"], 1)
            loop_chunks(dve, gated_out)
            dve.wait_ge(O1["added"], CHUNKS)
            clear_sums()
            layer_norm(dve, mix, link, False)
            link(nc.vector.tensor_tensor(mix, mix, gamma[:].unsqueeze(1).to_broadcast([P, NODE_TILES, D]), ALU.mult))
            link(nc.vector.tensor_tensor(mix, mix, beta[:].unsqueeze(1).to_broadcast([P, NODE_TILES, D]), ALU.add))
            link(nc.vector.tensor_tensor(nodes[:], nodes[:], mix, ALU.add))
            layer_norm(dve, nodes[:], link, True)
            attend_dve(dve, regs)

            def attend_out(i, first):
                dve.wait_ge(O2["acc_ps"], i + 1)
                quotients(dve, O2, i, first, mix[:, tiles(i), :], 1e-6)
            loop_chunks(dve, attend_out)
            dve.wait_ge(O2["mixed"], CHUNKS)
            clear_sums()
            link(nc.vector.tensor_tensor(nodes[:], nodes[:], mix, ALU.add))
            layer_norm(dve, nodes[:], link, True)
            gin_dve(dve, G0, regs)

            def gin_sum(i, first):
                dve.wait_ge(M3["xt_ps"], i + 1)
                if not first:
                    dve.wait_ge(M3["hid_ps"], i)
                nc.vector.tensor_tensor(chunk_t, chunk_x, acc[0:D, bass.ds(i * CP, CP)], ALU.add).then_inc(M3["part"], 1)
                dve.wait_ge(M3["part"], i + 1)
                nc.vector.tensor_tensor(chunk_t, chunk_t, acc_odd[0:D, bass.ds(i * CP, CP)], ALU.add).then_inc(M3["sum"], 1)
            loop_chunks(dve, gin_sum)
            dve.wait_ge(M3["sum"], CHUNKS)
            clear_sums()
            gin_dve(dve, G1, regs)

            def gin_out(i, first):
                dve.wait_ge(O3["acc_ps"], i + 1)
                nc.vector.tensor_tensor(mix[:, tiles(i), :], mix[:, tiles(i), :], chunk_a[:, :, 0:D], ALU.add).then_inc(O3["added"], 1)
            loop_chunks(dve, gin_out)
            dve.wait_ge(O3["added"], CHUNKS)
            link(nc.vector.tensor_tensor(mix, mix, b_g2[:].unsqueeze(1).to_broadcast([P, NODE_TILES, D]), ALU.add))
            link(nc.vector.tensor_tensor(nodes[:], nodes[:], mix, ALU.add))
            layer_norm(dve, nodes[:], link, True)


_INS = ["x", "src", "dst", "edge_attr_32", "edge_attr_64",
        "L0_gnn_Wq", "L0_gnn_Wk", "L0_gnn_Wv", "L0_gnn_Wo",
        "L1_gnn_W1n", "L1_gnn_b1n", "L1_gnn_W2n", "L1_gnn_b2n", "L1_gnn_W1e", "L1_gnn_b1e",
        "L1_gnn_W2e", "L1_gnn_b2e", "L1_gnn_res_w", "L1_gnn_dp_scale", "L1_gnn_gamma", "L1_gnn_beta",
        "L2_gnn_Wq", "L2_gnn_Wk", "L2_gnn_We", "L2_gnn_Wv",
        "L3_gnn_W1", "L3_gnn_b1", "L3_gnn_W2", "L3_gnn_b2"]


def kernel(**inputs):
    import numpy as _np
    import concourse.bacc as _bacc
    from concourse import mybir as _mybir
    from concourse.bass_utils import run_bass_kernel_spmd as _run

    nc = _bacc.Bacc("TRN2", target_bir_lowering=False, num_devices=1)
    arrays, args = {}, []
    for name in _INS:
        a = _np.ascontiguousarray(inputs[name])
        arrays[f"in_{name}_dram"] = a
        args.append(nc.dram_tensor(f"in_{name}_dram", a.shape, _mybir.dt.from_np(a.dtype), kind="ExternalInput").ap())
    shape = tuple(inputs["x"].shape)
    args.append(nc.dram_tensor("out_0_dram", shape, _mybir.dt.float32, kind="ExternalOutput").ap())
    build_gnn(nc, *args)
    r = _run(nc, [arrays], core_ids=[0])
    return r.results[0]["out_0_dram"]
```

```python
import concourse.bass as bass
from concourse import mybir
from contextlib import ExitStack

P = 128
GROUP = 8
CHUNK = 4
INDEXES = 4
BIG = 1.0e30
SLOPE = 0.1
EPS = 1.0e-5
CHAIN2 = 4


def build_gnn(nc, x, src, dst, edge_attr_32, edge_attr_64,
              L0_gnn_Wq, L0_gnn_Wk, L0_gnn_Wv, L0_gnn_Wo,
              L1_gnn_W1n, L1_gnn_b1n, L1_gnn_W2n, L1_gnn_b2n, L1_gnn_W1e, L1_gnn_b1e,
              L1_gnn_W2e, L1_gnn_b2e, L1_gnn_res_w, L1_gnn_dp_scale, L1_gnn_gamma, L1_gnn_beta,
              L2_gnn_Wq, L2_gnn_Wk, L2_gnn_We, L2_gnn_Wv,
              L3_gnn_W1, L3_gnn_b1, L3_gnn_W2, L3_gnn_b2, out):
    f32, i32 = mybir.dt.float32, mybir.dt.int32
    ALU, ACT, AX = mybir.AluOpType, mybir.ActivationFunctionType, mybir.AxisListType.X

    N, D = x.shape
    E = src.shape[0]
    H = 4
    DH = D // H
    DE = edge_attr_32.shape[1]
    HID = L3_gnn_W1.shape[1]
    A = D + H

    TILES = -(-E // P)
    GROUPS = -(-TILES // GROUP)
    GROUPS += GROUPS % 2
    PAIRS = GROUPS // 2
    assert (GROUPS - 2) % INDEXES == 0
    EG = GROUP * P
    LAST = GROUPS - 1
    TAIL_TILES = (E - LAST * EG) // P
    TAIL_ROWS = (E - LAST * EG) % P
    assert 0 < TAIL_TILES < GROUP and TAIL_ROWS

    NAT = -(-GROUPS * GROUP // P)
    PARTS = 2 * GROUPS * GROUP
    PART_TILES = -(-2 * NAT * P // P)
    PART_BANKS = -(-PART_TILES // 4)
    LINE_BANKS = -(-PARTS // 512)
    assert PART_BANKS <= 8 and LINE_BANKS <= 8
    CUT = P + 2
    SLOTS = 512 // CUT
    assert 2 * SLOTS < GROUP <= 3 * SLOTS
    FULL = TILES - 1
    NODE_TILES = -(-(N + P) // P)
    NODE_TILES += -NODE_TILES % CHUNK
    CHUNKS = NODE_TILES // CHUNK
    NPAD = NODE_TILES * P
    NREM = N % P
    NFULL = N // P
    CD = CHUNK * D
    CP = CHUNK * P
    BIGW = 22000

    def dram(name, shape, dt=f32):
        return nc.dram_tensor(name, shape, dt, kind="Internal").ap()

    kv_table = dram("kv_table", [NPAD, 2 * D])
    q_table = dram("q_table", [NPAD, D])
    kv2_table = dram("kv2_table", [NPAD, 2 * D])
    q2_table = dram("q2_table", [NPAD, D])
    xt_table = dram("xt_table", [NPAD, D])
    x3_table = dram("x3_table", [NPAD, D])
    y3_table = dram("y3_table", [NPAD, D])
    cut_tiles = dram("cut_tiles", [NAT * P, CUT])
    cut_edges = dram("cut_edges", [NAT * P // GROUP, H, GROUP, CUT])
    part_line = dram("part_line", [1, P + 2 * NAT * P + P])
    part_sums = dram("part_sums", [NPAD, A])
    start_line = dram("start_line", [NAT, P], i32)

    ctx = ExitStack()
    with ctx:
        def sb(name, shape, dt=f32):
            return ctx.enter_context(nc.sbuf_tensor(name, shape, dt))

        def sem(name):
            return ctx.enter_context(nc.semaphore(name))

        def sems(prefix, names):
            return {n: sem(f"{prefix}_{n}") for n in names.split()}

        src_idx = sb("src_idx", [P, NAT * P], i32)
        dst_rel = sb("dst_rel", [P, NAT * P])
        dst_code = sb("dst_code", [P, NAT * P])
        part_index = sb("part_index", [P, PART_TILES], i32)
        head_rows = sb("head_rows", [H, A])
        starts = sb("starts", [1, NAT * P], i32)
        nodes = sb("nodes", [P, NODE_TILES, D])
        acc = sb("acc", [P, NPAD])
        ident = sb("ident", [P, P])
        iota = sb("iota", [P, P + 2])
        ones = sb("ones", [1, P])
        w_qkv = sb("w_qkv", [D, 3 * D])
        w_o = sb("w_o", [D, D])
        w_1n = sb("w_1n", [D, HID])
        w_2n = sb("w_2n", [HID, D])
        w_1e = sb("w_1e", [P, P // DE, 2 * D])
        w_2e = sb("w_2e", [P, D])
        w_nat = sb("w_nat", [D, 4 * D])
        w_2 = sb("w_2", [D, 3 * D])
        w_e = sb("w_e", [P, 2 * D])
        w_g1 = sb("w_g1", [D, HID])
        w_g2 = sb("w_g2", [HID, D])
        b_1n = sb("b_1n", [HID, 1])
        b_1e = sb("b_1e", [P, 1])
        b_g1 = sb("b_g1", [HID, 1])
        b_2n = sb("b_2n", [P, D])
        b_2e = sb("b_2e", [1, D])
        b_g2 = sb("b_g2", [P, D])
        gamma = sb("gamma", [P, D])
        beta = sb("beta", [P, D])
        gains = sb("gains", [P, 2])
        gain = sb("gain", [P, 1])
        index = sb("index", [P, INDEXES, GROUP], i32)
        work = sb("work", [P, 2 * GROUP * 4 * D])
        rows = work[:, 0:4 * GROUP * D].rearrange("p (u k f) -> p u k f", u=2, k=GROUP)
        window = work[:, 4 * GROUP * D:6 * GROUP * D].rearrange("p (u k f) -> p u k f", u=2, k=GROUP)
        product = work[:, 6 * GROUP * D:8 * GROUP * D].rearrange("p (u k f) -> p u k f", u=2, k=GROUP)
        onehot = sb("onehot", [P, 2, GROUP, P])
        onehot_t = sb("onehot_t", [P, 2, GROUP, P])
        message = sb("message", [P, 2, GROUP, A])
        score = sb("score", [P, 2, H * GROUP])
        score_t = sb("score_t", [H * GROUP, 2, P])
        edge_in = sb("edge_in", [P, 2, GROUP, D])
        edge_t = sb("edge_t", [P, 2, 4, P])
        hidden_t = onehot_t
        big = sb("big", [P, BIGW])

        psum = ctx.enter_context(nc.psum_tensor("psum", [P, 8, 512], f32))
        bank = [psum[:, 2 * i:2 * i + 2, :] for i in range(4)]

        def banks(n):
            return psum[:, n, :]

        block = ctx.enter_context(nc.Block())

        def gathers(name):
            return [sem(f"{name}_gathered{u}") for u in range(2)]

        filled = sem("filled")
        consts = sem("consts")
        graph_in = sem("graph_in")
        weights_in = sem("weights_in")
        nodes_in = sem("nodes_in")
        graph_cast = sem("graph_cast")
        graph_ps = sem("graph_ps")
        graph_out = sem("graph_out")
        lines_out = sem("lines_out")
        starts_in = sem("starts_in")
        weights_ps = sem("weights_ps")
        weights_t = sem("weights_t")
        norm = sem("norm")
        parts = sem("parts")
        parts_chain = sem("parts_chain")
        parts_in = sem("parts_in")
        parts_ps = sem("parts_ps")
        parts_act = sem("parts_act")
        parts_out = sem("parts_out")
        parts_back = sem("parts_back")
        code_ps = sem("code_ps")
        code_out = sem("code_out")
        cuts_out = sem("cuts_out")
        cuts_h = sem("cuts_h")
        w_scaled = sem("w_scaled")
        variance = sem("variance")
        root = sem("root")
        zeroed = sem("zeroed")
        normed = sem("normed")
        stored = sem("stored")
        K0 = sems("kv0", "staged xt_ps xt proj_ps proj table")
        O0 = sems("out0", "staged whole acc_ps den mixed mixed_ps mixed_t proj_ps added")
        K1 = sems("mlp1", "staged xt_ps xt hid_ps hid leaky proj_ps proj table")
        O1 = sems("out1", "staged acc_ps added")
        K2 = sems("kv2", "staged xt_ps xt proj_ps proj table")
        O2 = sems("out2", "staged acc_ps den mixed")
        M3 = sems("gin_mid", "staged xt_ps xt sum hid_ps hid proj_ps proj")
        O3 = sems("out3", "staged acc_ps added")
        A0 = sems("mix", "index onehot onehot_ps onehot_t expanded product score score_ps score_t scan shifted "
                         "exp weights_ps weights kept coded message reduced ends added")
        A0["gathered"], A0["window"] = gathers("mix"), [sem(f"mix_window{u}") for u in range(2)]
        A0["cuts"] = [sem(f"mix_cuts{u}") for u in range(2)]
        B0 = sems("gated", "index onehot edge_ps edge_t hid_ps hid edge_mm message reduced added")
        B0["gathered"], B0["edge"] = gathers("gated"), [sem(f"gated_edge{u}") for u in range(2)]
        C0 = sems("attend", "index onehot onehot_ps onehot_t expanded edge_ps edge_t edge_mm chain weights "
                            "message reduced added")
        C0["gathered"], C0["window"] = gathers("attend"), [sem(f"attend_window{u}") for u in range(2)]
        C0["edge"] = [sem(f"attend_edge{u}") for u in range(2)]
        G0 = sems("gin_a", "index onehot reduced added")
        G0["gathered"] = gathers("gin_a")
        G1 = sems("gin_b", "index onehot reduced added")
        G1["gathered"] = gathers("gin_b")

        NATW = NAT * P
        assert 4 * NATW <= NPAD
        nat_src = acc[:, 0:NATW].bitcast(i32).rearrange("p (c e) -> p c e", e=P)
        nat_dst = acc[:, NATW:2 * NATW].bitcast(i32).rearrange("p (c e) -> p c e", e=P)
        flt_src = acc[:, 2 * NATW:3 * NATW].rearrange("p (c e) -> p c e", e=P)
        flt_dst = acc[:, 3 * NATW:4 * NATW].rearrange("p (c e) -> p c e", e=P)
        flt_rel = big[:, 0:NATW].rearrange("p (c e) -> p c e", e=P)
        flt_code = big[:, NATW:2 * NATW].rearrange("p (c e) -> p c e", e=P)
        in_first = big[:, 2 * NATW:3 * NATW].rearrange("p (c e) -> p c e", e=P)
        in_last = big[:, 3 * NATW:4 * NATW].rearrange("p (c e) -> p c e", e=P)
        nat_cuts = onehot[:].rearrange("p u k e -> p (u k e)")[:, 0:NAT * CUT].rearrange("p (c e) -> p c e", e=CUT)
        small = onehot_t[:].rearrange("p u k e -> p (u k e)")
        start_f = small[:, 0:NAT]
        start_i = small[:, NAT:2 * NAT].bitcast(i32)
        at = 2 * NAT
        part_nodes = small[:, at:at + 2 * NAT].rearrange("p (c w) -> p c w", w=2)
        minus = small[0:1, at + 2 * NAT:at + 2 * NAT + P]
        nat_parts = small[0:PART_TILES, at + 2 * NAT + P:at + 2 * NAT + 3 * P].rearrange("p (a e) -> p a e", a=2)
        nothing = small[:, at + 2 * NAT + 3 * P:at + 2 * NAT + 3 * P + A]

        coded = big[:, 0:2 * GROUP * (P + 2)].rearrange("p (u k j) -> p u k j", u=2, k=GROUP)
        at = 2 * GROUP * (P + 2)
        kept = big[:, at:at + 2 * GROUP * D].rearrange("p (u k f) -> p u k f", u=2, k=GROUP)
        at += 2 * GROUP * D
        cuts_in = big[0:H * GROUP, at:at + 2 * CUT].rearrange("p (u e) -> p u e", u=2)
        at += 2 * CUT
        running = big[0:H * GROUP, at:at + 2 * P].rearrange("p (u e) -> p u e", u=2)
        exp_t = big[0:H * GROUP, at + 2 * P:at + 4 * P].rearrange("p (u e) -> p u e", u=2)
        at += 4 * P
        part_max = big[0:H * GROUP, at:at + 2 * GROUPS].rearrange("p (g w) -> p g w", w=2)
        at += 2 * GROUPS
        part_t = big[:, at:at + PART_TILES * P]
        at += PART_TILES * P
        part_line_in = big[:, at:at + PARTS + 2]
        same = big[:, at + PARTS + 2:at + 2 * PARTS + 3]
        assert at + 2 * PARTS + 3 <= BIGW - NPAD
        line_a = big[0:H, 0:PARTS]
        line_c = part_line_in[0:H, 0:PARTS + 1]
        line_m = work[0:H, 0:PARTS]
        assert PARTS <= 8 * GROUP * D
        part_rows = big[:, 0:PART_TILES * A].rearrange("p (c f) -> p c f", f=A)
        node_parts = big[:, PART_TILES * A:PART_TILES * A + NODE_TILES * A].rearrange("p (t f) -> p t f", f=A)

        W = NODE_TILES * D
        mix = big[:, 0:W].rearrange("p (t d) -> p t d", d=D)
        squares = big[:, W:2 * W].rearrange("p (t d) -> p t d", d=D)
        stats = big[:, 2 * W:2 * W + 2 * NODE_TILES].rearrange("p (a t) -> p a t", a=2)
        at = 2 * W + 2 * NODE_TILES
        chunk_t = big[0:D, at:at + CP]
        chunk_h = big[:, at + CP:at + 2 * CP]
        chunk_l = big[:, at + 2 * CP:at + 3 * CP]
        chunk_p = big[:, at + 3 * CP:at + 3 * CP + 3 * CD].rearrange("p (t f) -> p t f", f=3 * D)
        chunk_m = big[:, at + 3 * CP + 3 * CD:at + 3 * CP + 4 * CD].rearrange("p (t f) -> p t f", f=D)
        assert PART_TILES * A + NODE_TILES * A <= at and 4 * NATW <= at
        chunk_d = big[:, at + 3 * CP + 4 * CD:at + 3 * CP + 4 * CD + CHUNK * H].rearrange("p (t h) -> p t h", h=H)
        at += 3 * CP + 4 * CD + CHUNK * H
        stage_x = big[:, at:at + CD].rearrange("p (t d) -> p t d", d=D)
        stage_a = big[:, at + CD:at + CD + CP]
        acc_odd = big[:, BIGW - NPAD:BIGW]
        chunk_s = big[:, at + CD + CP:at + CD + CP + CHUNK * A].rearrange("p (t f) -> p t f", f=A)
        assert at + CD + CP + CHUNK * A <= BIGW - NPAD
        chunk_a = banks(1).rearrange("p (t f) -> p t f", f=P)
        chunk_x2 = banks(0)[:, 0:CP // 2].rearrange("p (m e) -> p m e", e=P)
        chunk_u = banks(4)[:, :]
        chunk_v = banks(5)[:, 0:CD].rearrange("p (t f) -> p t f", f=D)

        def chunk_w(t):
            return bank[1][:, t // 2, (t % 2) * 3 * D:(t % 2 + 1) * 3 * D]

        def tiles(i):
            return bass.ds(i * CHUNK, CHUNK)

        def loop_pairs(eng, body, peeled=1):
            for i in range(peeled):
                body(i)
            with eng.Fori(peeled, PAIRS - 1) as i:
                body(i)
            body(PAIRS - 1)

        def group_at(i, u, k=0):
            return 2 * i + u + k, (u + k) % 2, i + (u + k) // 2

        def since(g, n):
            return not isinstance(g, int) or g >= n

        def is_group(g):
            return not isinstance(g, int) or g < GROUPS

        def loop_chunks(eng, body):
            body(0, True)
            with eng.Fori(1, CHUNKS) as i:
                body(i, False)

        def loop_ahead(eng, body, ahead):
            body(0)
            with eng.Fori(1, CHUNKS - ahead) as i:
                body(i)
            for i in range(CHUNKS - ahead, CHUNKS):
                body(i)

        def is_first(i):
            return isinstance(i, int) and i == 0

        def is_chunk(i):
            return not isinstance(i, int) or i < CHUNKS

        def heads(ap):
            return ap.rearrange("p t (h d) -> p t h d", h=H)

        def blocks_of(v):
            c = FULL // P
            yield (slice(0, P), slice(0, c), slice(0, P)), v[0:c * P * P].rearrange("(c p e) -> p c e", p=P, e=P)
            yield (slice(0, FULL - c * P), c, slice(0, P)), v[c * P * P:FULL * P].rearrange("(p e) -> p e", e=P)
            yield (slice(FULL - c * P, FULL - c * P + 1), c, slice(0, E - FULL * P)), v[FULL * P:E].rearrange("(p e) -> p e", p=1)

        def row_of(v):
            return v.rearrange("(a n) -> a n", a=1)

        first_loads = [(w_qkv[:, 0:D], L0_gnn_Wk), (w_qkv[:, D:2 * D], L0_gnn_Wv), (w_qkv[:, 2 * D:], L0_gnn_Wq)]
        weight_loads = [
            (w_o[:], L0_gnn_Wo), (w_1n[:], L1_gnn_W1n), (w_2n[:], L1_gnn_W2n),
            (w_2e[0:D, :], L1_gnn_W2e), (w_2e[D:P, :], L1_gnn_W2e),
            (w_nat[:, 0:D], L2_gnn_Wk), (w_nat[:, D:2 * D], L2_gnn_Wv), (w_nat[:, 2 * D:3 * D], L2_gnn_Wq),
            (w_nat[:, 3 * D:], L2_gnn_We), (w_g1[:], L3_gnn_W1), (w_g2[:], L3_gnn_W2),
            (b_1n[:], L1_gnn_b1n.rearrange("(n a) -> n a", a=1)),
            (b_1e[0:D, :], L1_gnn_b1e.rearrange("(n a) -> n a", a=1)),
            (b_1e[D:P, :], L1_gnn_b1e.rearrange("(n a) -> n a", a=1)),
            (b_g1[:], L3_gnn_b1.rearrange("(n a) -> n a", a=1)),
            (b_2n[:], row_of(L1_gnn_b2n).to_broadcast([P, D])), (b_2e[:], row_of(L1_gnn_b2e)),
            (b_g2[:], row_of(L3_gnn_b2).to_broadcast([P, D])),
            (gamma[:], row_of(L1_gnn_gamma).to_broadcast([P, D])),
            (beta[:], row_of(L1_gnn_beta).to_broadcast([P, D])),
            (gains[:, 0:1], row_of(L1_gnn_dp_scale).to_broadcast([P, 1])),
            (gains[:, 1:2], row_of(L1_gnn_res_w).to_broadcast([P, 1])),
        ] + [(w_1e[DE * r:DE * (r + 1), r, D * c:D * (c + 1)], L1_gnn_W1e) for r in range(P // DE) for c in range(2)]
        WEIGHTS_IN = 16 * len(weight_loads)
        GRAPH_IN = 16 * 6
        assert NFULL % CHUNK == 0
        NODES_IN = 16 * (NFULL // CHUNK + 1 + len(first_loads))
        LINES_OUT = 16 * 5

        def store_tables(sp, K, parts):
            with sp.Fori(0, CHUNKS) as i:
                sp.wait_ge(K["proj"], parts * (i + 1))
                if parts == 2:
                    sp.dma_start(kv_table.rearrange("(t p) f -> p t f", p=P)[:, tiles(i), :],
                                 chunk_p[:, :, 0:2 * D]).then_inc(K["table"], 16)
                    sp.dma_start(q_table.rearrange("(t p) f -> p t f", p=P)[:, tiles(i), :],
                                 chunk_p[:, :, 2 * D:3 * D]).then_inc(K["table"], 16)
                else:
                    sp.dma_start(xt_table.rearrange("(t p) f -> p t f", p=P)[:, tiles(i), :],
                                 chunk_p[:, :, 0:D]).then_inc(K["table"], 16)

        def load_edges(sp, C, edges, g, u):
            to = edge_in[:, u, :, :].rearrange("p k f -> p (k f)")[:, 0:GROUP * edges.shape[1]].rearrange(
                "p (k f) -> p k f", k=GROUP)
            if since(g, 2):
                sp.wait_ge(C["edge_ps"], g - 1)
            if not (isinstance(g, int) and g == LAST):
                sp.dma_start(to, edges[bass.ds(g * EG, EG), :].rearrange("(k p) f -> p k f", p=P)).then_inc(C["edge"][u], 16)
            else:
                at = LAST * EG
                sp.dma_start(to[:, 0:TAIL_TILES, :], edges[at:at + TAIL_TILES * P, :].rearrange(
                    "(k p) f -> p k f", p=P)).then_inc(C["edge"][u], 16)
                sp.dma_start(to[0:TAIL_ROWS, TAIL_TILES, :], edges[at + TAIL_TILES * P:E, :]).then_inc(C["edge"][u], 16)

        def edge_landed(g, i):
            return 16 * (i + 2) if isinstance(g, int) and g == LAST else 16 * (i + 1)

        def load_windows(sp, C, regs, edges):
            if C is A0:
                sp.wait_ge(K0["table"], 32 * CHUNKS)
            else:
                sp.wait_ge(K2["table"], 32 * CHUNKS)

            def cuts(g, u):
                if isinstance(g, int) and g == 0:
                    sp.wait_ge(cuts_h, 16 * H)
                    sp.wait_ge(code_ps, 1)
                if since(g, 2):
                    sp.wait_ge(A0["scan"], 2 * (g - 1))
                sp.dma_start(cuts_in[:, u, :], cut_edges[bass.ds(g, 1)].rearrange("a h k e -> (a h k) e")
                             ).then_inc(A0["cuts"][u], 16)

            def body(i):
                for u in range(2):
                    g = 2 * i + u
                    if C is C0:
                        load_edges(sp, C, edges, g, u)
                    elif since(g, 1):
                        cuts(g - 1, 1 - u)
                    if since(g, 2):
                        sp.wait_ge(C["expanded"], g - 1)
                    sp.load(regs, starts[0:1, bass.ds(g * GROUP, GROUP)])
                    for k in range(GROUP):
                        at = sp.snap(regs[k], min_val=0, max_val=N - 1)
                        sp.dma_start(window[:, u, k, :], q_table[bass.ds(at, P), :]).then_inc(C["window"][u], 16)
            loop_pairs(sp, body, 2)
            if C is A0:
                cuts(LAST, 1)

        def gated_dma(sp):
            def body(i):
                for u in range(2):
                    load_edges(sp, B0, edge_attr_32, 2 * i + u, u)
            loop_pairs(sp, body)

        def gathered_rows(u, width):
            return rows[:, u, :, :].rearrange("p k f -> p (k f)")[:, 0:GROUP * width].rearrange("p (k f) -> p k f", k=GROUP)

        def clear_sums(even=True):
            if even:
                nc.gpsimd.memset(acc[:], 0.0)
            nc.gpsimd.memset(acc_odd, 0.0).then_inc(zeroed, 1)

        def gather(pool, C, table, width, users):
            def body(g, pair, m, first, last):
                u = m % 2
                if not first:
                    for s, n in users:
                        if isinstance(s, list):
                            pool.wait_ge(s[u], n * pair)
                        else:
                            pool.wait_ge(s, n * (g - 1))
                pool.wait_ge(C["index"], g + 1)
                if not last:
                    nc.gpsimd.tensor_copy(index[:, (m + 1) % INDEXES, :], src_idx[:, bass.ds((g + 1) * GROUP, GROUP)]
                                          ).then_inc(C["index"], 1)
                for k in range(GROUP):
                    pool.indirect_dma_start(gathered_rows(u, width)[:, k, :], None, table,
                                            bass.IndirectOffsetOnAxis(index[:, m, k:k + 1], 0)
                                            ).then_inc(C["gathered"][u], 16)

            nc.gpsimd.tensor_copy(index[:, 0, :], src_idx[:, 0:GROUP]).then_inc(C["index"], 1)
            body(0, 0, 0, True, False)
            body(1, 0, 1, True, False)
            with pool.Fori(0, (GROUPS - 2) // INDEXES - 1) as i:
                for v in range(INDEXES):
                    body(INDEXES * i + 2 + v, INDEXES // 2 * i + 1 + v // 2, (2 + v) % INDEXES, False, False)
            for v in range(INDEXES):
                g = GROUPS - INDEXES + v
                body(g, g // 2, g % INDEXES, False, v == INDEXES - 1)

        def landed(i):
            return 16 * GROUP * (i + 1)

        def stage_nodes(act, K, i, first):
            if not first:
                act.wait_ge(K["xt_ps"], i)
            nc.scalar.copy(stage_x, nodes[:, tiles(i), :]).then_inc(K["staged"], 1)

        def copy_turned(to):
            to = to.rearrange("f (m a e) -> f m a e", a=2, e=P)
            nc.scalar.copy(to[:, :, 0, :], chunk_x2[0:D])
            return nc.scalar.copy(to[:, :, 1, :], chunk_x2[D:P])

        def square_root(act, n):
            act.wait_ge(variance, n)
            nc.scalar.activation(stats[:, 1, :], stats[:, 1, :], ACT.Sqrt).then_inc(root, 1)

        def copy_projections(act, K, parts):
            def body(i):
                act.wait_ge(K["xt_ps"], i + 1)
                if not is_first(i):
                    act.wait_ge(K["proj_ps"], i)
                copy_turned(chunk_t).then_inc(K["xt"], 1)
                if is_chunk(i + 1):
                    stage_nodes(act, K, i + 1, False)
                act.wait_ge(K["proj_ps"], i + 1)
                if not is_first(i):
                    act.wait_ge(K["table"], 16 * parts * i)
                nc.scalar.copy(chunk_p[:, 0:2, :], bank[1][:, 0, 0:6 * D].rearrange("p (t f) -> p t f", t=2)).then_inc(K["proj"], 1)
                nc.scalar.copy(chunk_p[:, 2:4, :], bank[1][:, 1, 0:6 * D].rearrange("p (t f) -> p t f", t=2)).then_inc(K["proj"], 1)
            stage_nodes(act, K, 0, True)
            loop_ahead(act, body, 1)

        def mix_act(act):
            def onehots(g, u):
                act.wait_ge(A0["onehot_ps"], g + 1)
                if since(g, 2):
                    act.wait_ge(A0["expanded"], g - 1)
                nc.scalar.copy(onehot_t[:, u, :, :], bank[0][:].rearrange("p a (k j) -> p (a k) j", j=P)
                               ).then_inc(A0["onehot_t"], 1)

            def weights(g, u):
                act.wait_ge(A0["shifted"], g + 1)
                nc.scalar.activation(exp_t[:, u, :], exp_t[:, u, :], ACT.Exp, scale=-1.0).then_inc(A0["exp"], 1)
                act.wait_ge(A0["weights_ps"], g + 1)
                if since(g, 2):
                    act.wait_ge(A0["reduced"], g - 1)
                nc.scalar.copy(message[:, u, :, D:A],
                               banks(7)[:, (8 + u) * 32:(9 + u) * 32].rearrange("p (h k) -> p k h", h=H)
                               ).then_inc(A0["weights"], 1)

            def keep(g, u, i):
                act.wait_ge(A0["gathered"][u], landed(i))
                if since(g, 2):
                    act.wait_ge(A0["message"], g - 1)
                nc.scalar.copy(kept[:, u, :, :], rows[:, u, :, D:2 * D]).then_inc(A0["kept"], 1)

            def scores(g, u):
                act.wait_ge(A0["score_ps"], g + 1)
                if since(g, 2):
                    act.wait_ge(A0["shifted"], g - 1)
                nc.scalar.mul(score_t[:, u, :], banks(7)[0:H * GROUP, u * P:(u + 1) * P], DH ** -0.5
                              ).then_inc(A0["score_t"], 1)

            def body(i):
                for u in range(2):
                    g = 2 * i + u
                    if is_group(g + 1):
                        onehots(g + 1, 1 - u)
                    if since(g, 1):
                        weights(g - 1, 1 - u)
                    keep(g, u, i)
                    scores(g, u)
            onehots(0, 0)
            loop_pairs(act, body)
            weights(LAST, 1)

        def parts_on_act(act):
            for k in range(GROUP):
                act.wait_ge(parts_ps, k + 1)
                last = nc.scalar.copy(line_a.rearrange("h (g k w) -> h g k w", k=GROUP, w=2)[:, :, k, :],
                                      banks(k)[0:H, 0:2 * GROUPS].rearrange("h (g w) -> h g w", w=2))
            last.then_inc(parts_act, 1)
            act.wait_ge(parts, 4)
            nc.scalar.activation(line_m, line_m, ACT.Exp, scale=-1.0).then_inc(parts_act, 1)
            for b in range(PART_BANKS):
                n = min(PART_TILES - 4 * b, 4)
                act.wait_ge(parts_ps, GROUP + LINE_BANKS + b + 1)
                nc.scalar.copy(part_rows[:, 4 * b:4 * b + n, :], banks(b).rearrange("p (c f) -> p c f", f=P)[:, 0:n, 0:A]
                               ).then_inc(parts_act, 1)

        def mixed_act(act):
            def body(i):
                act.wait_ge(O0["mixed_ps"], i + 1)
                if not is_first(i):
                    act.wait_ge(O0["proj_ps"], i)
                copy_turned(chunk_t).then_inc(O0["mixed_t"], 1)
            loop_ahead(act, body, 1)

        def mlp_act(act):
            act.wait_ge(normed, 1)

            def turned_nodes(i):
                act.wait_ge(K1["xt_ps"], i + 1)
                if not is_first(i):
                    act.wait_ge(K1["hid_ps"], i)
                copy_turned(chunk_t).then_inc(K1["xt"], 1)

            def body(i):
                act.wait_ge(K1["hid_ps"], i + 1)
                if not is_first(i):
                    act.wait_ge(K1["leaky"], i)
                nc.scalar.activation(chunk_h, chunk_u, ACT.Identity, bias=b_1n[:, 0:1]).then_inc(K1["hid"], 1)
                if is_chunk(i + 1):
                    turned_nodes(i + 1)
                if is_chunk(i + 2):
                    stage_nodes(act, K1, i + 2, False)
            stage_nodes(act, K1, 0, True)
            turned_nodes(0)
            stage_nodes(act, K1, 1, False)
            loop_ahead(act, body, 2)

        def gated_act(act):
            def features(g, u):
                act.wait_ge(B0["edge_ps"], g + 1)
                if since(g, 2):
                    act.wait_ge(B0["hid_ps"], g - 1)
                nc.scalar.copy(edge_t[:, u, 0:2, :], bank[2][:, 0, 0:2 * P].rearrange("p (m e) -> p m e", m=2)
                               ).then_inc(B0["edge_t"], 1)

            def hidden(g, u):
                act.wait_ge(B0["hid_ps"], g + 1)
                if since(g, 2):
                    act.wait_ge(B0["edge_mm"], g - 1)
                hid = bank[1][:].rearrange("p a (k e) -> p (a k) e", e=P)
                nc.scalar.activation(hidden_t[0:D, u, :, :], hid[0:D], ACT.Identity, bias=b_1e[0:D, 0:1]
                                     ).then_inc(B0["hid"], 1)
                nc.scalar.activation(hidden_t[D:P, u, :, :], hid[D:P], ACT.Relu, bias=b_1e[D:P, 0:1]
                                     ).then_inc(B0["hid"], 1)

            def body(i):
                for u in range(2):
                    h, v, _ = group_at(i, u, 1)
                    if is_group(h):
                        features(h, v)
                        hidden(h, v)
            features(0, 0)
            hidden(0, 0)
            loop_pairs(act, body)

        def attend_act(act):
            def body(i):
                for u in range(2):
                    g = 2 * i + u
                    act.wait_ge(C0["onehot_ps"], g + 1)
                    if since(g, 2):
                        act.wait_ge(C0["expanded"], g - 1)
                        act.wait_ge(C0["edge_mm"], g - 1)
                    nc.scalar.copy(onehot_t[:, u, :, :], bank[1][:].rearrange("p a (k j) -> p (a k) j", j=P)
                                   ).then_inc(C0["onehot_t"], 1)
                    act.wait_ge(C0["edge_ps"], g + 1)
                    nc.scalar.copy(edge_t[:, u, :, :], bank[3][:, 0, :].rearrange("p (m e) -> p m e", m=4)
                                   ).then_inc(C0["edge_t"], 1)
                    act.wait_ge(C0["chain"], CHAIN2 * (g + 1))
                    if since(g, 2):
                        act.wait_ge(C0["reduced"], g - 1)
                    nc.scalar.activation(message[:, u, :, D:A], score[:, u, :].rearrange("p (k h) -> p k h", h=H),
                                         ACT.Exp, scale=DH ** -0.5).then_inc(C0["weights"], 1)
            loop_pairs(act, body)

        def gin_start_act(act):
            act.wait_ge(normed, 3)

            def body(i):
                act.wait_ge(M3["xt_ps"], i + 1)
                copy_turned(acc[0:D, bass.ds(i * CP, CP)]).then_inc(M3["xt"], 1)
                if is_chunk(i + 1):
                    stage_nodes(act, M3, i + 1, False)
            stage_nodes(act, M3, 0, True)
            loop_ahead(act, body, 1)

        def gin_act(act):
            def body(i):
                act.wait_ge(M3["hid_ps"], i + 1)
                if not is_first(i):
                    act.wait_ge(M3["proj_ps"], i)
                nc.scalar.activation(chunk_h, chunk_u, ACT.Relu, bias=b_g1[:, 0:1]).then_inc(M3["hid"], 1)
                act.wait_ge(M3["proj_ps"], i + 1)
                nc.scalar.copy(mix[:, tiles(i), :], chunk_v).then_inc(M3["proj"], 1)
            loop_ahead(act, body, 1)

        def turned(to, of, eye):
            return nc.tensor.matmul(to, of, eye, start=True, stop=True)

        def turn_pairs(of):
            for m in range(CHUNK // 2):
                last = nc.tensor.transpose(chunk_x2[:, m, :], of[:, 2 * m:2 * m + 2, :].rearrange("p t d -> p (t d)"), ident[:])
            return last

        def turn_nodes(pe, i, K):
            pe.wait_ge(K["staged"], i + 1)
            turn_pairs(stage_x).then_inc(K["xt_ps"], 1)

        def project(pe, K, w):
            def body(i, first):
                if not first:
                    pe.wait_ge(K["xt"], i)
                turn_nodes(pe, i, K)
                pe.wait_ge(K["xt"], i + 1)
                if not first:
                    pe.wait_ge(K["proj"], 2 * i)
                for t in range(CHUNK):
                    last = nc.tensor.matmul(chunk_w(t), chunk_t[:, t * P:(t + 1) * P], w[:], start=True, stop=True)
                last.then_inc(K["proj_ps"], 1)
            loop_chunks(pe, body)

        def expand(C, u, to):
            for k in range(GROUP):
                last = nc.tensor.matmul(to[:, k * D:(k + 1) * D], onehot_t[:, u, k, :], window[:, u, k, :],
                                        start=True, stop=True)
            last.then_inc(C["expanded"], 1)

        def turn_onehots(C, u, to):
            for k in range(GROUP):
                last = nc.tensor.transpose(to[:, k // 4, k % 4 * P:(k % 4 + 1) * P], onehot[:, u, k, :], ident[:])
            last.then_inc(C["onehot_ps"], 1)

        def sums_in(of):
            return lambda k: of[:, k // 4, k % 4 * P:(k % 4 + 1) * P]

        def tile_sums(k):
            return psum[:, 2 + k // SLOTS, k % SLOTS * CUT:(k % SLOTS + 1) * CUT]

        def ends_of(b):
            if b == 0:
                return psum[0:A, 2:4, 0:SLOTS * CUT].rearrange("p b (k j) -> p b k j", j=CUT)[:, :, :, P:CUT]
            return psum[0:A, 4, 0:(GROUP - 2 * SLOTS) * CUT].rearrange("p (k j) -> p k j", j=CUT)[:, :, P:CUT]

        def reduce(C, u, to, width, of):
            for k in range(GROUP):
                last = nc.tensor.matmul(to[0:width, k // 4, k % 4 * P:(k % 4 + 1) * P], of(k), onehot[:, u, k, :],
                                        start=True, stop=True)
            last.then_inc(C["reduced"], 1)

        def mix_pe(pe):
            pe.wait_ge(K0["proj"], 2 * CHUNKS)

            def turn(g, u):
                pe.wait_ge(A0["onehot"], g + 1)
                if since(g, 1):
                    pe.wait_ge(A0["onehot_t"], g)
                turn_onehots(A0, u, bank[0])

            def sums(g, u):
                pe.wait_ge(A0["message"], g + 1)
                pe.wait_ge(A0["coded"], g + 1)
                if since(g, 1):
                    pe.wait_ge(A0["added"], GROUP * g)
                    pe.wait_ge(A0["ends"], 2 * g)
                for k in range(GROUP):
                    last = nc.tensor.matmul(tile_sums(k)[0:A, :], message[:, u, k, :], coded[:, u, k, :], start=True, stop=True)
                last.then_inc(A0["reduced"], 1)

            def turn_scores(g, u):
                pe.wait_ge(A0["score"], g + 1)
                if since(g, 1):
                    pe.wait_ge(A0["weights"], g)
                turned(banks(7)[0:H * GROUP, u * P:(u + 1) * P], score[:, u, :], ident[:]).then_inc(A0["score_ps"], 1)

            def turn_weights(g, u):
                pe.wait_ge(A0["exp"], g + 1)
                pe.wait_ge(A0["score_t"], g + 1)
                turned(banks(7)[:, (8 + u) * 32:(9 + u) * 32], exp_t[:, u, :], ident[0:H * GROUP, 0:H * GROUP]
                       ).then_inc(A0["weights_ps"], 1)

            def body(i):
                for u in range(2):
                    g = 2 * i + u
                    if is_group(g + 1):
                        turn(g + 1, 1 - u)
                    pe.wait_ge(A0["onehot_t"], g + 1)
                    pe.wait_ge(A0["window"][u], landed(i))
                    if since(g, 2):
                        pe.wait_ge(A0["product"], g - 1)
                    expand(A0, u, banks(5 + u))
                    if since(g, 2):
                        sums(g - 2, u)
                    if since(g, 1):
                        turn_weights(g - 1, 1 - u)
                    turn_scores(g, u)
            turn(0, 0)
            loop_pairs(pe, body, 2)
            sums(LAST - 1, 0)
            turn_weights(LAST, 1)
            sums(LAST, 1)

        def parts_pe(pe):
            pe.wait_ge(A0["scan"], 2 * GROUPS)
            pe.wait_ge(A0["added"], GROUP * GROUPS)
            pe.wait_ge(A0["ends"], 2 * GROUPS)
            for k in range(GROUP):
                nc.tensor.matmul(banks(k)[0:H, 0:2 * GROUPS], ident[0:H * GROUP, k:H * GROUP:GROUP],
                                 part_max.rearrange("p g w -> p (g w)"), start=True, stop=True).then_inc(parts_ps, 1)
            pe.wait_ge(parts_act, 2)
            pe.wait_ge(A0["score_ps"], GROUPS)
            for b in range(LINE_BANKS):
                n = min(PARTS - 512 * b, 512)
                nc.tensor.matmul(banks(b)[0:A, 0:n], head_rows[:], line_m[:, 512 * b:512 * b + n], start=True, stop=True
                                 ).then_inc(parts_ps, 1)
            pe.wait_ge(parts, 6)
            for c in range(PART_TILES):
                last = nc.tensor.transpose(banks(c // 4)[:, c % 4 * P:(c % 4 + 1) * P], part_t[:, c * P:(c + 1) * P], ident[:])
                if c % 4 == 3 or c == PART_TILES - 1:
                    last.then_inc(parts_ps, 1)

        def turn_sums(pe, O):
            def body(i, first):
                if not first:
                    pe.wait_ge(O["mixed"] if O is O2 else O["added"], i)
                turn_chunk_sums(pe, i, O)
            loop_chunks(pe, body)

        def turn_chunk_sums(pe, i, O):
            pe.wait_ge(O["staged"], i + 1)
            for t in range(CHUNK):
                last = nc.tensor.transpose(chunk_a[:, t, :], stage_a[:, t * P:(t + 1) * P], ident[:])
            last.then_inc(O["acc_ps"], 1)

        def mix_out_pe(pe):
            def body(i):
                if is_chunk(i + 1):
                    pe.wait_ge(O0["whole"], i + 1)
                    turn_chunk_sums(pe, i + 1, O0)
                pe.wait_ge(O0["mixed"], i + 1)
                if not is_first(i):
                    pe.wait_ge(O0["mixed_t"], i)
                turn_pairs(chunk_m).then_inc(O0["mixed_ps"], 1)
                pe.wait_ge(O0["mixed_t"], i + 1)
                if not is_first(i):
                    pe.wait_ge(O0["added"], i)
                for t in range(CHUNK):
                    last = nc.tensor.matmul(chunk_v[:, t, :], chunk_t[:, t * P:(t + 1) * P], w_o[:], start=True, stop=True)
                last.then_inc(O0["proj_ps"], 1)
            pe.wait_ge(parts_act, 2 + PART_BANKS)
            turn_chunk_sums(pe, 0, O0)
            loop_ahead(pe, body, 1)

        def mlp_pe(pe):
            pe.wait_ge(normed, 1)

            def hidden(i):
                pe.wait_ge(K1["xt"], i + 1)
                if not is_first(i):
                    pe.wait_ge(K1["hid"], i)
                nc.tensor.matmul(chunk_u, w_1n[:], chunk_t, start=True, stop=True).then_inc(K1["hid_ps"], 1)

            def body(i):
                if is_chunk(i + 1):
                    pe.wait_ge(K1["xt"], i + 1)
                    turn_nodes(pe, i + 1, K1)
                    hidden(i + 1)
                pe.wait_ge(K1["leaky"], i + 1)
                if not is_first(i):
                    pe.wait_ge(K1["proj"], i)
                for t in range(CHUNK):
                    last = nc.tensor.matmul(chunk_v[:, t, :], chunk_l[:, t * P:(t + 1) * P], w_2n[:], start=True, stop=True)
                last.then_inc(K1["proj_ps"], 1)
            turn_nodes(pe, 0, K1)
            hidden(0)
            loop_ahead(pe, body, 1)

        def gated_pe(pe):
            pe.wait_ge(w_scaled, 2)
            pe.wait_ge(K1["proj"], CHUNKS)

            def turn_features(g, u, i):
                pe.wait_ge(B0["edge"][u], edge_landed(g, i))
                if since(g, 1):
                    pe.wait_ge(B0["edge_t"], g)
                flat = edge_in[:, u, :, :].rearrange("p k f -> p (k f)")
                for m in range(2):
                    last = nc.tensor.transpose(bank[2][:, 0, m * P:(m + 1) * P], flat[:, m * P:(m + 1) * P], ident[:])
                last.then_inc(B0["edge_ps"], 1)

            def hidden(g, u):
                pe.wait_ge(B0["edge_t"], g + 1)
                if since(g, 1):
                    pe.wait_ge(B0["hid"], 2 * g)
                for k in range(GROUP):
                    last = nc.tensor.matmul(bank[1][:, k // 4, k % 4 * P:(k % 4 + 1) * P], w_1e[:, k % (P // DE), :],
                                            edge_t[:, u, k * DE // P, :], start=True, stop=True)
                last.then_inc(B0["hid_ps"], 1)

            def second(g, u):
                pe.wait_ge(B0["hid"], 2 * (g + 1))
                if since(g, 1):
                    pe.wait_ge(B0["message"], g)
                for k in range(GROUP):
                    to = bank[2][:, 1, k * D:(k + 1) * D]
                    nc.tensor.matmul(to, hidden_t[:, u, k, :], w_2e[:], start=True, stop=False)
                    last = nc.tensor.matmul(to, ones[:], b_2e[:], start=False, stop=True)
                last.then_inc(B0["edge_mm"], 1)

            def sums(g, u):
                pe.wait_ge(B0["message"], g + 1)
                pe.wait_ge(B0["onehot"], g + 1)
                if since(g, 2):
                    pe.wait_ge(B0["added"], GROUP * (g - 1))
                reduce(B0, u, bank[3 * u], D, message_of(u, D))

            def body(i):
                for u in range(2):
                    g = 2 * i + u
                    h, v, j = group_at(i, u, 1)
                    if is_group(h):
                        turn_features(h, v, j)
                    second(g, u)
                    if is_group(h):
                        hidden(h, v)
                    if since(g, 1):
                        sums(g - 1, 1 - u)
            turn_features(0, 0, 0)
            hidden(0, 0)
            loop_pairs(pe, body)
            sums(LAST, 1)

        def message_of(u, width):
            return lambda k: message[:, u, k, 0:width]

        def attend_pe(pe):
            pe.wait_ge(K2["proj"], 2 * CHUNKS)

            def sums(g, u):
                pe.wait_ge(C0["message"], g + 1)
                if since(g, 1):
                    pe.wait_ge(C0["added"], GROUP * g)
                reduce(C0, u, bank[0], A, message_of(u, A))

            def body(i):
                for u in range(2):
                    g = 2 * i + u
                    pe.wait_ge(C0["onehot"], g + 1)
                    if since(g, 1):
                        pe.wait_ge(C0["onehot_t"], g)
                    turn_onehots(C0, u, bank[1])
                    pe.wait_ge(C0["edge"][u], edge_landed(g, i))
                    if since(g, 1):
                        pe.wait_ge(C0["edge_t"], g)
                    for m in range(4):
                        last = nc.tensor.transpose(bank[3][:, 0, m * P:(m + 1) * P],
                                                   edge_in[:, u, 2 * m:2 * m + 2, :].rearrange("p k f -> p (k f)"), ident[:])
                    last.then_inc(C0["edge_ps"], 1)
                    pe.wait_ge(C0["onehot_t"], g + 1)
                    pe.wait_ge(C0["window"][u], landed(i))
                    if since(g, 1):
                        pe.wait_ge(C0["chain"], CHAIN2 * (g - 1) + 2)
                    expand(C0, u, bank[2][:, 0, :])
                    pe.wait_ge(C0["edge_t"], g + 1)
                    for m in range(GROUP // 2):
                        last = nc.tensor.matmul(bank[2][:, 1, m * 2 * D:(m + 1) * 2 * D], edge_t[:, u, m, :], w_e[:],
                                                start=True, stop=True)
                    last.then_inc(C0["edge_mm"], 1)
                    if since(g, 1):
                        sums(g - 1, 1 - u)
            loop_pairs(pe, body)
            sums(LAST, 1)

        def gin_pe(pe, G):
            def body(i):
                for u in range(2):
                    g = 2 * i + u
                    pe.wait_ge(G["onehot"], g + 1)
                    pe.wait_ge(G["gathered"][u], landed(i))
                    if since(g, 2):
                        pe.wait_ge(G["added"], GROUP * (g - 1))
                    reduce(G, u, bank[u], D, lambda k: gathered_rows(u, D)[:, k, :])
            loop_pairs(pe, body)

        def gin_start_pe(pe):
            def body(i, first):
                if not first:
                    pe.wait_ge(M3["xt"], i)
                turn_nodes(pe, i, M3)
            loop_chunks(pe, body)

        def gin_mid_pe(pe):
            def hidden(i):
                pe.wait_ge(M3["sum"], i + 1)
                if not is_first(i):
                    pe.wait_ge(M3["hid"], i)
                nc.tensor.matmul(chunk_u, w_g1[:], chunk_t, start=True, stop=True).then_inc(M3["hid_ps"], 1)

            def body(i):
                if is_chunk(i + 1):
                    hidden(i + 1)
                pe.wait_ge(M3["hid"], i + 1)
                if not is_first(i):
                    pe.wait_ge(M3["proj"], i)
                for t in range(CHUNK):
                    last = nc.tensor.matmul(chunk_v[:, t, :], chunk_h[:, t * P:(t + 1) * P], w_g2[:], start=True, stop=True)
                last.then_inc(M3["proj_ps"], 1)
            hidden(0)
            loop_ahead(pe, body, 1)


        roots = [0]

        def layer_norm(dve, v, link, signal):
            mean, var = stats[:, 0, :], stats[:, 1, :]
            link(nc.vector.tensor_reduce(mean, v, AX, ALU.add))
            link(nc.vector.tensor_scalar_mul(mean, mean, 1.0 / D))
            link(nc.vector.tensor_tensor(v, v, mean.unsqueeze(2).to_broadcast([P, NODE_TILES, D]), ALU.subtract))
            link(nc.vector.tensor_tensor(squares, v, v, ALU.mult))
            link(nc.vector.tensor_reduce(var, squares, AX, ALU.add))
            nc.vector.tensor_scalar(var, var, 1.0 / D, EPS, ALU.mult, ALU.add).then_inc(variance, 1)
            roots[0] += 1
            dve.wait_ge(root, roots[0])
            link(nc.vector.reciprocal(var, var))
            last = nc.vector.tensor_tensor(v, v, var.unsqueeze(2).to_broadcast([P, NODE_TILES, D]), ALU.mult)
            if signal:
                last.then_inc(normed, 1)
            else:
                link(last)

        def both_sums(dve, O, i):
            if not is_first(i):
                dve.wait_ge(O["acc_ps"], i)
            nc.vector.tensor_tensor(stage_a, acc[:, bass.ds(i * CP, CP)], acc_odd[:, bass.ds(i * CP, CP)], ALU.add
                                    ).then_inc(O["staged"], 1)

        def loop_sums(dve, C, O, body):
            dve.wait_ge(C["added"], GROUP * GROUPS)

            def ahead(i):
                if is_chunk(i + 1):
                    both_sums(dve, O, i + 1)
                body(i)
            both_sums(dve, O, 0)
            loop_ahead(dve, ahead, 1)

        def quotients(dve, O, sums, i, first, to, eps):
            if not first:
                dve.wait_ge(O["mixed_ps"] if O is O0 else O["mixed"], i)
            nc.vector.tensor_scalar_add(chunk_d, sums[:, :, D:A], eps).then_inc(O["den"], 1)
            dve.wait_ge(O["den"], 2 * i + 1)
            nc.vector.reciprocal(chunk_d, chunk_d).then_inc(O["den"], 1)
            dve.wait_ge(O["den"], 2 * i + 2)
            nc.vector.tensor_tensor(heads(to), heads(sums[:, :, 0:D]), chunk_d.unsqueeze(3).to_broadcast([P, CHUNK, H, DH]),
                                    ALU.mult).then_inc(O["mixed"], 1)

        def one_hots(C, g, u):
            nc.vector.tensor_tensor(onehot[:, u, :, :], iota[:, 0:P].unsqueeze(1).to_broadcast([P, GROUP, P]),
                                    dst_rel[:, bass.ds(g * GROUP, GROUP)].unsqueeze(2).to_broadcast([P, GROUP, P]),
                                    ALU.is_equal).then_inc(C["onehot"], 1)

        def add_sums(dve, C, g, of, width, regs):
            dve.wait_ge(C["reduced"], g + 1)
            if C is A0:
                for b, n in enumerate((4 * SLOTS, 2 * GROUP - 4 * SLOTS)):
                    to = part_t[0:A, bass.ds(g * 2 * GROUP + b * 4 * SLOTS, n)]
                    to = to.rearrange("p (b k w) -> p b k w", b=2, w=2) if b == 0 else to.rearrange("p (k w) -> p k w", w=2)
                    nc.vector.tensor_copy(to, ends_of(b)).then_inc(C["ends"], 1)
            dve.load(regs, starts[0:1, bass.ds(g * GROUP, GROUP)])
            for k in range(GROUP):
                at = dve.snap(regs[k], min_val=0, max_val=N - 1)
                if not isinstance(g, int) or g * GROUP + k >= 2:
                    dve.wait_ge(C["added"], g * GROUP + k - 1)
                to = (acc if k % 2 == 0 else acc_odd)[0:width, bass.ds(at, P)]
                nc.vector.tensor_tensor(to, to, of(k)[0:width, 0:P], ALU.add).then_inc(C["added"], 1)

        def weighted(u, values):
            return nc.vector.tensor_tensor(heads(message[:, u, :, 0:D]), heads(values),
                                           message[:, u, :, D:A].unsqueeze(3).to_broadcast([P, GROUP, H, DH]), ALU.mult)

        def mix_dve(dve, regs):
            dve.wait_ge(zeroed, 1)

            def onehots(g, u):
                if since(g, 2):
                    dve.wait_ge(A0["onehot_ps"], g - 1)
                one_hots(A0, g, u)

            def scan(g, u, i):
                dve.wait_ge(A0["score_t"], g + 1)
                dve.wait_ge(A0["cuts"][u], 16 * (i + 1))
                if since(g, 2):
                    dve.wait_ge(A0["shifted"], g - 1)
                of, to = score_t[:, u, :], running[:, u, :]
                nc.vector.tensor_tensor_scan(to, cuts_in[:, u, 0:P], of, -BIG, ALU.add, ALU.max).then_inc(A0["scan"], 1)
                dve.wait_ge(A0["scan"], 2 * g + 1)
                nc.vector.tensor_tensor_scan(to[:, ::-1], cuts_in[:, u, 1:P + 1][:, ::-1], to[:, ::-1], -BIG, ALU.add, ALU.max
                                             ).then_inc(A0["scan"], 1)
                dve.wait_ge(A0["scan"], 2 * g + 2)
                nc.vector.tensor_scalar_max(part_max[:, bass.ds(g, 1), :].rearrange("p a w -> p (a w)"),
                                            to[:, 0:P:P - 1], -1.0e9)
                if since(g, 2):
                    dve.wait_ge(A0["weights_ps"], g - 1)
                nc.vector.scalar_tensor_tensor(exp_t[:, u, :], to, -1.0e9, of, ALU.max, ALU.subtract).then_inc(A0["shifted"], 1)

            def codes(g, u):
                if since(g, 2):
                    dve.wait_ge(A0["reduced"], g - 1)
                nc.vector.tensor_tensor(coded[:, u, :, :], iota[:].unsqueeze(1).to_broadcast([P, GROUP, P + 2]),
                                        dst_code[:, bass.ds(g * GROUP, GROUP)].unsqueeze(2).to_broadcast([P, GROUP, P + 2]),
                                        ALU.is_equal).then_inc(A0["coded"], 1)

            def messages(g, u):
                dve.wait_ge(A0["weights"], g + 1)
                dve.wait_ge(A0["kept"], g + 1)
                weighted(u, kept[:, u, :, :]).then_inc(A0["message"], 1)

            def body(i):
                for u in range(2):
                    g = 2 * i + u
                    dve.wait_ge(A0["expanded"], g + 1)
                    dve.wait_ge(A0["gathered"][u], landed(i))
                    if since(g, 2):
                        dve.wait_ge(A0["score"], g - 1)
                    nc.vector.tensor_tensor(product[:, u, :, :], rows[:, u, :, 0:D],
                                            banks(5 + u).rearrange("p (k f) -> p k f", k=GROUP), ALU.mult
                                            ).then_inc(A0["product"], 1)
                    if since(g, 1):
                        scan(g - 1, 1 - u, group_at(i, u, -1)[2])
                    dve.wait_ge(A0["product"], g + 1)
                    if since(g, 2):
                        dve.wait_ge(A0["score_ps"], g - 1)
                    nc.vector.tensor_reduce(score[:, u, :].rearrange("p (h k) -> p k h", h=H),
                                            heads(product[:, u, :, :]), AX, ALU.add).then_inc(A0["score"], 1)
                    if is_group(g + 2):
                        onehots(g + 2, u)
                    if since(g, 1):
                        codes(g - 1, 1 - u)
                        messages(g - 1, 1 - u)
                    if since(g, 2):
                        add_sums(dve, A0, g - 2, tile_sums, A, regs)
            onehots(0, 0)
            onehots(1, 1)
            dve.wait_ge(parts_in, 16)
            nc.vector.tensor_tensor(same, part_line_in[:, 1:PARTS + 2], part_line_in[:, 0:PARTS + 1], ALU.is_equal
                                    ).then_inc(parts, 1)
            dve.wait_ge(parts, 1)
            nc.vector.tensor_scalar(line_c, same[0:H, :], 1.0, BIG, ALU.subtract, ALU.mult).then_inc(parts, 1)
            loop_pairs(dve, body, 2)
            scan(LAST, 1, PAIRS - 1)
            add_sums(dve, A0, LAST - 1, tile_sums, A, regs)
            codes(LAST, 1)
            messages(LAST, 1)
            add_sums(dve, A0, LAST, tile_sums, A, regs)

        def parts_dve(dve):
            dve.wait_ge(parts, 2)
            dve.wait_ge(parts_act, 1)
            nc.vector.tensor_tensor_scan(line_m, line_c[:, 0:PARTS], line_a, -BIG, ALU.add, ALU.max).then_inc(parts_chain, 1)
            dve.wait_ge(parts_chain, 1)
            nc.vector.tensor_tensor_scan(line_m[:, ::-1], line_c[:, 1:PARTS + 1][:, ::-1], line_m[:, ::-1], -BIG,
                                         ALU.add, ALU.max).then_inc(parts, 1)
            dve.wait_ge(parts, 3)
            nc.vector.tensor_tensor(line_m, line_m, line_a, ALU.subtract).then_inc(parts, 1)
            for b in range(LINE_BANKS):
                dve.wait_ge(parts_ps, GROUP + b + 1)
                n = min(PARTS - 512 * b, 512)
                to = part_t[0:A, 512 * b:512 * b + n]
                last = nc.vector.tensor_tensor(to, to, banks(b)[0:A, 0:n], ALU.mult)
            last.then_inc(parts, 1)
            dve.wait_ge(parts, 5)
            nc.vector.tensor_tensor_scan(part_t[0:A, 0:PARTS], same[0:A, 0:PARTS], part_t[0:A, 0:PARTS], 0.0,
                                         ALU.mult, ALU.add).then_inc(parts, 1)

        def gated_dve(dve, regs):
            dve.wait_ge(zeroed, 2)

            def body(i):
                for u in range(2):
                    g = 2 * i + u
                    if since(g, 2):
                        dve.wait_ge(B0["reduced"], g - 1)
                    one_hots(B0, g, u)
                    dve.wait_ge(B0["edge_mm"], g + 1)
                    dve.wait_ge(B0["gathered"][u], landed(i))
                    nc.vector.tensor_tensor(message[:, u, :, 0:D], gathered_rows(u, D),
                                            bank[2][:, 1, :].rearrange("p (k f) -> p k f", k=GROUP), ALU.mult
                                            ).then_inc(B0["message"], 1)
                    if since(g, 2):
                        add_sums(dve, B0, g - 2, sums_in(bank[3 * u]), D, regs)
            loop_pairs(dve, body, 2)
            add_sums(dve, B0, LAST - 1, sums_in(bank[0]), D, regs)
            add_sums(dve, B0, LAST, sums_in(bank[3]), D, regs)

        def attend_dve(dve, regs):
            dve.wait_ge(zeroed, 3)

            def body(i):
                for u in range(2):
                    g = 2 * i + u
                    dve.wait_ge(C0["expanded"], g + 1)
                    dve.wait_ge(C0["gathered"][u], landed(i))
                    qd = bank[2][:, 0, :].rearrange("p (k f) -> p k f", k=GROUP)
                    ee = bank[2][:, 1, :].rearrange("p (k f) -> p k f", k=GROUP)
                    nc.vector.tensor_tensor(product[:, u, :, :], rows[:, u, :, 0:D], qd, ALU.mult).then_inc(C0["chain"], 1)
                    dve.wait_ge(C0["chain"], CHAIN2 * g + 1)
                    dve.wait_ge(C0["edge_mm"], g + 1)
                    nc.vector.tensor_tensor(product[:, u, :, :], product[:, u, :, :], ee, ALU.mult).then_inc(C0["chain"], 1)
                    dve.wait_ge(C0["chain"], CHAIN2 * g + 2)
                    if since(g, 2):
                        dve.wait_ge(C0["weights"], g - 1)
                    nc.vector.tensor_reduce(score[:, u, :].rearrange("p (k h) -> p k h", h=H),
                                            heads(product[:, u, :, :]), AX, ALU.add).then_inc(C0["chain"], 1)
                    dve.wait_ge(C0["chain"], CHAIN2 * g + 3)
                    nc.vector.tensor_scalar(score[:, u, :], score[:, u, :], 5.0 * DH ** 0.5, -5.0 * DH ** 0.5,
                                            ALU.min, ALU.max).then_inc(C0["chain"], 1)
                    if is_group(g + 1):
                        if since(g, 1):
                            dve.wait_ge(C0["reduced"], g)
                        one_hots(C0, g + 1, 1 - u)
                    dve.wait_ge(C0["weights"], g + 1)
                    weighted(u, rows[:, u, :, D:2 * D]).then_inc(C0["message"], 1)
                    if since(g, 1):
                        add_sums(dve, C0, g - 1, sums_in(bank[0]), A, regs)
            one_hots(C0, 0, 0)
            loop_pairs(dve, body)
            add_sums(dve, C0, LAST, sums_in(bank[0]), A, regs)

        def gin_dve(dve, G, regs):
            dve.wait_ge(zeroed, 4 if G is G0 else 5)
            if G is G0:
                dve.wait_ge(M3["xt"], CHUNKS)

            def body(i):
                for u in range(2):
                    g = 2 * i + u
                    if since(g, 2):
                        dve.wait_ge(G["reduced"], g - 1)
                    one_hots(G, g, u)
                    if since(g, 1):
                        add_sums(dve, G, g - 1, sums_in(bank[1 - u]), D, regs)
            loop_pairs(dve, body)
            add_sums(dve, G, LAST, sums_in(bank[1]), D, regs)

        @block.sync
        def _(sp):
            sp.wait_ge(filled, 1)
            for nat, v in ((nat_src, src), (nat_dst, dst)):
                for where, part in blocks_of(v):
                    sp.dma_start(nat[where], part).then_inc(graph_in, 16)
            for to, v in first_loads:
                sp.dma_start(to, v).then_inc(nodes_in, 16)
            with sp.Fori(0, NFULL // CHUNK) as i:
                sp.dma_start(nodes[:, tiles(i), :], x[bass.ds(i * CP, CP), :].rearrange("(t p) d -> p t d", p=P)
                             ).then_inc(nodes_in, 16)
            sp.dma_start(nodes[0:NREM, NFULL, :], x[NFULL * P:N, :]).then_inc(nodes_in, 16)
            sp.dma_start(part_sums.rearrange("(t p) f -> p t f", p=P), nothing.unsqueeze(1).to_broadcast([P, NODE_TILES, A])
                         ).then_inc(lines_out, 16)
            sp.dma_start(part_line[0:1, 0:P], minus).then_inc(lines_out, 16)
            sp.dma_start(part_line[0:1, P + 2 * NAT * P:2 * P + 2 * NAT * P], minus).then_inc(lines_out, 16)
            sp.wait_ge(graph_cast, 4)
            sp.dma_start(part_line[0, P:P + 2 * NAT * P].rearrange("(c p w) -> p c w", p=P, w=2), part_nodes).then_inc(lines_out, 16)
            sp.dma_start(start_line.rearrange("c p -> p c"), start_i, allow_slow_non_contiguous=True).then_inc(lines_out, 16)
            store_tables(sp, K0, 2)
            sp.wait_ge(lines_out, LINES_OUT)
            sp.dma_start(starts[:], start_line.rearrange("c p -> (c p)").rearrange("(a n) -> a n", a=1)).then_inc(starts_in, 16)
            for n in range(2):
                sp.dma_start(nat_parts[:, n, :], part_line[0, P + n:P + n + PART_TILES * P].rearrange("(c e) -> c e", e=P)
                             ).then_inc(starts_in, 16)
            sp.wait_ge(graph_cast, 5)
            sp.dma_start(cut_tiles.rearrange("(c p) e -> p c e", p=P), nat_cuts).then_inc(cuts_out, 16)
            sp.wait_ge(cuts_out, 16)
            for h in range(H):
                sp.dma_start(cut_edges[:, h, :, :], cut_tiles.rearrange("(g k) e -> g k e", k=GROUP)).then_inc(cuts_h, 16)

            sp.wait_ge(starts_in, 48)
            score_regs = [sp.alloc_register(f"sp_start{k}") for k in range(GROUP)]
            sp.wait_ge(K0["table"], 32 * CHUNKS)
            sp.dma_start(part_line_in, part_line[0:1, P - 1:P + PARTS + 1].to_broadcast([P, PARTS + 2])).then_inc(parts_in, 16)
            load_windows(sp, A0, score_regs, None)
            sp.wait_ge(parts_out, 16 * PART_TILES)
            sp.dma_start(node_parts, part_sums.rearrange("(t p) f -> p t f", p=P)).then_inc(parts_back, 16)
            store_tables(sp, K1, 1)
            gated_dma(sp)
            store_tables(sp, K2, 2)
            load_windows(sp, C0, score_regs, edge_attr_64)
            sp.wait_ge(normed, 3)
            sp.dma_start(x3_table.rearrange("(t p) d -> p t d", p=P), nodes[:]).then_inc(stored, 16)
            sp.wait_ge(M3["proj"], CHUNKS)
            sp.dma_start(y3_table.rearrange("(t p) d -> p t d", p=P), mix).then_inc(stored, 16)
            sp.wait_ge(normed, 4)
            sp.dma_start(out[0:NFULL * P, :].rearrange("(t p) d -> p t d", p=P), nodes[:, 0:NFULL, :]).then_inc(stored, 16)
            sp.dma_start(out[NFULL * P:N, :], nodes[0:NREM, NFULL, :]).then_inc(stored, 16)
            sp.wait_ge(stored, 64)

        @block.gpsimd
        def _(pool):
            nc.gpsimd.memset(ones[:], 1.0).then_inc(consts, 1)
            nc.gpsimd.memset(ident[:], 0.0).then_inc(consts, 1)
            nc.gpsimd.iota(iota[:], pattern=[[1, P + 2]], base=0, channel_multiplier=0,
                           allow_small_or_imprecise_dtypes=True).then_inc(consts, 1)
            pool.wait_ge(consts, 3)
            nc.gpsimd.affine_select(out=ident[:], in_=ident[:], compare_op=ALU.not_equal, fill=1.0, base=0,
                                    pattern=[[-1, P]], channel_multiplier=1).then_inc(consts, 1)
            pool.wait_ge(filled, 1)
            for to, v in weight_loads:
                pool.dma_start(to, v).then_inc(weights_in, 16)
            pool.wait_ge(graph_ps, 1)
            pool.wait_ge(graph_cast, 6)
            clear_sums()
            pool.wait_ge(graph_out, 2)
            pool.wait_ge(K0["table"], 32 * CHUNKS)
            gather(pool, A0, kv_table, 2 * D, [(A0["product"], 1), (A0["kept"], 1)])
            for c in range(PART_TILES):
                pool.wait_ge(parts_act, 3 + c // 4)
                pool.indirect_dma_start(part_sums, bass.IndirectOffsetOnAxis(part_index[:, c:c + 1], 0), part_rows[:, c, :], None,
                                        bounds_check=NPAD - 1, oob_is_err=False).then_inc(parts_out, 16)
            pool.wait_ge(O0["staged"], CHUNKS)
            clear_sums()
            pool.wait_ge(K1["table"], 16 * CHUNKS)
            gather(pool, B0, xt_table, D, [(B0["message"], 1)])
            pool.wait_ge(O1["staged"], CHUNKS)
            clear_sums()
            pool.wait_ge(K2["table"], 32 * CHUNKS)
            gather(pool, C0, kv_table, 2 * D, [(C0["message"], 1)])
            pool.wait_ge(O2["staged"], CHUNKS)
            clear_sums(even=False)
            pool.wait_ge(stored, 16)
            gather(pool, G0, x3_table, D, [(G0["reduced"], 1)])
            pool.wait_ge(M3["sum"], CHUNKS)
            clear_sums()
            pool.wait_ge(stored, 32)
            gather(pool, G1, y3_table, D, [(G1["reduced"], 1)])

        @block.scalar
        def _(act):
            act.wait_ge(graph_ps, 1)
            for b in range(2):
                n = min(NATW - b * 1024, 1024)
                last = nc.scalar.copy(dst_rel[:, b * 1024:b * 1024 + n],
                                      bank[b][:].rearrange("p a b -> p (a b)")[:, 0:n])
            last.then_inc(graph_out, 1)
            for b in range(2):
                n = min(NATW - b * 1024, 1024)
                last = nc.scalar.copy(src_idx[:, b * 1024:b * 1024 + n],
                                      bank[2 + b][:].rearrange("p a b -> p (a b)")[:, 0:n])
            last.then_inc(graph_out, 1)
            act.wait_ge(nodes_in, NODES_IN)
            copy_projections(act, K0, 2)
            act.wait_ge(code_ps, 1)
            for b in range(2):
                n = min(NATW - b * 1024, 1024)
                nc.scalar.copy(dst_code[:, b * 1024:b * 1024 + n], bank[b][:].rearrange("p a b -> p (a b)")[:, 0:n])
            nc.scalar.copy(part_index[:], banks(4)[:, 0:PART_TILES]).then_inc(code_out, 1)
            act.wait_ge(weights_ps, 1)
            nc.scalar.copy(w_2[:], banks(0)[0:D, 0:3 * D]).then_inc(weights_t, 1)
            nc.scalar.copy(w_e[0:D, 0:D], banks(0)[0:D, 3 * D:4 * D]).then_inc(weights_t, 1)
            nc.scalar.copy(w_e[D:P, D:2 * D], banks(0)[0:D, 3 * D:4 * D]).then_inc(weights_t, 1)
            mix_act(act)
            parts_on_act(act)
            mixed_act(act)
            square_root(act, 1)
            mlp_act(act)
            gated_act(act)
            square_root(act, 2)
            square_root(act, 3)
            act.wait_ge(normed, 2)
            copy_projections(act, K2, 2)
            attend_act(act)
            square_root(act, 4)
            gin_start_act(act)
            gin_act(act)
            square_root(act, 5)

        @block.tensor
        def _(pe):
            pe.wait_ge(consts, 4)
            pe.wait_ge(graph_cast, 3)
            for c in range(NAT):
                nc.tensor.transpose(bank[c // 8][:, c // 4 % 2, c % 4 * P:(c % 4 + 1) * P], flt_rel[:, c, :], ident[:])
                last = nc.tensor.transpose(bank[2 + c // 8][:, c // 4 % 2, c % 4 * P:(c % 4 + 1) * P], flt_src[:, c, :], ident[:])
            last.then_inc(graph_ps, 1)
            pe.wait_ge(graph_out, 2)
            project(pe, K0, w_qkv)
            pe.wait_ge(K0["proj"], 2 * CHUNKS)
            pe.wait_ge(weights_in, WEIGHTS_IN)
            pe.wait_ge(graph_cast, 7)
            for c in range(NAT):
                nc.tensor.transpose(bank[c // 8][:, c // 4 % 2, c % 4 * P:(c % 4 + 1) * P], flt_code[:, c, :], ident[:])
            nc.tensor.transpose(banks(4)[:, 0:PART_TILES], nat_parts[:, 0, :], ident[0:PART_TILES, 0:PART_TILES]).then_inc(code_ps, 1)
            pe.wait_ge(code_out, 1)
            for n in range(4):
                last = nc.tensor.transpose(banks(0)[0:D, n * D:(n + 1) * D], w_nat[:, n * D:(n + 1) * D], ident[0:D, 0:D])
            last.then_inc(weights_ps, 1)
            pe.wait_ge(weights_t, 3)
            mix_pe(pe)
            parts_pe(pe)
            mix_out_pe(pe)
            mlp_pe(pe)
            gated_pe(pe)
            turn_sums(pe, O1)
            pe.wait_ge(normed, 2)
            project(pe, K2, w_2)
            attend_pe(pe)
            turn_sums(pe, O2)
            gin_start_pe(pe)
            gin_pe(pe, G0)
            gin_mid_pe(pe)
            gin_pe(pe, G1)
            turn_sums(pe, O3)

        @block.vector
        def _(dve):
            steps = [0]

            def link(ins):
                steps[0] += 1
                ins.then_inc(norm, 1)
                dve.wait_ge(norm, steps[0])

            regs = [dve.alloc_register(f"dve_start{k}") for k in range(GROUP)]
            nc.vector.memset(nat_src, 0)
            nc.vector.memset(nat_dst, 4 * NPAD)
            nc.vector.memset(nodes[:], 0.0)
            nc.vector.memset(minus, -1.0)
            nc.vector.memset(w_1e[:], 0.0)
            nc.vector.memset(w_e[:], 0.0)
            nc.vector.memset(nothing, 0.0)
            nc.vector.memset(nat_cuts, 0.0).then_inc(filled, 1)
            dve.wait_ge(graph_in, GRAPH_IN)
            link(nc.vector.tensor_copy(flt_dst, nat_dst))
            link(nc.vector.tensor_scalar_min(start_f, flt_dst[:, :, 0], float(N - 1)))
            nc.vector.tensor_copy(start_i, start_f).then_inc(graph_cast, 1)
            nc.vector.tensor_copy(flt_src, nat_src).then_inc(graph_cast, 1)
            nc.vector.tensor_tensor(flt_rel, flt_dst, start_f.unsqueeze(2).to_broadcast([P, NAT, P]),
                                    ALU.subtract).then_inc(graph_cast, 1)
            nc.vector.tensor_copy(part_nodes, flt_dst[:, :, 0:P:P - 1]).then_inc(graph_cast, 1)
            link(nc.vector.tensor_tensor(nat_cuts[:, :, 1:P], flt_dst[:, :, 1:P], flt_dst[:, :, 0:P - 1], ALU.not_equal))
            nc.vector.tensor_scalar_mul(nat_cuts[:, :, 1:P], nat_cuts[:, :, 1:P], -BIG).then_inc(graph_cast, 1)
            link(nc.vector.tensor_tensor(in_first, flt_dst, flt_dst[:, :, 0:1].to_broadcast([P, NAT, P]), ALU.is_equal))
            link(nc.vector.tensor_tensor(in_last, flt_dst, flt_dst[:, :, P - 1:P].to_broadcast([P, NAT, P]), ALU.is_equal))
            link(nc.vector.tensor_tensor(in_last, in_last, in_first, ALU.subtract))
            dve.wait_ge(graph_cast, 5)
            link(nc.vector.scalar_tensor_tensor(flt_code, in_last, P + 1.0, flt_rel, ALU.mult, ALU.max))
            nc.vector.scalar_tensor_tensor(flt_code, in_first, float(P), flt_code, ALU.mult, ALU.max).then_inc(graph_cast, 1)
            dve.wait_ge(starts_in, 48)
            link(nc.vector.tensor_tensor(nat_parts[:, 1, :], nat_parts[:, 0, :], nat_parts[:, 1, :], ALU.is_equal))
            nc.vector.scalar_tensor_tensor(nat_parts[:, 0, :], nat_parts[:, 1, :], 4.0 * NPAD, nat_parts[:, 0, :],
                                           ALU.mult, ALU.add).then_inc(graph_cast, 1)
            dve.wait_ge(weights_in, WEIGHTS_IN)
            nc.vector.tensor_tensor(gain[:], gains[:, 0:1], gains[:, 1:2], ALU.mult).then_inc(w_scaled, 1)
            nc.vector.tensor_scalar_mul(w_2e[0:D, :], w_2e[0:D, :], SLOPE)
            nc.vector.tensor_scalar_mul(w_2e[D:P, :], w_2e[D:P, :], 1.0 - SLOPE).then_inc(w_scaled, 1)
            dve.wait_ge(graph_out, 2)
            dve.wait_ge(consts, 4)

            nc.vector.tensor_copy(head_rows[:, 0:D].rearrange("h (a d) -> h a d", d=DH),
                                  ident[0:H, 0:H].unsqueeze(2).to_broadcast([H, H, DH]))
            nc.vector.tensor_copy(head_rows[:, D:A], ident[0:H, 0:H])
            dve.wait_ge(lines_out, LINES_OUT)
            dve.wait_ge(cuts_out, 16)
            dve.wait_ge(code_out, 1)
            dve.wait_ge(K0["table"], 32 * CHUNKS)
            nc.vector.memset(part_t, 0.0)
            mix_dve(dve, regs)
            parts_dve(dve)

            def mixed(i):
                dve.wait_ge(O0["acc_ps"], i + 1)
                if not is_first(i):
                    dve.wait_ge(O0["mixed"], i)
                nc.vector.tensor_tensor(chunk_s, chunk_a[:, :, 0:A], node_parts[:, tiles(i), :], ALU.add).then_inc(O0["whole"], 1)
                dve.wait_ge(O0["whole"], i + 1)
                quotients(dve, O0, chunk_s, i, is_first(i), chunk_m, 1e-9)

            def mixed_out(i):
                if is_chunk(i + 1):
                    mixed(i + 1)
                if is_chunk(i + 2):
                    both_sums(dve, O0, i + 2)
                dve.wait_ge(O0["proj_ps"], i + 1)
                nc.vector.tensor_tensor(nodes[:, tiles(i), :], nodes[:, tiles(i), :], chunk_v, ALU.add).then_inc(O0["added"], 1)
            dve.wait_ge(A0["added"], GROUP * GROUPS)
            both_sums(dve, O0, 0)
            dve.wait_ge(parts_back, 16)
            mixed(0)
            both_sums(dve, O0, 1)
            loop_ahead(dve, mixed_out, 2)
            dve.wait_ge(O0["added"], CHUNKS)
            layer_norm(dve, nodes[:], link, True)

            def leaky(i, first):
                dve.wait_ge(K1["hid"], i + 1)
                nc.vector.scalar_tensor_tensor(chunk_l, chunk_h, SLOPE, chunk_h, ALU.mult, ALU.max).then_inc(K1["leaky"], 1)
                dve.wait_ge(K1["proj_ps"], i + 1)
                if not first:
                    dve.wait_ge(K1["table"], 16 * i)
                nc.vector.tensor_tensor(chunk_p[:, :, 0:D], chunk_v, b_2n[:].unsqueeze(1).to_broadcast([P, CHUNK, D]),
                                        ALU.add).then_inc(K1["proj"], 1)
            loop_chunks(dve, leaky)
            gated_dve(dve, regs)

            def gated_out(i):
                dve.wait_ge(O1["acc_ps"], i + 1)
                nc.vector.scalar_tensor_tensor(mix[:, tiles(i), :], chunk_a[:, :, 0:D], gain[:, 0:1],
                                               nodes[:, tiles(i), :], ALU.mult, ALU.add).then_inc(O1["added"], 1)
            loop_sums(dve, B0, O1, gated_out)
            dve.wait_ge(O1["added"], CHUNKS)
            layer_norm(dve, mix, link, False)
            link(nc.vector.tensor_tensor(mix, mix, gamma[:].unsqueeze(1).to_broadcast([P, NODE_TILES, D]), ALU.mult))
            link(nc.vector.tensor_tensor(mix, mix, beta[:].unsqueeze(1).to_broadcast([P, NODE_TILES, D]), ALU.add))
            link(nc.vector.tensor_tensor(nodes[:], nodes[:], mix, ALU.add))
            layer_norm(dve, nodes[:], link, True)
            attend_dve(dve, regs)

            def attend_out(i):
                dve.wait_ge(O2["acc_ps"], i + 1)
                quotients(dve, O2, chunk_a, i, is_first(i), mix[:, tiles(i), :], 1e-6)
            loop_sums(dve, C0, O2, attend_out)
            dve.wait_ge(O2["mixed"], CHUNKS)
            link(nc.vector.tensor_tensor(nodes[:], nodes[:], mix, ALU.add))
            layer_norm(dve, nodes[:], link, True)
            gin_dve(dve, G0, regs)

            def gin_sum(i, first):
                if not first:
                    dve.wait_ge(M3["hid_ps"], i)
                nc.vector.tensor_tensor(chunk_t, acc[0:D, bass.ds(i * CP, CP)], acc_odd[0:D, bass.ds(i * CP, CP)], ALU.add
                                        ).then_inc(M3["sum"], 1)
            dve.wait_ge(G0["added"], GROUP * GROUPS)
            loop_chunks(dve, gin_sum)
            dve.wait_ge(M3["sum"], CHUNKS)
            dve.wait_ge(M3["proj"], CHUNKS)
            link(nc.vector.tensor_tensor(nodes[:], nodes[:], mix, ALU.add))
            link(nc.vector.tensor_tensor(nodes[:], nodes[:], b_g2[:].unsqueeze(1).to_broadcast([P, NODE_TILES, D]), ALU.add))
            gin_dve(dve, G1, regs)

            def gin_out(i):
                dve.wait_ge(O3["acc_ps"], i + 1)
                nc.vector.tensor_tensor(nodes[:, tiles(i), :], nodes[:, tiles(i), :], chunk_a[:, :, 0:D], ALU.add).then_inc(O3["added"], 1)
            loop_sums(dve, G1, O3, gin_out)
            dve.wait_ge(O3["added"], CHUNKS)
            layer_norm(dve, nodes[:], link, True)


_INS = ["x", "src", "dst", "edge_attr_32", "edge_attr_64",
        "L0_gnn_Wq", "L0_gnn_Wk", "L0_gnn_Wv", "L0_gnn_Wo",
        "L1_gnn_W1n", "L1_gnn_b1n", "L1_gnn_W2n", "L1_gnn_b2n", "L1_gnn_W1e", "L1_gnn_b1e",
        "L1_gnn_W2e", "L1_gnn_b2e", "L1_gnn_res_w", "L1_gnn_dp_scale", "L1_gnn_gamma", "L1_gnn_beta",
        "L2_gnn_Wq", "L2_gnn_Wk", "L2_gnn_We", "L2_gnn_Wv",
        "L3_gnn_W1", "L3_gnn_b1", "L3_gnn_W2", "L3_gnn_b2"]


def kernel(**inputs):
    import numpy as _np
    import concourse.bacc as _bacc
    from concourse import mybir as _mybir
    from concourse.bass_utils import run_bass_kernel_spmd as _run

    nc = _bacc.Bacc("TRN2", target_bir_lowering=False, num_devices=1)
    arrays, args = {}, []
    for name in _INS:
        a = _np.ascontiguousarray(inputs[name])
        arrays[f"in_{name}_dram"] = a
        args.append(nc.dram_tensor(f"in_{name}_dram", a.shape, _mybir.dt.from_np(a.dtype), kind="ExternalInput").ap())
    shape = tuple(inputs["x"].shape)
    args.append(nc.dram_tensor("out_0_dram", shape, _mybir.dt.float32, kind="ExternalOutput").ap())
    build_gnn(nc, *args)
    r = _run(nc, [arrays], core_ids=[0])
    return r.results[0]["out_0_dram"]
```
